# Optimizing a Trainium2 kernel written in Bass

```python
import numpy as np
import jax
import jax.numpy as jnp

def _softmax(x, axis=-1):
    return jax.nn.softmax(x, axis=axis)

def _gelu(x):
    return jax.nn.gelu(x, approximate=True)

def _silu(x):
    return jax.nn.silu(x)

def _sigmoid(x):
    return jax.nn.sigmoid(x)

def _layernorm(x, axis=-1, eps=1e-05):
    m = jnp.mean(x, axis=axis, keepdims=True)
    v = jnp.var(x, axis=axis, keepdims=True)
    return (x - m) / jnp.sqrt(v + eps)

def _scatter_add(tgt, idx, src, axis=0):
    return tgt.at[idx].add(src)

def _segment_sum(src, seg, n):
    return jax.ops.segment_sum(src, seg, n)
kernel_name = 'mk_gnn_ffn_d2_gnn_r32_910a26'

def setup_inputs(seed: int=0):
    np.random.seed(seed)
    _w = jnp.asarray

    def _rec_inputs():
        import jax
        import jax.numpy as jnp
        _gk = jax.random.key(seed)
        x = -0.0003713 + 1 * jax.random.normal(jax.random.fold_in(_gk, 1), (3125, 256), jnp.float32)
        src = jax.random.randint(jax.random.fold_in(_gk, 2), (50000,), 0, 3125, jnp.int32)
        dst = jnp.minimum((3125 * jax.random.uniform(jax.random.fold_in(_gk, 3), (50000,)) ** 2.0).astype(jnp.int32), 99999)
        _o = jnp.argsort(dst, stable=True)
        src = src[_o]
        dst = dst[_o]
        return (x, src, dst)
    x, src, dst = _rec_inputs()

    def _L0_gnn_setup():
        import jax, jax.numpy as jnp
        import numpy as np
        N_NODES = 50000
        N_EDGES = 20000
        IN_FEATS = 256
        H_FEATS = 256

        def _sage_mean(h, src, dst, W_self, W_neigh, b, n_nodes):
            msg = h[src]
            agg = jax.ops.segment_sum(msg, dst, num_segments=n_nodes)
            deg = jax.ops.segment_sum(jnp.ones_like(dst, dtype=h.dtype), dst, num_segments=n_nodes)
            h_neigh = agg / jnp.clip(deg, 1.0)[:, None]
            return h @ W_self.T + h_neigh @ W_neigh.T + b
        key = jax.random.key(seed)
        ks = jax.random.split(key, 12)
        s = 0.05
        return {'x': jax.random.normal(ks[0], (N_NODES, IN_FEATS), dtype=jnp.float32), 'src': jax.random.randint(ks[1], (N_EDGES,), 0, N_NODES, dtype=jnp.int32), 'dst': jax.random.randint(ks[2], (N_EDGES,), 0, N_NODES, dtype=jnp.int32), 'raw_weights': jnp.ones((IN_FEATS,), dtype=jnp.float32), 'W_self1': jax.random.normal(ks[3], (H_FEATS, IN_FEATS), dtype=jnp.float32) * s, 'W_neigh1': jax.random.normal(ks[4], (H_FEATS, IN_FEATS), dtype=jnp.float32) * s, 'b1': jnp.zeros((H_FEATS,), dtype=jnp.float32), 'W_self2': jax.random.normal(ks[5], (H_FEATS, H_FEATS), dtype=jnp.float32) * s, 'W_neigh2': jax.random.normal(ks[6], (H_FEATS, H_FEATS), dtype=jnp.float32) * s, 'b2': jnp.zeros((H_FEATS,), dtype=jnp.float32)}
    _L0_gnn_all = _L0_gnn_setup()
    _L0_gnn_in = {k: v for k, v in _L0_gnn_all.items() if k in ('raw_weights', 'W_self1', 'W_neigh1', 'b1', 'W_self2', 'W_neigh2', 'b2')}
    del _L0_gnn_all

    def _L0_ffn_setup():
        import jax, jax.numpy as jnp
        import numpy as np
        DIM = 256
        H = 8
        D = 64
        G = 64
        INNER = H * D
        SCALE = D ** (-0.5)
        key = jax.random.key(seed)
        ks = jax.random.split(key, 12)
        B, N = (4, 512)
        x = jax.random.normal(ks[0], (B, N, DIM), dtype=jnp.float32)
        s = lambda fan_in: 1.0 / np.sqrt(fan_in)
        W_fx = jax.random.normal(ks[1], (DIM, INNER), dtype=jnp.float32) * s(DIM)
        b_fx = jnp.zeros((INNER,), dtype=jnp.float32)
        W_x = jax.random.normal(ks[2], (DIM, INNER), dtype=jnp.float32) * s(DIM)
        b_x = jnp.zeros((INNER,), dtype=jnp.float32)
        A = jax.random.normal(ks[3], (G, D), dtype=jnp.float32)
        Q, _ = jnp.linalg.qr(A.T)
        W_slice = Q[:, :G].astype(jnp.float32)
        b_slice = jnp.zeros((G,), dtype=jnp.float32)
        W_q = jax.random.normal(ks[4], (D, D), dtype=jnp.float32) * s(D)
        W_k = jax.random.normal(ks[5], (D, D), dtype=jnp.float32) * s(D)
        W_v = jax.random.normal(ks[6], (D, D), dtype=jnp.float32) * s(D)
        W_out = jax.random.normal(ks[7], (INNER, DIM), dtype=jnp.float32) * s(INNER)
        b_out = jnp.zeros((DIM,), dtype=jnp.float32)
        temperature = jnp.ones((1, H, 1, 1), dtype=jnp.float32) * 0.5
        return {'x': x, 'W_fx': W_fx, 'b_fx': b_fx, 'W_x': W_x, 'b_x': b_x, 'W_slice': W_slice, 'b_slice': b_slice, 'W_q': W_q, 'W_k': W_k, 'W_v': W_v, 'W_out': W_out, 'b_out': b_out, 'temperature': temperature}
    _L0_ffn_all = _L0_ffn_setup()
    _L0_ffn_in = {k: v for k, v in _L0_ffn_all.items() if k in ('W_fx', 'b_fx', 'W_x', 'b_x', 'W_slice', 'b_slice', 'W_q', 'W_k', 'W_v', 'W_out', 'b_out', 'temperature')}
    del _L0_ffn_all

    def _L1_gnn_setup():
        import jax, jax.numpy as jnp
        import numpy as np
        N, E = (50000, 25000)
        IN, HID, HEADS, OUT = (256, 64, 4, 256)
        FIRST_OUT = HID * HEADS

        def gat_conv(x, src, dst, W, a_src, a_dst, b, concat):
            n = x.shape[0]
            H, C = a_src.shape
            h = (x @ W).reshape(n, H, C)
            es = jnp.einsum('nhc,hc->nh', h, a_src)[src]
            ed = jnp.einsum('nhc,hc->nh', h, a_dst)[dst]
            e = jax.nn.leaky_relu(es + ed, negative_slope=0.2)
            m = jax.ops.segment_max(e, dst, num_segments=n)
            p = jnp.exp(e - m[dst])
            z = jax.ops.segment_sum(p, dst, num_segments=n)
            alpha = p / z[dst]
            out = jax.ops.segment_sum(h[src] * alpha[:, :, None], dst, num_segments=n)
            out = out.reshape(n, H * C) if concat else out.mean(axis=1)
            return out + b

        def batchnorm(x, gamma, beta, eps=1e-05):
            mu = x.mean(axis=0)
            var = ((x - mu) ** 2).mean(axis=0)
            return gamma * (x - mu) / jnp.sqrt(var + eps) + beta
        key = jax.random.key(seed)
        ks = jax.random.split(key, 10)
        s = 0.05
        return {'x': jax.random.normal(ks[0], (N, IN), jnp.float32), 'edge_index': jax.random.randint(ks[1], (2, E), 0, N, dtype=jnp.int64), 'W0': jax.random.normal(ks[2], (IN, HEADS * HID), jnp.float32) * s, 'a_src0': jax.random.normal(ks[3], (HEADS, HID), jnp.float32) * s, 'a_dst0': jax.random.normal(ks[4], (HEADS, HID), jnp.float32) * s, 'b0': jnp.zeros((HEADS * HID,), jnp.float32), 'gamma0': jnp.ones((FIRST_OUT,), jnp.float32), 'beta0': jnp.zeros((FIRST_OUT,), jnp.float32), 'W1': jax.random.normal(ks[5], (FIRST_OUT, OUT), jnp.float32) * s, 'a_src1': jax.random.normal(ks[6], (1, OUT), jnp.float32) * s, 'a_dst1': jax.random.normal(ks[7], (1, OUT), jnp.float32) * s, 'b1': jnp.zeros((OUT,), jnp.float32)}
    _L1_gnn_all = _L1_gnn_setup()
    _L1_gnn_in = {k: v for k, v in _L1_gnn_all.items() if k in ('W0', 'a_src0', 'a_dst0', 'b0', 'gamma0', 'beta0', 'W1', 'a_src1', 'a_dst1', 'b1')}
    del _L1_gnn_all

    def _L1_ffn_setup():
        import jax, jax.numpy as jnp
        import numpy as np
        B, N, D = (16, 128, 256)
        NUM_EXPERTS, TOP_K, HEADS = (4, 2, 4)
        N_EDGES = 32768
        LN_EPS = 1e-05

        def _layernorm(x, g, b):
            mu = x.mean(-1, keepdims=True)
            var = ((x - mu) ** 2).mean(-1, keepdims=True)
            return (x - mu) * jax.lax.rsqrt(var + LN_EPS) * g + b

        def _forward(x, edge_index, W_gat, att_src, att_dst, b_gat, ln_gamma, ln_beta, W1, b1, W2, b2):
            Bc, Nc, Dc = x.shape
            M = Bc * Nc
            x_flat = x.reshape(M, Dc)
            h = (x_flat @ W_gat).reshape(M, HEADS, NUM_EXPERTS)
            loops = jnp.arange(M, dtype=edge_index.dtype)
            src = jnp.concatenate([edge_index[0], loops])
            dst = jnp.concatenate([edge_index[1], loops])
            a_src = (h * att_src).sum(-1)
            a_dst = (h * att_dst).sum(-1)
            e = jax.nn.leaky_relu(a_src[src] + a_dst[dst], negative_slope=0.2)
            e_max = jax.ops.segment_max(e, dst, num_segments=M)
            ee = jnp.exp(e - e_max[dst])
            denom = jax.ops.segment_sum(ee, dst, num_segments=M)
            alpha = ee / (denom[dst] + 1e-16)
            msg = h[src] * alpha[:, :, None]
            agg = jax.ops.segment_sum(msg, dst, num_segments=M).reshape(M, HEADS * NUM_EXPERTS) + b_gat
            scores = _layernorm(agg, ln_gamma, ln_beta).reshape(M, HEADS, NUM_EXPERTS).mean(1)
            scores = scores.reshape(Bc, Nc, NUM_EXPERTS)
            topk_s, topk_i = jax.lax.top_k(scores, TOP_K)
            w = jax.nn.softmax(topk_s, axis=-1)
            out = jnp.zeros_like(x)
            for ei in range(NUM_EXPERTS):
                g = jnp.where(topk_i == ei, w, 0.0).sum(-1)
                hh = jax.nn.gelu(x @ W1[ei] + b1[ei], approximate=False)
                out = out + g[..., None] * (hh @ W2[ei] + b2[ei])
            return out
        key = jax.random.key(seed)
        ks = jax.random.split(key, 8)
        s = 0.05
        return {'x': jax.random.normal(ks[0], (B, N, D), jnp.float32), 'W_gat': jax.random.normal(ks[1], (D, HEADS * NUM_EXPERTS), jnp.float32) * s, 'att_src': jax.random.normal(ks[2], (HEADS, NUM_EXPERTS), jnp.float32) * s, 'att_dst': jax.random.normal(ks[3], (HEADS, NUM_EXPERTS), jnp.float32) * s, 'b_gat': jnp.zeros((HEADS * NUM_EXPERTS,), jnp.float32), 'ln_gamma': jnp.ones((HEADS * NUM_EXPERTS,), jnp.float32), 'ln_beta': jnp.zeros((HEADS * NUM_EXPERTS,), jnp.float32), 'W1': jax.random.normal(ks[4], (NUM_EXPERTS, D, 2 * D), jnp.float32) * s, 'b1': jnp.zeros((NUM_EXPERTS, 2 * D), jnp.float32), 'W2': jax.random.normal(ks[5], (NUM_EXPERTS, 2 * D, D), jnp.float32) * s, 'b2': jnp.zeros((NUM_EXPERTS, D), jnp.float32), 'edge_index': jax.random.randint(ks[6], (2, N_EDGES), 0, B * N, jnp.int32)}
    _L1_ffn_all = _L1_ffn_setup()
    _L1_ffn_in = {k: v for k, v in _L1_ffn_all.items() if k in ('W_gat', 'att_src', 'att_dst', 'b_gat', 'ln_gamma', 'ln_beta', 'W1', 'b1', 'W2', 'b2', 'edge_index')}
    del _L1_ffn_all
    return {'x': x, 'src': src, 'dst': dst, 'L0_gnn_raw_weights': _L0_gnn_in['raw_weights'], 'L0_gnn_W_self1': _L0_gnn_in['W_self1'], 'L0_gnn_W_neigh1': _L0_gnn_in['W_neigh1'], 'L0_gnn_b1': _L0_gnn_in['b1'], 'L0_gnn_W_self2': _L0_gnn_in['W_self2'], 'L0_gnn_W_neigh2': _L0_gnn_in['W_neigh2'], 'L0_gnn_b2': _L0_gnn_in['b2'], 'L0_ffn_W_fx': _L0_ffn_in['W_fx'], 'L0_ffn_b_fx': _L0_ffn_in['b_fx'], 'L0_ffn_W_x': _L0_ffn_in['W_x'], 'L0_ffn_b_x': _L0_ffn_in['b_x'], 'L0_ffn_W_slice': _L0_ffn_in['W_slice'], 'L0_ffn_b_slice': _L0_ffn_in['b_slice'], 'L0_ffn_W_q': _L0_ffn_in['W_q'], 'L0_ffn_W_k': _L0_ffn_in['W_k'], 'L0_ffn_W_v': _L0_ffn_in['W_v'], 'L0_ffn_W_out': _L0_ffn_in['W_out'], 'L0_ffn_b_out': _L0_ffn_in['b_out'], 'L0_ffn_temperature': _L0_ffn_in['temperature'], 'L1_gnn_W0': _L1_gnn_in['W0'], 'L1_gnn_a_src0': _L1_gnn_in['a_src0'], 'L1_gnn_a_dst0': _L1_gnn_in['a_dst0'], 'L1_gnn_b0': _L1_gnn_in['b0'], 'L1_gnn_gamma0': _L1_gnn_in['gamma0'], 'L1_gnn_beta0': _L1_gnn_in['beta0'], 'L1_gnn_W1': _L1_gnn_in['W1'], 'L1_gnn_a_src1': _L1_gnn_in['a_src1'], 'L1_gnn_a_dst1': _L1_gnn_in['a_dst1'], 'L1_gnn_b1': _L1_gnn_in['b1'], 'L1_ffn_W_gat': _L1_ffn_in['W_gat'], 'L1_ffn_att_src': _L1_ffn_in['att_src'], 'L1_ffn_att_dst': _L1_ffn_in['att_dst'], 'L1_ffn_b_gat': _L1_ffn_in['b_gat'], 'L1_ffn_ln_gamma': _L1_ffn_in['ln_gamma'], 'L1_ffn_ln_beta': _L1_ffn_in['ln_beta'], 'L1_ffn_W1': _L1_ffn_in['W1'], 'L1_ffn_b1': _L1_ffn_in['b1'], 'L1_ffn_W2': _L1_ffn_in['W2'], 'L1_ffn_b2': _L1_ffn_in['b2'], 'L1_ffn_edge_index': _L1_ffn_in['edge_index']}

def reference(x, src, dst, L0_gnn_raw_weights, L0_gnn_W_self1, L0_gnn_W_neigh1, L0_gnn_b1, L0_gnn_W_self2, L0_gnn_W_neigh2, L0_gnn_b2, L0_ffn_W_fx, L0_ffn_b_fx, L0_ffn_W_x, L0_ffn_b_x, L0_ffn_W_slice, L0_ffn_b_slice, L0_ffn_W_q, L0_ffn_W_k, L0_ffn_W_v, L0_ffn_W_out, L0_ffn_b_out, L0_ffn_temperature, L1_gnn_W0, L1_gnn_a_src0, L1_gnn_a_dst0, L1_gnn_b0, L1_gnn_gamma0, L1_gnn_beta0, L1_gnn_W1, L1_gnn_a_src1, L1_gnn_a_dst1, L1_gnn_b1, L1_ffn_W_gat, L1_ffn_att_src, L1_ffn_att_dst, L1_ffn_b_gat, L1_ffn_ln_gamma, L1_ffn_ln_beta, L1_ffn_W1, L1_ffn_b1, L1_ffn_W2, L1_ffn_b2, L1_ffn_edge_index):
    import jax
    import jax.numpy as jnp

    def _L0_gnn_ref(x, src, dst, raw_weights, W_self1, W_neigh1, b1, W_self2, W_neigh2, b2):
        import jax, jax.numpy as jnp
        import numpy as np
        N_NODES = 50000
        N_EDGES = 20000
        IN_FEATS = 256
        H_FEATS = 256

        def _sage_mean(h, src, dst, W_self, W_neigh, b, n_nodes):
            msg = h[src]
            agg = jax.ops.segment_sum(msg, dst, num_segments=n_nodes)
            deg = jax.ops.segment_sum(jnp.ones_like(dst, dtype=h.dtype), dst, num_segments=n_nodes)
            h_neigh = agg / jnp.clip(deg, 1.0)[:, None]
            return h @ W_self.T + h_neigh @ W_neigh.T + b
        n = x.shape[0]
        w = jax.nn.softmax(raw_weights)
        wx = x * w
        out1 = jax.nn.relu(_sage_mean(wx, src, dst, W_self1, W_neigh1, b1, n)) + wx
        out2 = jax.nn.relu(_sage_mean(out1, src, dst, W_self2, W_neigh2, b2, n)) + out1
        return out2

    def _L0_ffn_ref(x, W_fx, b_fx, W_x, b_x, W_slice, b_slice, W_q, W_k, W_v, W_out, b_out, temperature):
        import jax, jax.numpy as jnp
        import numpy as np
        DIM = 256
        H = 8
        D = 64
        G = 64
        INNER = H * D
        SCALE = D ** (-0.5)
        B, N, _ = x.shape
        fx_mid = (x @ W_fx + b_fx).reshape(B, N, H, D).transpose(0, 2, 1, 3)
        x_mid = (x @ W_x + b_x).reshape(B, N, H, D).transpose(0, 2, 1, 3)
        temp = jnp.clip(temperature, 0.1, 5.0)
        slice_weights = jax.nn.softmax((x_mid @ W_slice + b_slice) / temp, axis=-1)
        slice_norm = slice_weights.sum(axis=2)
        slice_token = jnp.einsum('bhnc,bhng->bhgc', fx_mid, slice_weights)
        slice_token = slice_token / (slice_norm[..., None] + 1e-05)
        q = slice_token @ W_q
        k = slice_token @ W_k
        v = slice_token @ W_v
        attn = jax.nn.softmax(jnp.einsum('bhgc,bhkc->bhgk', q, k) * SCALE, axis=-1)
        out_slice = jnp.einsum('bhgk,bhkc->bhgc', attn, v)
        out_x = jnp.einsum('bhgc,bhng->bhnc', out_slice, slice_weights)
        out_x = out_x.transpose(0, 2, 1, 3).reshape(B, N, INNER)
        return out_x @ W_out + b_out

    def _L1_gnn_ref(x, edge_index, W0, a_src0, a_dst0, b0, gamma0, beta0, W1, a_src1, a_dst1, b1):
        import jax, jax.numpy as jnp
        import numpy as np
        N, E = (50000, 25000)
        IN, HID, HEADS, OUT = (256, 64, 4, 256)
        FIRST_OUT = HID * HEADS

        def gat_conv(x, src, dst, W, a_src, a_dst, b, concat):
            n = x.shape[0]
            H, C = a_src.shape
            h = (x @ W).reshape(n, H, C)
            es = jnp.einsum('nhc,hc->nh', h, a_src)[src]
            ed = jnp.einsum('nhc,hc->nh', h, a_dst)[dst]
            e = jax.nn.leaky_relu(es + ed, negative_slope=0.2)
            m = jax.ops.segment_max(e, dst, num_segments=n)
            p = jnp.exp(e - m[dst])
            z = jax.ops.segment_sum(p, dst, num_segments=n)
            alpha = p / z[dst]
            out = jax.ops.segment_sum(h[src] * alpha[:, :, None], dst, num_segments=n)
            out = out.reshape(n, H * C) if concat else out.mean(axis=1)
            return out + b

        def batchnorm(x, gamma, beta, eps=1e-05):
            mu = x.mean(axis=0)
            var = ((x - mu) ** 2).mean(axis=0)
            return gamma * (x - mu) / jnp.sqrt(var + eps) + beta
        n = x.shape[0]
        loops = jnp.arange(n, dtype=edge_index.dtype)
        src = jnp.concatenate([edge_index[0], loops])
        dst = jnp.concatenate([edge_index[1], loops])
        h = gat_conv(x, src, dst, W0, a_src0, a_dst0, b0, concat=True)
        h = batchnorm(h, gamma0, beta0)
        h = jax.nn.elu(h)
        h = gat_conv(h, src, dst, W1, a_src1, a_dst1, b1, concat=False)
        norm = jnp.maximum(jnp.linalg.norm(h, axis=-1, keepdims=True), 1e-12)
        return h / norm

    def _L1_ffn_ref(x, W_gat, att_src, att_dst, b_gat, ln_gamma, ln_beta, W1, b1, W2, b2, edge_index):
        import jax, jax.numpy as jnp
        import numpy as np
        B, N, D = (16, 128, 256)
        NUM_EXPERTS, TOP_K, HEADS = (4, 2, 4)
        N_EDGES = 32768
        LN_EPS = 1e-05

        def _layernorm(x, g, b):
            mu = x.mean(-1, keepdims=True)
            var = ((x - mu) ** 2).mean(-1, keepdims=True)
            return (x - mu) * jax.lax.rsqrt(var + LN_EPS) * g + b

        def _forward(x, edge_index, W_gat, att_src, att_dst, b_gat, ln_gamma, ln_beta, W1, b1, W2, b2):
            Bc, Nc, Dc = x.shape
            M = Bc * Nc
            x_flat = x.reshape(M, Dc)
            h = (x_flat @ W_gat).reshape(M, HEADS, NUM_EXPERTS)
            loops = jnp.arange(M, dtype=edge_index.dtype)
            src = jnp.concatenate([edge_index[0], loops])
            dst = jnp.concatenate([edge_index[1], loops])
            a_src = (h * att_src).sum(-1)
            a_dst = (h * att_dst).sum(-1)
            e = jax.nn.leaky_relu(a_src[src] + a_dst[dst], negative_slope=0.2)
            e_max = jax.ops.segment_max(e, dst, num_segments=M)
            ee = jnp.exp(e - e_max[dst])
            denom = jax.ops.segment_sum(ee, dst, num_segments=M)
            alpha = ee / (denom[dst] + 1e-16)
            msg = h[src] * alpha[:, :, None]
            agg = jax.ops.segment_sum(msg, dst, num_segments=M).reshape(M, HEADS * NUM_EXPERTS) + b_gat
            scores = _layernorm(agg, ln_gamma, ln_beta).reshape(M, HEADS, NUM_EXPERTS).mean(1)
            scores = scores.reshape(Bc, Nc, NUM_EXPERTS)
            topk_s, topk_i = jax.lax.top_k(scores, TOP_K)
            w = jax.nn.softmax(topk_s, axis=-1)
            out = jnp.zeros_like(x)
            for ei in range(NUM_EXPERTS):
                g = jnp.where(topk_i == ei, w, 0.0).sum(-1)
                hh = jax.nn.gelu(x @ W1[ei] + b1[ei], approximate=False)
                out = out + g[..., None] * (hh @ W2[ei] + b2[ei])
            return out
        return _forward(x, edge_index, W_gat, att_src, att_dst, b_gat, ln_gamma, ln_beta, W1, b1, W2, b2)
    edge_index = jnp.stack([src, dst])
    x = x + _L0_gnn_ref(_layernorm(x, axis=-1), src, dst, L0_gnn_raw_weights, L0_gnn_W_self1, L0_gnn_W_neigh1, L0_gnn_b1, L0_gnn_W_self2, L0_gnn_W_neigh2, L0_gnn_b2)
    x = x + _L0_ffn_ref(_layernorm(x, axis=-1)[None], L0_ffn_W_fx, L0_ffn_b_fx, L0_ffn_W_x, L0_ffn_b_x, L0_ffn_W_slice, L0_ffn_b_slice, L0_ffn_W_q, L0_ffn_W_k, L0_ffn_W_v, L0_ffn_W_out, L0_ffn_b_out, L0_ffn_temperature)[0]
    x = x + _L1_gnn_ref(_layernorm(x, axis=-1), edge_index, L1_gnn_W0, L1_gnn_a_src0, L1_gnn_a_dst0, L1_gnn_b0, L1_gnn_gamma0, L1_gnn_beta0, L1_gnn_W1, L1_gnn_a_src1, L1_gnn_a_dst1, L1_gnn_b1)
    x = x + _L1_ffn_ref(_layernorm(x, axis=-1)[None], L1_ffn_W_gat, L1_ffn_att_src, L1_ffn_att_dst, L1_ffn_b_gat, L1_ffn_ln_gamma, L1_ffn_ln_beta, L1_ffn_W1, L1_ffn_b1, L1_ffn_W2, L1_ffn_b2, L1_ffn_edge_index)[0]
    return x

_drawn_inputs = setup_inputs


def setup_inputs(seed=0):
    import zlib

    import numpy as np

    out = dict(_drawn_inputs(seed))
    spreads = {'L0_gnn_raw_weights': (1.0, 0.6),
     'L0_gnn_b1': (0.0, 0.1),
     'L0_gnn_b2': (0.0, 0.1),
     'L0_ffn_b_fx': (0.0, 0.1),
     'L0_ffn_b_x': (0.0, 0.467),
     'L0_ffn_b_slice': (0.0, 0.387),
     'L0_ffn_b_out': (0.0, 0.1),
     'L0_ffn_temperature': (0.5, 0.6),
     'L1_gnn_b0': (0.0, 2.0),
     'L1_gnn_gamma0': (1.0, 0.2),
     'L1_gnn_beta0': (0.0, 0.284),
     'L1_gnn_b1': (0.0, 0.1),
     'L1_ffn_b_gat': (0.0, 0.1),
     'L1_ffn_ln_gamma': (1.0, 0.2),
     'L1_ffn_ln_beta': (0.0, 0.1),
     'L1_ffn_b1': (0.0, 0.1),
     'L1_ffn_b2': (0.0, 0.1)}
    factors = {'L0_gnn_W_self1': 7.612,
     'L0_gnn_W_neigh1': 8.0,
     'L0_ffn_W_slice': 2.819,
     'L0_ffn_W_q': 8.0,
     'L0_ffn_W_k': 8.0,
     'L1_gnn_a_src0': 2.734,
     'L1_gnn_a_dst0': 18.486,
     'L1_gnn_a_dst1': 12.127,
     'L1_ffn_att_dst': 2.682}
    for name, (base, spread) in spreads.items():
        noise = np.random.default_rng([zlib.crc32(name.encode()), seed]).standard_normal(out[name].shape)
        drawn = base * np.exp(spread * noise) if base else spread * noise
        out[name] = jnp.asarray(drawn.astype(out[name].dtype))
    for name, factor in factors.items():
        out[name] = (out[name] * factor).astype(out[name].dtype)
    return out
```

```python
import concourse.bass as bass
from concourse import mybir

F32 = mybir.dt.float32
I32 = mybir.dt.int32
ALU = mybir.AluOpType
ACT = mybir.ActivationFunctionType
AX = mybir.AxisListType

P = 128
NODES = 3125
D = 256
BUCKETS = -(-NODES // P)
T = BUCKETS + BUCKETS % 2
GRAPH_EDGES = (125, 400)
ROUTER_EDGES = (128, 256)
RING = 8
ROW = 260
HEADS = 4
EXPERTS = 4
HIDDEN = 512
SLICE_HEADS = 8
SLICE = 64
EPS = 1e-5
FAR = 1e30


def chunks_of(edges):
    need = -(-edges[0] * edges[1] // P) + BUCKETS
    return -(-need // RING) * RING


GRAPH_CHUNKS = chunks_of(GRAPH_EDGES)
ROUTER_CHUNKS = chunks_of(ROUTER_EDGES)

ROWS = [("raw", D), ("sb1", D), ("sb2", D), ("b_slice", SLICE), ("temp", SLICE_HEADS), ("b_out", D),
        ("as0", D), ("ad0", D), ("gb0", D), ("gamma0", D), ("beta0", D), ("as1", D), ("ad1", D), ("gb1", D),
        ("ras", 16), ("rad", 16), ("rb", 16), ("lng", 16), ("lnb", 16), ("eb2", EXPERTS * D)]
ROW_AT = {}
for _name, _n in ROWS:
    ROW_AT[_name] = (sum(n for m, n in ROWS[:len(ROW_AT)]), _n)
ROWS_LEN = sum(n for _, n in ROWS)


class Count:

    def __init__(self, nc, name):
        self.sem, self.base = nc.alloc_semaphore(name), RING


class Steps:

    def __init__(self, eng, count):
        self.eng, self.count, self.at, self.n, self.per, self.parity = eng, count, count.base, 0, None, 0

    def did(self, ins):
        ins.then_inc(self.count.sem, 1)
        self.n += 1
        return self.n

    def wait(self, back=0):
        self.eng.wait_ge(self.count.sem, self.at + (self.n - back))

    def do(self, ins):
        self.did(ins)
        self.wait()

    def enter(self, turn, per, turns):
        self.at, self.after, self.per, self.n = self.at + self.n + turn * per, self.at + self.n + turns * per, per, 0

    def leave(self):
        assert self.n == self.per, (self.n, self.per)
        self.at, self.n = self.after, 0

    def end(self):
        self.count.base = self.at + self.n


def row(r, name):
    at, n = ROW_AT[name]
    return r[:, at:at + n]


def mid(ap, n):
    return ap.unsqueeze(1).broadcast_to([ap.shape[0], n, ap.shape[1]])


def last(ap, n):
    return ap.unsqueeze(2).broadcast_to([ap.shape[0], ap.shape[1], n])


def constants(nc, c, ins):
    with nc.Block() as block:
        @block.sync
        def _(sp):
            sp.dma_start(c.x[:, :, :].rearrange("p t f -> p (t f)"), ins["x"]).then_inc(c.loaded.sem, 16)
            sp.dma_start(c.rows[:, :], ins["rows"].broadcast_to([P, ROWS_LEN])).then_inc(c.loaded.sem, 16)
            sp.wait_ge(c.loaded.sem, 32)
            c.loaded.base = 32

        @block.gpsimd
        def _(pool):
            g = Steps(pool, c.pool_step)
            g.did(nc.gpsimd.iota(c.itmp[:, :], pattern=[[1, 512]], base=0, channel_multiplier=0))
            g.do(nc.gpsimd.iota(c.ptmp[:, :], pattern=[[1, 1]], base=0, channel_multiplier=1))
            g.did(nc.gpsimd.tensor_copy(c.iota[:, :], c.itmp[:, :]))
            g.did(nc.gpsimd.tensor_copy(c.part[:, :], c.ptmp[:, :]))
            g.did(nc.gpsimd.memset(c.ones[:, :], 1.0))
            g.end()
            made = c.pool_step.base

        @block.vector
        def _(dve):
            v = Steps(dve, c.dve_step)
            dve.wait_ge(c.pool_step.sem, c.pool_step.base)
            v.did(nc.vector.tensor_scalar(c.ident[:, :], c.iota[:, 0:P], c.part[:, 0:1], None, ALU.is_equal))
            v.did(nc.vector.tensor_scalar(c.lower[:, :], c.iota[:, 0:P], c.part[:, 0:1], None, ALU.is_gt))
            v.did(nc.vector.tensor_scalar(c.pick[:, :, :], last(c.iota[0:HEADS, 0:HEADS], P), c.part[0:HEADS, 0:1],
                                          None, ALU.is_equal))
            v.did(nc.vector.memset(c.zero[:, :], 0.0))
            v.did(nc.vector.memset(c.valid[:, :], 1.0))
            v.wait()
            v.did(nc.vector.memset(c.valid[:, BUCKETS:T], 0.0))
            v.did(nc.vector.tensor_scalar(c.valid[:, BUCKETS - 1:BUCKETS], c.part[:, 0:1],
                                          float(NODES - (BUCKETS - 1) * P), None, ALU.is_lt))
            v.did(nc.vector.memset(c.eps[:, :], EPS))
            v.end()


def place_edges(nc, c, dst, src, edges, chunks, out):
    E, J = edges
    with (
        nc.sbuf_tensor(f"dst_{chunks}", [E, J], I32) as di, nc.sbuf_tensor(f"src_{chunks}", [E, J], I32) as si,
        nc.sbuf_tensor(f"hi_{chunks}", [E, J], F32) as hi, nc.sbuf_tensor(f"tag_{chunks}", [E, J], F32) as tag,
        nc.sbuf_tensor(f"slot_{chunks}", [E, J], F32) as slot, nc.sbuf_tensor(f"ti_{chunks}", [E, J], I32) as ti,
        nc.sbuf_tensor(f"tj_{chunks}", [E, J], I32) as tj,
        nc.sbuf_tensor(f"pp_{chunks}", [E, J], F32) as pp, nc.sbuf_tensor(f"kk_{chunks}", [E, J], F32) as kk,
        nc.sbuf_tensor(f"oh_{chunks}", [E, BUCKETS * J], F32) as oh, nc.sbuf_tensor(f"pre_{chunks}", [E, BUCKETS * J], F32) as pre,
        nc.sbuf_tensor(f"tot_{chunks}", [P, 8, 32], F32) as tot, nc.sbuf_tensor(f"toti_{chunks}", [P, 32], I32) as toti,
        nc.sbuf_tensor(f"at_{chunks}", [1, chunks, BUCKETS], F32) as atk, nc.sbuf_tensor(f"am_{chunks}", [1, chunks], F32) as am,
        nc.sbuf_tensor(f"a1_{chunks}", [E, 4, P], F32) as a1, nc.sbuf_tensor(f"a2_{chunks}", [E, 4, chunks], F32) as a2,
        nc.sbuf_tensor(f"gi_{chunks}", [P, chunks], I32) as gi,
        nc.psum_tensor(f"base_{chunks}", [P, 64], F32) as basep, nc.psum_tensor(f"grid_{chunks}", [P, 512], F32) as grid,
        nc.Block() as block,
    ):
        counts_at, ready_at, used_at, prefix_at = c.totals.base + 1, c.onehots.base, c.placed.base, c.prefixes.base + 1
        loaded_at = c.loaded.base + 32

        @block.sync
        def _(sp):
            sp.dma_start(di[:, :], dst).then_inc(c.loaded.sem, 16)
            sp.dma_start(si[:, :], src).then_inc(c.loaded.sem, 16)
            sp.wait_ge(c.loaded.sem, loaded_at)

        @block.vector
        def _(dve):
            v = Steps(dve, c.dve_step)
            nv = nc.vector
            dve.wait_ge(c.loaded.sem, loaded_at)
            v.did(nv.tensor_scalar(ti[:, :], di[:, :], 7, None, ALU.arith_shift_right))
            v.did(nv.tensor_scalar(tj[:, :], di[:, :], P - 1, None, ALU.bitwise_and))
            v.do(nv.tensor_scalar(tag[:, :], si[:, :], 256.0, 1.0, ALU.mult, ALU.add))
            v.did(nv.tensor_copy(hi[:, :], ti[:, :]))
            v.do(nv.tensor_tensor(tag[:, :], tag[:, :], tj[:, :], ALU.add))
            oh3, pre3 = (x[:, :].rearrange("p (b j) -> p b j", b=BUCKETS) for x in (oh, pre))
            v.do(nv.tensor_tensor(oh3, mid(hi[:, :], BUCKETS), last(c.iota[0:E, 0:BUCKETS], J), ALU.is_equal))
            v.do(nv.tensor_tensor_scan(pre[:, :], oh[:, :], c.zero[0:E, 0:1].broadcast_to([E, BUCKETS * J]), 0.0, ALU.add, ALU.add))
            v.did(nv.memset(tot[:, :, :], 0.0))
            v.wait()
            v.do(nv.tensor_copy(tot[0:E, 0, 1:BUCKETS + 1], pre3[:, :, J - 1]))
            nv.tensor_tensor(tot[0:E, 1, 0:BUCKETS], tot[0:E, 0, 1:BUCKETS + 1], tot[0:E, 0, 0:BUCKETS],
                             ALU.subtract).then_inc(c.totals.sem, 1)
            dve.wait_ge(c.prefixes.sem, prefix_at)
            v.do(nv.tensor_scalar(tot[:, 2, 0:BUCKETS], basep[:, 32:32 + BUCKETS], float(P - 1), None, ALU.add))
            v.do(nv.tensor_copy(toti[:, 0:BUCKETS], tot[:, 2, 0:BUCKETS]))
            v.do(nv.tensor_scalar(toti[:, 0:BUCKETS], toti[:, 0:BUCKETS], 7, None, ALU.arith_shift_right))
            v.do(nv.tensor_copy(tot[:, 3, 0:BUCKETS], toti[:, 0:BUCKETS]))
            v.do(nv.tensor_tensor_scan(tot[:, 4, 0:BUCKETS], tot[:, 3, 0:BUCKETS], tot[:, 7, 0:BUCKETS], 0.0, ALU.add, ALU.add))
            v.do(nv.tensor_tensor(tot[:, 5, 0:BUCKETS], tot[:, 4, 0:BUCKETS], tot[:, 3, 0:BUCKETS], ALU.subtract))
            v.do(nv.scalar_tensor_tensor(tot[:, 6, 0:BUCKETS], tot[:, 5, 0:BUCKETS], float(P), basep[:, 0:BUCKETS],
                                         ALU.mult, ALU.add))
            v.do(nv.tensor_tensor(tot[0:E, 6, 0:BUCKETS], tot[0:E, 6, 0:BUCKETS], tot[0:E, 0, 0:BUCKETS], ALU.subtract))
            v.do(nv.tensor_scalar(tot[0:E, 6, 0:BUCKETS], tot[0:E, 6, 0:BUCKETS], -1.0, None, ALU.add))
            v.do(nv.tensor_tensor(pre3, pre3, last(tot[0:E, 6, 0:BUCKETS], J), ALU.add))
            v.do(nv.tensor_tensor(oh3, pre3, oh3, ALU.mult))
            v.do(nv.tensor_reduce(slot[:, :], oh[:, :].rearrange("p (b j) -> p j b", b=BUCKETS), AX.X, ALU.add))
            v.do(nv.tensor_copy(ti[:, :], slot[:, :]))
            v.do(nv.tensor_scalar(tj[:, :], ti[:, :], P - 1, None, ALU.bitwise_and))
            v.did(nv.tensor_copy(pp[:, :], tj[:, :]))
            v.do(nv.tensor_scalar(ti[:, :], ti[:, :], 7, None, ALU.arith_shift_right))
            v.did(nv.tensor_copy(kk[:, :], ti[:, :]))
            v.do(nv.tensor_tensor(atk[:, :, :], last(c.iota[0:1, 0:chunks], BUCKETS), mid(tot[0:1, 5, 0:BUCKETS], chunks), ALU.is_ge))
            v.do(nv.tensor_reduce(am[:, :], atk[:, :, :], AX.X, ALU.add))
            v.do(nv.tensor_scalar(out.tile[:, :], am[:, :], -1.0, None, ALU.add))
            with dve.Fori(0, J // 4) as i:
                for u in range(4):
                    j = i * 4 + u
                    dve.wait_ge(c.placed.sem, used_at + i * 4 + (u - 2))
                    nv.tensor_scalar(a1[:, u, :], c.iota[0:E, 0:P], pp[:, bass.ds(j, 1)], None, ALU.is_equal)
                    nv.tensor_scalar(a2[:, u, :], c.iota[0:E, 0:chunks], kk[:, bass.ds(j, 1)], tag[:, bass.ds(j, 1)],
                                     ALU.is_equal, ALU.mult).then_inc(c.onehots.sem, 1)
            dve.wait_ge(c.placed.sem, used_at + J + 2)
            v.do(nv.tensor_copy(gi[:, :], grid[:, 0:chunks]))
            v.did(nv.tensor_scalar(out.src[:, 0:chunks], gi[:, :], 8, None, ALU.arith_shift_right))
            v.did(nv.memset(out.src[:, chunks:chunks + RING], 0))
            v.do(nv.tensor_scalar(gi[:, :], gi[:, :], 255, None, ALU.bitwise_and))
            v.do(nv.tensor_scalar(out.place[:, :], gi[:, :], -1.0, None, ALU.add))
            v.end()

        @block.tensor
        def _(pe):
            pe.wait_ge(c.totals.sem, counts_at)
            nc.tensor.matmul(basep[:, 0:BUCKETS], c.lower[0:E, :], tot[0:E, 1, 0:BUCKETS], start=True, stop=True)
            nc.tensor.matmul(basep[:, 32:32 + BUCKETS], c.ones[0:E, :], tot[0:E, 1, 0:BUCKETS], start=True,
                             stop=True).then_inc(c.prefixes.sem, 1)
            nc.tensor.matmul(grid[:, 0:chunks], c.zero[0:E, :], c.zero[0:E, 0:1].broadcast_to([E, chunks]),
                             start=True, stop=False).then_inc(c.placed.sem, 1)
            with pe.Fori(0, J // 4) as i:
                for u in range(4):
                    pe.wait_ge(c.onehots.sem, ready_at + i * 4 + (u + 1))
                    nc.tensor.matmul(grid[:, 0:chunks], a1[:, u, :], a2[:, u, :], start=False,
                                     stop=False).then_inc(c.placed.sem, 1)
            nc.tensor.matmul(grid[:, 0:chunks], c.zero[0:E, :], c.zero[0:E, 0:1].broadcast_to([E, chunks]),
                             start=False, stop=True).then_inc(c.placed.sem, 1)

        c.loaded.base, c.totals.base, c.prefixes.base = loaded_at, counts_at, prefix_at
        c.onehots.base, c.placed.base = ready_at + J, used_at + J + 2


def layer_stats(nc, c):
    with nc.sbuf_tensor(f"bn{c.fresh()}", [P, T, 6], F32) as bn, nc.Block() as block:
        mean, rstd = c.stat[:, :, 0], c.stat[:, :, 1]

        @block.vector
        def _(dve):
            v = Steps(dve, c.dve_step)
            nv = nc.vector
            with dve.Fori(0, T // 2) as i:
                v.enter(i, 2, T // 2)
                for u in range(2):
                    v.did(nv.bn_stats(flat(bn[:, bass.ds(i * 2 + u, 1), :]), flat(c.x[:, bass.ds(i * 2 + u, 1), :])))
                v.leave()
            v.wait()
            v.did(nv.tensor_tensor(mean, bn[:, :, 1], bn[:, :, 4], ALU.add))
            v.do(nv.tensor_tensor(rstd, bn[:, :, 1], bn[:, :, 4], ALU.subtract))
            v.do(nv.tensor_tensor(rstd, rstd, rstd, ALU.mult))
            v.did(nv.tensor_scalar(mean, mean, 0.5, None, ALU.mult))
            v.do(nv.tensor_scalar(rstd, rstd, 0.25, None, ALU.mult))
            v.do(nv.scalar_tensor_tensor(rstd, bn[:, :, 2], 1.0 / D, rstd, ALU.mult, ALU.add))
            v.did(nv.scalar_tensor_tensor(rstd, bn[:, :, 5], 1.0 / D, rstd, ALU.mult, ALU.add))
            dve.wait_ge(c.act_step.sem, c.act_step.base + 1)
            v.did(nv.reciprocal(rstd, rstd))
            v.end()

        @block.scalar
        def _(act):
            a = Steps(act, c.act_step)
            act.wait_ge(c.dve_step.sem, c.dve_step.base - 1)
            a.did(nc.scalar.activation(rstd, rstd, ACT.Sqrt, bias=c.eps[:, 0:1]))
            a.end()


def weighted_rows(nc, c):
    with nc.sbuf_tensor("w_soft", [P, D], F32) as w, nc.sbuf_tensor("w_m", [P, 4], F32) as m, nc.Block() as block:
        @block.vector
        def _(dve):
            v = Steps(dve, c.dve_step)
            nv = nc.vector
            v.do(nv.tensor_reduce(m[:, 0:1], row(c.rows, "raw"), AX.X, ALU.max))
            v.did(nv.tensor_scalar(m[:, 1:2], m[:, 0:1], -1.0, None, ALU.mult))
            negated = v.at + v.n
            v.did(nv.memset(c.table[:, :, :], 0.0))
            v.wait()
            v.did(nv.memset(c.table[:, :, D:D + 1], 1.0))
            dve.wait_ge(c.act_step.sem, c.act_step.base + 1)
            v.do(nv.reciprocal(m[:, 3:4], m[:, 2:3]))
            v.do(nv.tensor_scalar(w[:, :], w[:, :], m[:, 3:4], None, ALU.mult))
            with dve.Fori(0, T) as t:
                v.enter(t, 2, T)
                v.do(normalized(nc, c, c.table[:, bass.ds(t, 1), 0:D].rearrange("p t f -> p (t f)"), t))
                tab = c.table[:, bass.ds(t, 1), 0:D].rearrange("p t f -> p (t f)")
                v.did(nv.tensor_tensor(tab, tab, w[:, :], ALU.mult))
                v.leave()
            v.end()
            c.negated = negated

        @block.scalar
        def _(act):
            a = Steps(act, c.act_step)
            act.wait_ge(c.dve_step.sem, c.negated)
            a.did(nc.scalar.activation(w[:, :], row(c.rows, "raw"), ACT.Exp, bias=m[:, 1:2], accum_out=m[:, 2:3]))
            a.end()


def normalized(nc, c, out, t):
    return nc.vector.tensor_scalar(out, c.x[:, bass.ds(t, 1), :].rearrange("p t f -> p (t f)"),
                                   c.stat[:, bass.ds(t, 1), 0], c.stat[:, bass.ds(t, 1), 1], ALU.subtract, ALU.mult)


def store_table(nc, c, table, dram):
    with nc.Block() as block:
        @block.sync
        def _(sp):
            sp.dma_start(dram.rearrange("(t p) f -> p t f", p=P), table[:, :, :]).then_inc(c.stored.sem, 16)
            c.stored.base += 16
            sp.wait_ge(c.stored.sem, c.stored.base)


def dense(nc, c, halves, width, weights, prep, post, per_prep, per_post, extra=None):
    n = c.fresh()
    turns = T // 2
    rows_at, flip_at, flat_at, prod_at, taken_at = (s.base for s in (c.rows_in, c.flipped, c.feature_major, c.product, c.taken))
    with (
        nc.sbuf_tensor(f"rows{n}", [P, 2, halves * P], F32) as a, nc.sbuf_tensor(f"rowsT{n}", [P, 2, halves, P], F32) as at,
        nc.psum_tensor(f"flip{n}", [P, 2, 512], F32) as flip, nc.psum_tensor(f"prod{n}", [P, 2, 512], F32) as prod,
        nc.Block() as block,
    ):
        @block.vector
        def _(dve):
            v = Steps(dve, c.dve_step)
            with dve.Fori(0, turns) as i:
                v.enter(i, 2 * (per_prep + per_post), turns)
                for u in range(2):
                    dve.wait_ge(c.flipped.sem, flip_at + i * 2 + (u - 1))
                    prep(v, i * 2 + u, a[:, u, :]).then_inc(c.rows_in.sem, 1)
                for u in range(2):
                    dve.wait_ge(c.product.sem, prod_at + i * 2 + u + 1)
                    post(v, i * 2 + u, prod[:, u, 0:width]).then_inc(c.taken.sem, 1)
                v.leave()
            v.end()

        @block.tensor
        def _(pe):
            with pe.Fori(0, turns) as i:
                for u in range(2):
                    pe.wait_ge(c.rows_in.sem, rows_at + i * 2 + u + 1)
                    pe.wait_ge(c.feature_major.sem, flat_at + i * 2 + (u - 1))
                    for h in range(halves):
                        ins = nc.tensor.transpose(flip[:, u, h * P:(h + 1) * P], a[:, u, h * P:(h + 1) * P], c.ident[:, :])
                    ins.then_inc(c.flipped.sem, 1)
                for u in range(2):
                    pe.wait_ge(c.feature_major.sem, flat_at + i * 2 + u + 1)
                    pe.wait_ge(c.taken.sem, taken_at + i * 2 + (u - 1))
                    for h in range(halves):
                        ins = nc.tensor.matmul(prod[:, u, 0:width], at[:, u, h, :], weights(h), start=(h == 0), stop=(h == halves - 1))
                    ins.then_inc(c.product.sem, 1)

        @block.scalar
        def _(act):
            with act.Fori(0, turns) as i:
                for u in range(2):
                    act.wait_ge(c.flipped.sem, flip_at + i * 2 + u + 1)
                    act.wait_ge(c.product.sem, prod_at + i * 2 + (u - 1))
                    nc.scalar.copy(at[:, u, :, :].rearrange("p h n -> p (h n)"), flip[:, u, 0:halves * P]).then_inc(c.feature_major.sem, 1)

        for s in (c.rows_in, c.flipped, c.feature_major, c.product, c.taken):
            s.base += T


def gather_sum(nc, c, table, width, heads, slots, chunks, acc):
    n = c.fresh()
    W = width + (HEADS if heads else ROW - D)
    turns = chunks // RING
    index_at, gathered_at, onehot_at = c.indexed.base, c.gather_base, c.onehots.base
    summed_at, added_at, ready_at = c.summed.base, c.added.base, c.ready.base
    flip_at, flat_at, looked_at, expo_at, loaded_at = (s.base for s in (c.flipped, c.feature_major, c.looked, c.expo, c.loaded))
    quads = 2
    with (
        nc.sbuf_tensor(f"g{n}", [P, RING, W], F32) as g, nc.sbuf_tensor(f"oh{n}", [P, RING, P], F32) as oh,
        nc.sbuf_tensor(f"idx{n}", [P, RING], I32) as idx, nc.sbuf_tensor(f"ohT{n}", [P, 4, P], F32) as oht,
        nc.sbuf_tensor(f"e{n}", [P, 2, 4, HEADS], F32) as e, nc.sbuf_tensor(f"e2{n}", [P, 2, 4, HEADS], F32) as e2,
        nc.sbuf_tensor(f"p{n}", [P, 2, 4, HEADS], F32) as pr,
        nc.psum_tensor(f"sum{n}", [P, 4, 512], F32) as total, nc.psum_tensor(f"flip{n}", [P, 2, 512], F32) as flip,
        nc.psum_tensor(f"look{n}", [P, 2, 4, 2 * HEADS], F32) as look,
        nc.Block() as block,
    ):
        @block.gpsimd
        def _(pool):
            freed = pool.alloc_register(f"freed{n}")
            pool.reg_mov(freed, summed_at + 1 - RING)
            with pool.Fori(0, turns) as i:
                for u in range(RING):
                    pool.wait_ge(c.indexed.sem, index_at + i * RING + (u + 1))
                    pool.wait_ge(c.summed.sem, freed)
                    pool.reg_add(freed, freed, 1)
                    nc.gpsimd.indirect_dma_start(
                        out=g[:, u, :], out_offset=None, in_=table,
                        in_offset=bass.IndirectOffsetOnAxis(ap=idx[:, u:u + 1], axis=0)).then_inc(c.gathered[u], 16)

        @block.scalar
        def _(act):
            for u in range(RING):
                nc.scalar.copy(idx[:, u:u + 1], slots.src[:, u:u + 1]).then_inc(c.indexed.sem, 1)
            with act.Fori(0, turns) as i:
                for u in range(RING):
                    if heads:
                        act.wait_ge(c.flipped.sem, flip_at + i * RING + (u + 1))
                        act.wait_ge(c.looked.sem, looked_at + i * RING + (u + 1 - 4))
                        nc.scalar.copy(oht[:, u % 4, :], flip[:, u % 2, 0:P]).then_inc(c.feature_major.sem, 1)
                    if heads and u % 4 == 3:
                        q = u // 4
                        act.wait_ge(c.ready.sem, ready_at + i * quads + (q + 1))
                        nc.scalar.activation(pr[:, q, :, 0:heads], e[:, q, :, 0:heads], ACT.Exp).then_inc(c.expo.sem, 1)
                    if u % 4 == 3:
                        for w in range(u - 3, u + 1):
                            act.wait_ge(c.gathered[w], gathered_at + i * 16 + 16)
                            nc.scalar.copy(idx[:, w:w + 1], slots.src[:, bass.ds(i * RING + (w + RING), 1)]).then_inc(c.indexed.sem, 1)

        @block.vector
        def _(dve):
            nv = nc.vector
            v = Steps(dve, c.dve_step)
            with dve.Fori(0, turns) as i:
                v.enter(i, (4 if heads else 0), turns)
                for u in range(RING):
                    dve.wait_ge(c.summed.sem, summed_at + i * RING + (u + 1 - RING))
                    nv.tensor_scalar(oh[:, u, :], c.iota[:, 0:P], slots.place[:, bass.ds(i * RING + u, 1)], None,
                                     ALU.is_equal).then_inc(c.onehots.sem, 1)
                for q in range(quads):
                    us = range(4 * q, 4 * q + 4)
                    if heads:
                        for u in us:
                            dve.wait_ge(c.gathered[u], gathered_at + i * 16 + 16)
                        dve.wait_ge(c.looked.sem, looked_at + i * RING + (4 * q + 4))
                        es = g[:, 4 * q:4 * q + 4, width:width + heads]
                        v.do(nv.tensor_tensor(e2[:, q, :, 0:heads], es, look[:, q, :, 0:heads], ALU.add))
                        v.do(nv.scalar_tensor_tensor(e2[:, q, :, 0:heads], e2[:, q, :, 0:heads], 0.2, e2[:, q, :, 0:heads], ALU.mult, ALU.max))
                        nv.tensor_tensor(e[:, q, :, 0:heads], e2[:, q, :, 0:heads], look[:, q, :, HEADS:HEADS + heads],
                                         ALU.subtract).then_inc(c.ready.sem, 1)
                        dve.wait_ge(c.expo.sem, expo_at + i * quads + (q + 1))
                        C = width // heads
                        for u in us:
                            gv = g[:, u, 0:width].rearrange("p (h c) -> p h c", h=heads)
                            nv.tensor_tensor(gv, gv, last(pr[:, q, u % 4, 0:heads], C), ALU.mult)
                            nv.tensor_copy(g[:, u, width:width + heads], pr[:, q, u % 4, 0:heads]).then_inc(c.weighted.sem, 1)
                    for u in us:
                        t = dve.value_load(slots.tile[0:1, bass.ds(i * RING + u, 1)], min_val=0, max_val=BUCKETS - 1)
                        dve.wait_ge(c.summed.sem, summed_at + i * RING + (u + 1))
                        dve.wait_ge(c.added.sem, added_at + i * RING + u)
                        at = acc[:, bass.ds(t, 1), :].rearrange("p t f -> p (t f)")
                        nv.tensor_tensor(at, at, total[:, u % 4, 0:W], ALU.add).then_inc(c.added.sem, 1)
                v.leave()
            v.end()

        @block.tensor
        def _(pe):
            weighted_at = c.weighted.base
            with pe.Fori(0, turns) as i:
                def look_up(u):
                    pe.wait_ge(c.onehots.sem, onehot_at + i * RING + (u + 1))
                    pe.wait_ge(c.feature_major.sem, flat_at + i * RING + (u - 1))
                    nc.tensor.transpose(flip[:, u % 2, 0:P], oh[:, u, :], c.ident[:, :]).then_inc(c.flipped.sem, 1)
                for q in range(quads):
                    if heads:
                        for u in range(4 * q, 4 * q + 4):
                            look_up(u)
                            t = pe.value_load(slots.tile[0:1, bass.ds(i * RING + u, 1)], min_val=0, max_val=BUCKETS - 1)
                            pe.wait_ge(c.feature_major.sem, flat_at + i * RING + (u + 1))
                            pe.wait_ge(c.ready.sem, ready_at + i * quads + (q + 1 - quads))
                            nc.tensor.matmul(look[:, q, u % 4, :], oht[:, u % 4, :], c.edm[:, bass.ds(t * 2 * HEADS, 2 * HEADS)],
                                             start=True, stop=True).then_inc(c.looked.sem, 1)
                    for u in range(4 * q, 4 * q + 4):
                        if heads:
                            pe.wait_ge(c.weighted.sem, weighted_at + i * RING + (u + 1))
                        else:
                            pe.wait_ge(c.onehots.sem, onehot_at + i * RING + (u + 1))
                            pe.wait_ge(c.gathered[u], gathered_at + i * 16 + 16)
                        pe.wait_ge(c.added.sem, added_at + i * RING + (u + 1 - 4))
                        nc.tensor.matmul(total[:, u % 4, 0:W], oh[:, u, :], g[:, u, :], start=True, stop=True).then_inc(c.summed.sem, 1)

    c.indexed.base += chunks + RING
    c.gather_base += 16 * turns
    for s in (c.onehots, c.summed, c.added):
        s.base += chunks
    if heads:
        for s in (c.flipped, c.feature_major, c.looked, c.weighted):
            s.base += chunks
        for s in (c.ready, c.expo):
            s.base += quads * turns


def segment_max(nc, c, table, width, heads, slots, chunks):
    n = c.fresh()
    W = width + HEADS
    gathered_at, loaded_at = c.max_gathered.base, c.loaded.base
    index_at, onehot_at, flip_at, flat_at, spread_at, done_at = (
        s.base for s in (c.indexed, c.onehots, c.flipped, c.feature_major, c.looked, c.added))
    with (
        nc.sbuf_tensor(f"mg{n}", [P, W], F32) as g, nc.sbuf_tensor(f"moh{n}", [P, P], F32) as oh,
        nc.sbuf_tensor(f"midx{n}", [P, 1], I32) as idx, nc.sbuf_tensor(f"mesT{n}", [HEADS, P], F32) as est,
        nc.sbuf_tensor(f"mfar{n}", [P, P], F32) as far, nc.sbuf_tensor(f"mv{n}", [P, HEADS, P], F32) as val,
        nc.sbuf_tensor(f"mc{n}", [P, HEADS], F32) as cm,
        nc.psum_tensor(f"mflip{n}", [P, P], F32) as flip, nc.psum_tensor(f"mest{n}", [HEADS, P], F32) as estp,
        nc.psum_tensor(f"mspread{n}", [P, HEADS, P], F32) as spread, nc.Block() as block,
    ):
        @block.scalar
        def _(act):
            with act.Fori(0, chunks) as k:
                act.wait_ge(c.added.sem, done_at + k)
                nc.scalar.copy(idx[:, :], slots.src[:, bass.ds(k, 1)]).then_inc(c.indexed.sem, 1)
                act.wait_ge(c.flipped.sem, flip_at + k + 1)
                nc.scalar.copy(est[0:heads, :], estp[0:heads, :]).then_inc(c.feature_major.sem, 1)

        @block.gpsimd
        def _(pool):
            asked = pool.alloc_register(f"asked{n}")
            pool.reg_mov(asked, index_at + 1)
            with pool.Fori(0, chunks) as k:
                pool.wait_ge(c.indexed.sem, asked)
                pool.reg_add(asked, asked, 1)
                nc.gpsimd.indirect_dma_start(out=g[:, :], out_offset=None, in_=table,
                                             in_offset=bass.IndirectOffsetOnAxis(ap=idx[:, 0:1], axis=0)).then_inc(c.max_gathered.sem, 16)

        @block.tensor
        def _(pe):
            with pe.Fori(0, chunks) as k:
                pe.wait_ge(c.onehots.sem, onehot_at + k + 1)
                nc.tensor.transpose(flip[:, :], oh[:, :], c.ident[:, :])
                pe.wait_ge(c.max_gathered.sem, gathered_at + k * 16 + 16)
                nc.tensor.transpose(estp[0:heads, :], g[:, width:width + heads], c.ident[:, :]).then_inc(c.flipped.sem, 1)
                pe.wait_ge(c.feature_major.sem, flat_at + k + 1)
                for h in range(heads):
                    ins = nc.tensor.matmul(spread[:, h, :], c.pick[0:heads, h, :], est[0:heads, :], start=True, stop=True)
                ins.then_inc(c.looked.sem, 1)

        @block.vector
        def _(dve):
            nv = nc.vector
            v = Steps(dve, c.dve_step)
            with dve.Fori(0, chunks) as k:
                v.enter(k, 3, chunks)
                nv.tensor_scalar(oh[:, :], c.iota[:, 0:P], slots.place[:, bass.ds(k, 1)], None, ALU.is_equal).then_inc(c.onehots.sem, 1)
                t = dve.value_load(slots.tile[0:1, bass.ds(k, 1)], min_val=0, max_val=BUCKETS - 1)
                dve.wait_ge(c.flipped.sem, flip_at + k + 1)
                v.do(nv.tensor_scalar(far[:, :], flip[:, :], -1.0, FAR, ALU.add, ALU.mult))
                dve.wait_ge(c.looked.sem, spread_at + k + 1)
                v.do(nv.tensor_tensor(val[:, 0:heads, :], spread[:, 0:heads, :], mid(far[:, :], heads), ALU.add))
                v.do(nv.tensor_reduce(cm[:, 0:heads], val[:, 0:heads, :], AX.X, ALU.max))
                at = c.top[:, bass.ds(t, 1), 0:heads].rearrange("p t h -> p (t h)")
                nv.tensor_tensor(at, at, cm[:, 0:heads], ALU.max).then_inc(c.added.sem, 1)
                dve.wait_ge(c.added.sem, done_at + k + 1)
                v.leave()
            v.end()
    c.max_gathered.base += 16 * chunks
    for s in (c.indexed, c.onehots, c.flipped, c.feature_major, c.looked, c.added):
        s.base += chunks


def attend(nc, c, table, dram, width, heads, slots, chunks, acc):
    C = width // heads
    store_table(nc, c, table, dram)
    with nc.Block() as block:
        @block.vector
        def _(dve):
            v = Steps(dve, c.dve_step)
            v.do(nc.vector.tensor_copy(c.top[:, :, 0:heads], table[:, :, width:width + heads]))
            v.end()
    segment_max(nc, c, dram, width, heads, slots, chunks)
    edm = c.edm[:, :].rearrange("p (t k) -> p t k", t=T)
    with nc.sbuf_tensor(f"self{c.fresh()}", [P, T, 3 * HEADS], F32) as s, nc.Block() as block:
        @block.vector
        def _(dve):
            v = Steps(dve, c.dve_step)
            nv = nc.vector
            es, a, b = table[:, :, width:width + heads], s[:, :, 0:heads], s[:, :, HEADS:HEADS + heads]
            ed, m = edm[:, :, 0:heads], edm[:, :, HEADS:HEADS + heads]
            v.did(nv.memset(c.edm[:, :], 0.0))
            v.did(nv.memset(acc[:, :, width:width + HEADS], 0.0))
            v.wait()
            v.did(nv.tensor_copy(ed, c.ed[:, :, 0:heads]))
            v.do(nv.tensor_tensor(b, c.top[:, :, 0:heads], c.ed[:, :, 0:heads], ALU.add))
            v.do(nv.scalar_tensor_tensor(m, b, 0.2, b, ALU.mult, ALU.max))
            v.do(nv.tensor_tensor(a, es, ed, ALU.add))
            v.do(nv.scalar_tensor_tensor(a, a, 0.2, a, ALU.mult, ALU.max))
            ready = v.did(nv.tensor_tensor(a, a, m, ALU.subtract)) + v.at
            c.self_ready = ready
            dve.wait_ge(c.act_step.sem, c.act_step.base + 1)
            for h in range(heads):
                v.did(nv.tensor_tensor(acc[:, :, h * C:(h + 1) * C], table[:, :, h * C:(h + 1) * C],
                                       s[:, :, 2 * HEADS + h].unsqueeze(2).broadcast_to([P, T, C]), ALU.mult))
            v.did(nv.tensor_copy(acc[:, :, width:width + heads], s[:, :, 2 * HEADS:2 * HEADS + heads]))
            v.end()

        @block.scalar
        def _(act):
            a = Steps(act, c.act_step)
            act.wait_ge(c.dve_step.sem, c.self_ready)
            a.did(nc.scalar.activation(s[:, :, 2 * HEADS:2 * HEADS + heads], s[:, :, 0:heads], ACT.Exp))
            a.end()
    gather_sum(nc, c, dram, width, heads, slots, chunks, acc)


def load(nc, c, pairs):
    with nc.Block() as block:
        @block.sync
        def _(sp):
            for dst, src in pairs:
                sp.dma_start(dst, src).then_inc(c.loaded.sem, 16)
                c.loaded.base += 16
            sp.wait_ge(c.loaded.sem, c.loaded.base)


def flat(ap):
    return ap.rearrange("p t f -> p (t f)")


def sage(nc, c, ins, k, slots):
    store_table(nc, c, c.table, c.dram)
    with nc.Block() as block:
        @block.vector
        def _(dve):
            v = Steps(dve, c.dve_step)
            v.did(nc.vector.memset(c.acc[:, :, :], 0.0))
            v.end()
    gather_sum(nc, c, c.dram, D, 0, slots, GRAPH_CHUNKS, c.acc)
    n = c.fresh()
    with nc.sbuf_tensor(f"sw{n}", [P, 4, D], F32) as w, nc.sbuf_tensor(f"rdeg{n}", [P, T], F32) as rdeg, \
            nc.sbuf_tensor(f"so{n}", [P, 2, D], F32) as o:
        load(nc, c, [(flat(w[:, :, :]), ins[f"sage{k}"])])
        with nc.Block() as block:
            @block.vector
            def _(dve):
                v = Steps(dve, c.dve_step)
                v.do(nc.vector.tensor_scalar(rdeg[:, :], c.acc[:, :, D], 1.0, None, ALU.max))
                v.do(nc.vector.reciprocal(rdeg[:, :], rdeg[:, :]))
                v.end()

        def prep(v, t, a):
            v.did(nc.vector.tensor_copy(a[:, 0:D], flat(c.table[:, bass.ds(t, 1), 0:D])))
            return nc.vector.tensor_scalar(a[:, D:2 * D], flat(c.acc[:, bass.ds(t, 1), 0:D]), rdeg[:, bass.ds(t, 1)], None, ALU.mult)

        def post(v, t, prod):
            u = v.parity
            v.parity ^= 1
            v.do(nc.vector.tensor_tensor(o[:, u, :], prod, row(c.rows, f"sb{k}"), ALU.add))
            tab = flat(c.table[:, bass.ds(t, 1), 0:D])
            if k == 1:
                return nc.vector.scalar_tensor_tensor(tab, o[:, u, :], 0.0, tab, ALU.max, ALU.add)
            v.do(nc.vector.scalar_tensor_tensor(o[:, u, :], o[:, u, :], 0.0, tab, ALU.max, ALU.add))
            x = flat(c.x[:, bass.ds(t, 1), :])
            return nc.vector.tensor_tensor(x, x, o[:, u, :], ALU.add)

        dense(nc, c, 4, D, lambda h: w[:, h, :], prep, post, 1, 1 if k == 1 else 2)


def ln_prep(nc, c):
    def prep(v, t, a):
        return normalized(nc, c, a, t)
    return prep


def gat_rows(nc, c, w, width, heads, table, from_acc=False):
    def prep(v, t, a):
        if from_acc:
            return nc.vector.tensor_copy(a, flat(c.acc[:, bass.ds(t, 1), 0:D]))
        return normalized(nc, c, a, t)

    def post(v, t, prod):
        v.did(nc.vector.tensor_copy(flat(table[:, bass.ds(t, 1), 0:width + heads]), prod[:, 0:width + heads]))
        return nc.vector.tensor_copy(flat(c.ed[:, bass.ds(t, 1), 0:heads]), prod[:, width + heads:width + 2 * heads])

    dense(nc, c, 2, width + 2 * heads, lambda h: w[:, h, :], prep, post, 0, 1)


def fold(nc, c, w, width, heads, src, dst):
    C = width // heads
    with nc.sbuf_tensor(f"fold{c.fresh()}", [P, 2, width], F32) as f, nc.Block() as block:
        @block.vector
        def _(dve):
            v = Steps(dve, c.dve_step)
            for n, name in enumerate((src, dst)):
                v.do(nc.vector.tensor_tensor(f[:, :, :], w[:, :, 0:width], mid(row(c.rows, name), 2), ALU.mult))
                for k in range(2):
                    v.do(nc.vector.tensor_reduce(w[:, k, width + n * heads:width + (n + 1) * heads],
                                                 f[:, k, :].rearrange("p (h c) -> p h c", h=heads), AX.X, ALU.add))
            v.end()


def gat_layer(nc, c, ins, slots):
    layer_stats(nc, c)
    with nc.sbuf_tensor("gw0", [P, 2, D + 2 * HEADS], F32) as w:
        load(nc, c, [(w[:, :, 0:D], ins["gw0"].rearrange("p (k f) -> p k f", k=2))])
        fold(nc, c, w, D, HEADS, "as0", "ad0")
        gat_rows(nc, c, w, D, HEADS, c.table)
    attend(nc, c, c.table, c.dram, D, HEADS, slots, GRAPH_CHUNKS, c.acc)
    with (
        nc.sbuf_tensor("bnrow", [P, 4, D], F32) as r, nc.psum_tensor("bnsum", [P, 2, 512], F32) as total, nc.Block() as block,
    ):
        full = c.acc[:, :, 0:D]
        tmp = c.table[:, :, 0:D]

        @block.vector
        def _(dve):
            v = Steps(dve, c.dve_step)
            nv = nc.vector
            v.do(nv.reciprocal(c.acc[:, :, D:D + HEADS], c.acc[:, :, D:D + HEADS]))
            for h in range(HEADS):
                part = c.acc[:, :, h * 64:(h + 1) * 64]
                v.did(nv.tensor_tensor(part, part, c.acc[:, :, D + h].unsqueeze(2).broadcast_to([P, T, 64]), ALU.mult))
            v.wait()
            v.do(nv.tensor_tensor(full, full, mid(row(c.rows, "gb0"), T), ALU.add))
            v.did(nv.tensor_tensor(full, full, last(c.valid[:, :], D), ALU.mult))
            c.bn1 = v.at + v.n
            dve.wait_ge(c.product.sem, c.product.base + 1)
            v.do(nv.tensor_scalar(r[:, 0, :], total[:, 0, 0:D], 1.0 / NODES, None, ALU.mult))
            v.do(nv.tensor_tensor(full, full, mid(r[:, 0, :], T), ALU.subtract))
            v.do(nv.tensor_tensor(full, full, last(c.valid[:, :], D), ALU.mult))
            v.did(nv.tensor_tensor(tmp, full, full, ALU.mult))
            c.bn2 = v.at + v.n
            dve.wait_ge(c.product.sem, c.product.base + 2)
            v.did(nv.tensor_scalar(r[:, 1, :], total[:, 1, 0:D], 1.0 / NODES, None, ALU.mult))
            c.bn3 = v.at + v.n
            dve.wait_ge(c.act_step.sem, c.act_step.base + 1)
            v.do(nv.reciprocal(r[:, 2, :], r[:, 2, :]))
            v.do(nv.tensor_tensor(r[:, 2, :], r[:, 2, :], row(c.rows, "gamma0"), ALU.mult))
            v.do(nv.tensor_tensor(full, full, mid(r[:, 2, :], T), ALU.mult))
            v.do(nv.tensor_tensor(full, full, mid(row(c.rows, "beta0"), T), ALU.add))
            v.did(nv.tensor_scalar(tmp, full, 0.0, None, ALU.min))
            c.bn4 = v.at + v.n
            dve.wait_ge(c.act_step.sem, c.act_step.base + 2)
            v.do(nv.scalar_tensor_tensor(full, full, 0.0, tmp, ALU.max, ALU.add))
            v.did(nv.tensor_scalar(full, full, -1.0, None, ALU.add))
            v.end()

        @block.scalar
        def _(act):
            a = Steps(act, c.act_step)
            act.wait_ge(c.dve_step.sem, c.bn3)
            a.did(nc.scalar.activation(r[:, 2, :], r[:, 1, :], ACT.Sqrt, bias=c.eps[:, 0:1]))
            act.wait_ge(c.dve_step.sem, c.bn4)
            a.did(nc.scalar.activation(tmp, tmp, ACT.Exp))
            a.end()

        @block.tensor
        def _(pe):
            for n, (at, what) in enumerate(((c.bn1, c.acc), (c.bn2, c.table))):
                pe.wait_ge(c.dve_step.sem, at)
                nc.tensor.matmul(total[:, n, 0:D], c.ones[:, :], what[:, 0, 0:D], start=True, stop=False)
                with pe.Fori(1, T - 1) as t:
                    nc.tensor.matmul(total[:, n, 0:D], c.ones[:, :], flat(what[:, bass.ds(t, 1), 0:D]), start=False, stop=False)
                nc.tensor.matmul(total[:, n, 0:D], c.ones[:, :], what[:, T - 1, 0:D], start=False, stop=True).then_inc(c.product.sem, 1)
            c.product.base += 2

    with nc.sbuf_tensor("gw1", [P, 2, D + 2], F32) as w:
        load(nc, c, [(w[:, :, 0:D], ins["gw1"].rearrange("p (k f) -> p k f", k=2))])
        fold(nc, c, w, D, 1, "as1", "ad1")
        with nc.Block() as block:
            @block.vector
            def _(dve):
                v = Steps(dve, c.dve_step)
                v.did(nc.vector.memset(c.table[:, :, D:ROW], 0.0))
                v.end()
        gat_rows(nc, c, w, D, 1, c.table, from_acc=True)
    attend(nc, c, c.table, c.dram, D, 1, slots, GRAPH_CHUNKS, c.acc)
    with nc.sbuf_tensor("nrm", [P, T, 2], F32) as nrm, nc.Block() as block:
        full, tmp = c.acc[:, :, 0:D], c.table[:, :, 0:D]

        @block.vector
        def _(dve):
            v = Steps(dve, c.dve_step)
            nv = nc.vector
            v.do(nv.reciprocal(nrm[:, :, 0], c.acc[:, :, D]))
            v.do(nv.tensor_tensor(full, full, last(nrm[:, :, 0], D), ALU.mult))
            v.do(nv.tensor_tensor(full, full, mid(row(c.rows, "gb1"), T), ALU.add))
            v.do(nv.tensor_tensor(tmp, full, full, ALU.mult))
            v.did(nv.tensor_reduce(nrm[:, :, 1], tmp, AX.X, ALU.add))
            c.squares = v.at + v.n
            dve.wait_ge(c.act_step.sem, c.act_step.base + 1)
            v.do(nv.tensor_scalar(nrm[:, :, 1], nrm[:, :, 1], 1e-12, None, ALU.max))
            v.do(nv.reciprocal(nrm[:, :, 1], nrm[:, :, 1]))
            v.do(nv.tensor_tensor(full, full, last(nrm[:, :, 1], D), ALU.mult))
            v.did(nv.tensor_tensor(c.x[:, :, :], c.x[:, :, :], full, ALU.add))
            v.end()

        @block.scalar
        def _(act):
            a = Steps(act, c.act_step)
            act.wait_ge(c.dve_step.sem, c.squares)
            a.did(nc.scalar.activation(nrm[:, :, 1], nrm[:, :, 1], ACT.Sqrt))
            a.end()


def slice_layer(nc, c, ins):
    SH, G = SLICE_HEADS, SLICE
    HG = SH * G
    layer_stats(nc, c)
    with (
        nc.sbuf_tensor("sw", [P, T, HG], F32) as sw, nc.sbuf_tensor("pooled", [P, 3, HG], F32) as pooled,
        nc.sbuf_tensor("zout", [P, 4, D], F32) as zout,
    ):
        with (
            nc.sbuf_tensor("wxT", [G, SH, D], F32) as wxt, nc.sbuf_tensor("wsl", [G, G], F32) as wsl,
            nc.sbuf_tensor("bx", [G, SH], F32) as bx, nc.sbuf_tensor("wl", [P, 2, HG], F32) as wl,
            nc.sbuf_tensor("bl", [P, HG], F32) as bl, nc.sbuf_tensor("invt", [P, SH], F32) as invt,
            nc.sbuf_tensor("bxw", [G, SH, P], F32) as bxw,
        ):
            load(nc, c, [(wxt[:, :, :].rearrange("p h k -> p (h k)"), ins["wxT"]), (wsl[:, :], ins["wslice"]), (bx[:, :], ins["bx"])])
            with nc.psum_tensor("wlp", [P, 2, 512], F32) as wlp, nc.psum_tensor("blp", [P, 512], F32) as blp, nc.Block() as block:
                @block.vector
                def _(dve):
                    v = Steps(dve, c.dve_step)
                    nv = nc.vector
                    v.did(nv.tensor_copy(bxw[:, :, :], last(bx[:, :], P)))
                    c.wide = v.at + v.n
                    v.do(nv.tensor_scalar(invt[:, :], row(c.rows, "temp"), 0.1, 5.0, ALU.max, ALU.min))
                    v.did(nv.reciprocal(invt[:, :], invt[:, :]))
                    dve.wait_ge(c.product.sem, c.product.base + 1)
                    v.did(nv.tensor_copy(wl[:, :, :], wlp[:, :, :]))
                    v.did(nv.tensor_tensor(bl[:, :].rearrange("p (h g) -> p h g", h=SH), blp[:, :].rearrange("p (h g) -> p h g", h=SH),
                                           mid(row(c.rows, "b_slice"), SH), ALU.add))
                    v.end()

                @block.tensor
                def _(pe):
                    pe.wait_ge(c.dve_step.sem, c.wide)
                    for h in range(SH):
                        for k in range(2):
                            nc.tensor.matmul(wlp[:, k, h * G:(h + 1) * G], wxt[:, h, k * P:(k + 1) * P], wsl[:, :], start=True, stop=True)
                        ins_ = nc.tensor.matmul(blp[:, h * G:(h + 1) * G], bxw[:, h, :], wsl[:, :], start=True, stop=True)
                    ins_.then_inc(c.product.sem, 1)
                    c.product.base += 1
            slice_weights(nc, c, sw, wl, bl, invt, pooled)
        slice_attention(nc, c, ins, pooled, zout)
        with nc.sbuf_tensor("so", [P, 2, D], F32) as o:
            def prep(v, t, a):
                return nc.vector.tensor_copy(a, flat(sw[:, bass.ds(t, 1), :]))

            def post(v, t, prod):
                u = v.parity
                v.parity ^= 1
                v.do(nc.vector.tensor_tensor(o[:, u, :], prod, row(c.rows, "b_out"), ALU.add))
                x = flat(c.x[:, bass.ds(t, 1), :])
                return nc.vector.tensor_tensor(x, x, o[:, u, :], ALU.add)

            dense(nc, c, 4, D, lambda h: zout[:, h, :], prep, post, 0, 1)


def slice_weights(nc, c, sw, wl, bl, invt, pooled):
    SH, G = SLICE_HEADS, SLICE
    HG = SH * G
    turns = T // 2
    rows_at, flip_at, flat_at, prod_at, ready_at, expo_at, weighted_at, pooled_at = (
        s.base for s in (c.rows_in, c.flipped, c.feature_major, c.product, c.ready, c.expo, c.weighted, c.taken))
    with (
        nc.sbuf_tensor("srows", [P, 2, D], F32) as a, nc.sbuf_tensor("srowsT", [P, 2, 2, P], F32) as at,
        nc.sbuf_tensor("slog", [P, 2, HG], F32) as lg, nc.sbuf_tensor("smx", [P, 2, 2, SH], F32) as mx,
        nc.psum_tensor("sflip", [P, 2, 512], F32) as flip, nc.psum_tensor("sprod", [P, 2, 512], F32) as prod,
        nc.psum_tensor("spool", [P, 3, 512], F32) as pool_, nc.Block() as block,
    ):
        @block.vector
        def _(dve):
            v = Steps(dve, c.dve_step)
            nv = nc.vector
            with dve.Fori(0, turns) as i:
                v.enter(i, 12, turns)
                for u in range(2):
                    dve.wait_ge(c.taken.sem, pooled_at + i * 2 + (u - 1))
                    normalized(nc, c, a[:, u, :], i * 2 + u).then_inc(c.rows_in.sem, 1)
                for u in range(2):
                    lv = lg[:, u, :].rearrange("p (h g) -> p h g", h=SH)
                    dve.wait_ge(c.product.sem, prod_at + i * 2 + u + 1)
                    v.do(nv.tensor_tensor(lg[:, u, :], prod[:, u, :], bl[:, :], ALU.add))
                    v.do(nv.tensor_tensor(lv, lv, last(invt[:, :], G), ALU.mult))
                    v.do(nv.tensor_reduce(mx[:, u, 0, :], lv, AX.X, ALU.max))
                    nv.tensor_tensor(lv, lv, last(mx[:, u, 0, :], G), ALU.subtract).then_inc(c.ready.sem, 1)
                for u in range(2):
                    t = i * 2 + u
                    sv = flat(sw[:, bass.ds(t, 1), :]).rearrange("p (h g) -> p h g", h=SH)
                    dve.wait_ge(c.expo.sem, expo_at + i * 2 + u + 1)
                    v.do(nv.tensor_reduce(mx[:, u, 1, :], sv, AX.X, ALU.add))
                    v.do(nv.reciprocal(mx[:, u, 1, :], mx[:, u, 1, :]))
                    v.do(nv.tensor_scalar(mx[:, u, 1, :], mx[:, u, 1, :], c.valid[:, bass.ds(t, 1)], None, ALU.mult))
                    nv.tensor_tensor(sv, sv, last(mx[:, u, 1, :], G), ALU.mult).then_inc(c.weighted.sem, 1)
                v.leave()
            dve.wait_ge(c.taken.sem, pooled_at + T + 1)
            v.did(nv.tensor_copy(pooled[:, :, :], pool_[:, :, :]))
            v.end()

        @block.scalar
        def _(act):
            with act.Fori(0, turns) as i:
                for u in range(2):
                    act.wait_ge(c.flipped.sem, flip_at + i * 2 + u + 1)
                    act.wait_ge(c.product.sem, prod_at + i * 2 + (u - 1))
                    nc.scalar.copy(at[:, u, :, :].rearrange("p h n -> p (h n)"), flip[:, u, 0:D]).then_inc(c.feature_major.sem, 1)
                for u in range(2):
                    act.wait_ge(c.ready.sem, ready_at + i * 2 + u + 1)
                    nc.scalar.activation(flat(sw[:, bass.ds(i * 2 + u, 1), :]), lg[:, u, :], ACT.Exp).then_inc(c.expo.sem, 1)

        @block.tensor
        def _(pe):
            zero = c.zero[:, 0:1].broadcast_to([P, 512])
            for n in range(3):
                nc.tensor.matmul(pool_[:, n, :], c.zero[:, :], zero, start=True, stop=False)
            with pe.Fori(0, turns) as i:
                for u in range(2):
                    pe.wait_ge(c.rows_in.sem, rows_at + i * 2 + u + 1)
                    pe.wait_ge(c.feature_major.sem, flat_at + i * 2 + (u - 1))
                    for h in range(2):
                        ins = nc.tensor.transpose(flip[:, u, h * P:(h + 1) * P], a[:, u, h * P:(h + 1) * P], c.ident[:, :])
                    ins.then_inc(c.flipped.sem, 1)
                for u in range(2):
                    pe.wait_ge(c.feature_major.sem, flat_at + i * 2 + u + 1)
                    pe.wait_ge(c.ready.sem, ready_at + i * 2 + (u - 1))
                    for h in range(2):
                        ins = nc.tensor.matmul(prod[:, u, :], at[:, u, h, :], wl[:, h, :], start=(h == 0), stop=(h == 1))
                    ins.then_inc(c.product.sem, 1)
                for u in range(2):
                    pe.wait_ge(c.weighted.sem, weighted_at + i * 2 + u + 1)
                    s = flat(sw[:, bass.ds(i * 2 + u, 1), :])
                    for n, left in enumerate((a[:, u, 0:P], a[:, u, P:D], c.ones[:, :])):
                        ins = nc.tensor.matmul(pool_[:, n, :], left, s, start=False, stop=False)
                    ins.then_inc(c.taken.sem, 1)
            for n in range(3):
                ins = nc.tensor.matmul(pool_[:, n, :], c.zero[:, :], zero, start=False, stop=True)
            ins.then_inc(c.taken.sem, 1)

        for s in (c.rows_in, c.flipped, c.feature_major, c.product, c.ready, c.expo, c.weighted):
            s.base += T
        c.taken.base += T + 1


def slice_attention(nc, c, ins, pooled, zout):
    SH, G = SLICE_HEADS, SLICE
    HG = SH * G
    with (
        nc.sbuf_tensor("wfx", [P, 2, HG], F32) as wfx, nc.sbuf_tensor("bfx", [G, SH], F32) as bfx,
        nc.sbuf_tensor("wqkv", [G, 3, G], F32) as wqkv, nc.sbuf_tensor("wo", [G, SH, D], F32) as wo,
        nc.sbuf_tensor("tok", [G, 9, HG], F32) as tok, nc.sbuf_tensor("amx", [G, 2, SH], F32) as amx,
    ):
        load(nc, c, [(wfx[:, :, :].rearrange("p k f -> p (k f)"), ins["wfx"]), (bfx[:, :], ins["bfx"]),
                     (wqkv[:, :, :].rearrange("p k f -> p (k f)"), ins["wqkv"]), (wo[:, :, :].rearrange("p k f -> p (k f)"), ins["wo"])])
        with (
            nc.psum_tensor("tokp", [G, 512], F32) as tokp, nc.psum_tensor("qkvp", [G, 3, 512], F32) as qkvp,
            nc.psum_tensor("attp", [G, 512], F32) as attp, nc.psum_tensor("atT", [G, 512], F32) as atp,
            nc.psum_tensor("zp", [P, 4, D], F32) as zp, nc.Block() as block,
        ):
            st, den, q, k, val, att, attT, osT = (tok[:, n, :] for n in range(8))
            hs = lambda x, h: x[:, h * G:(h + 1) * G]
            by_head = lambda x: x.rearrange("p (h g) -> p h g", h=SH)
            done = c.product.base

            @block.vector
            def _(dve):
                v = Steps(dve, c.dve_step)
                nv = nc.vector
                c.marks = []

                def mark():
                    c.marks.append(v.at + v.n)
                norm = pooled[0:G, 2, :]
                v.did(nv.tensor_tensor(by_head(st), by_head(norm), last(bfx[:, :], G), ALU.mult))
                v.do(nv.tensor_scalar(den, norm, EPS, None, ALU.add))
                v.do(nv.reciprocal(den, den))
                dve.wait_ge(c.product.sem, done + 1)
                v.do(nv.tensor_tensor(st, st, tokp[:, :], ALU.add))
                v.did(nv.tensor_tensor(st, st, den, ALU.mult))
                mark()
                dve.wait_ge(c.product.sem, done + 2)
                for n, x in enumerate((q, k, val)):
                    v.did(nv.tensor_copy(x, qkvp[:, n, :]))
                mark()
                dve.wait_ge(c.product.sem, done + 3)
                v.do(nv.tensor_scalar(att, attp[:, :], G ** -0.5, None, ALU.mult))
                v.do(nv.tensor_reduce(amx[:, 0, :], by_head(att), AX.X, ALU.max))
                v.did(nv.tensor_tensor(by_head(att), by_head(att), last(amx[:, 0, :], G), ALU.subtract))
                mark()
                dve.wait_ge(c.act_step.sem, c.act_step.base + 1)
                v.do(nv.tensor_reduce(amx[:, 1, :], by_head(att), AX.X, ALU.add))
                v.do(nv.reciprocal(amx[:, 1, :], amx[:, 1, :]))
                v.did(nv.tensor_tensor(by_head(att), by_head(att), last(amx[:, 1, :], G), ALU.mult))
                mark()
                dve.wait_ge(c.product.sem, done + 4)
                v.did(nv.tensor_copy(attT, atp[:, :]))
                mark()
                dve.wait_ge(c.product.sem, done + 5)
                v.did(nv.tensor_copy(osT, attp[:, :]))
                mark()
                dve.wait_ge(c.product.sem, done + 6)
                v.did(nv.tensor_copy(zout[:, :, :], zp[:, :, :]))
                v.end()

            @block.scalar
            def _(act):
                a = Steps(act, c.act_step)
                act.wait_ge(c.dve_step.sem, c.marks[2])
                a.did(nc.scalar.activation(att, att, ACT.Exp))
                a.end()

            @block.tensor
            def _(pe):
                mm = lambda out, l, r, s=True, e=True: nc.tensor.matmul(out, l, r, start=s, stop=e)
                for h in range(SH):
                    for kk in range(2):
                        ins_ = mm(hs(tokp, h), wfx[:, kk, h * G:(h + 1) * G], pooled[:, kk, h * G:(h + 1) * G], kk == 0, kk == 1)
                ins_.then_inc(c.product.sem, 1)
                pe.wait_ge(c.dve_step.sem, c.marks[0])
                mm(qkvp[:, 0, :], wqkv[:, 0, :], st)
                mm(qkvp[:, 1, :], wqkv[:, 1, :], st)
                for h in range(SH):
                    ins_ = mm(qkvp[:, 2, h * G:(h + 1) * G], hs(st, h), wqkv[:, 2, :])
                ins_.then_inc(c.product.sem, 1)
                pe.wait_ge(c.dve_step.sem, c.marks[1])
                for h in range(SH):
                    ins_ = mm(hs(attp, h), hs(q, h), hs(k, h))
                ins_.then_inc(c.product.sem, 1)
                pe.wait_ge(c.dve_step.sem, c.marks[3])
                for h in range(SH):
                    ins_ = nc.tensor.transpose(hs(atp, h), hs(att, h), c.ident[0:G, 0:G])
                ins_.then_inc(c.product.sem, 1)
                pe.wait_ge(c.dve_step.sem, c.marks[4])
                for h in range(SH):
                    ins_ = mm(hs(attp, h), hs(val, h), hs(attT, h))
                ins_.then_inc(c.product.sem, 1)
                pe.wait_ge(c.dve_step.sem, c.marks[5])
                for h in range(SH):
                    ins_ = mm(zp[(h % 2) * G:(h % 2 + 1) * G, h // 2, :], hs(osT, h), wo[:, h, :])
                ins_.then_inc(c.product.sem, 1)
                c.product.base += 6


def expert_layer(nc, c, ins, slots, out):
    T20 = 20
    layer_stats(nc, c)
    with (
        nc.sbuf_tensor("rtab", [P, T, T20], F32) as rtab, nc.sbuf_tensor("racc", [P, T, T20], F32) as racc,
        nc.sbuf_tensor("gates", [P, T, EXPERTS], F32) as gates,
    ):
        with nc.sbuf_tensor("rw", [P, 2, 24], F32) as w:
            load(nc, c, [(w[:, :, 0:16], ins["rw"].rearrange("p (k f) -> p k f", k=2))])
            fold(nc, c, w, 16, HEADS, "ras", "rad")
            gat_rows(nc, c, w, 16, HEADS, rtab)
        attend(nc, c, rtab, c.rdram, 16, HEADS, slots, ROUTER_CHUNKS, racc)
        route(nc, c, racc, gates)
        experts(nc, c, ins, gates, out)


def route(nc, c, racc, gates):
    E = EXPERTS
    with (
        nc.sbuf_tensor("r16", [P, T, 16], F32) as s16, nc.sbuf_tensor("q16", [P, T, 16], F32) as q16,
        nc.sbuf_tensor("m1", [P, 4, T], F32) as m1, nc.sbuf_tensor("sc", [P, T, E], F32) as sc,
        nc.sbuf_tensor("earlier", [P, E, E], F32) as earlier, nc.Block() as block,
    ):
        @block.vector
        def _(dve):
            v = Steps(dve, c.dve_step)
            nv = nc.vector
            z = racc[:, :, 16:16 + HEADS]
            v.do(nv.tensor_scalar(z, z, 1e-16, None, ALU.add))
            v.do(nv.reciprocal(z, z))
            for h in range(HEADS):
                v.did(nv.tensor_tensor(s16[:, :, h * E:(h + 1) * E], racc[:, :, h * E:(h + 1) * E],
                                       racc[:, :, 16 + h].unsqueeze(2).broadcast_to([P, T, E]), ALU.mult))
            v.wait()
            v.do(nv.tensor_tensor(s16[:, :, :], s16[:, :, :], mid(row(c.rows, "rb"), T), ALU.add))
            v.do(nv.tensor_reduce(m1[:, 0, :], s16[:, :, :], AX.X, ALU.add))
            v.do(nv.tensor_scalar(m1[:, 0, :], m1[:, 0, :], 1.0 / 16, None, ALU.mult))
            v.do(nv.tensor_tensor(s16[:, :, :], s16[:, :, :], last(m1[:, 0, :], 16), ALU.subtract))
            v.do(nv.tensor_tensor(q16[:, :, :], s16[:, :, :], s16[:, :, :], ALU.mult))
            v.do(nv.tensor_reduce(m1[:, 1, :], q16[:, :, :], AX.X, ALU.add))
            v.did(nv.tensor_scalar(m1[:, 1, :], m1[:, 1, :], 1.0 / 16, None, ALU.mult))
            c.var = v.at + v.n
            dve.wait_ge(c.act_step.sem, c.act_step.base + 1)
            v.do(nv.reciprocal(m1[:, 1, :], m1[:, 1, :]))
            v.do(nv.tensor_tensor(s16[:, :, :], s16[:, :, :], last(m1[:, 1, :], 16), ALU.mult))
            v.do(nv.tensor_tensor(s16[:, :, :], s16[:, :, :], mid(row(c.rows, "lng"), T), ALU.mult))
            v.do(nv.tensor_tensor(s16[:, :, :], s16[:, :, :], mid(row(c.rows, "lnb"), T), ALU.add))
            v.do(nv.tensor_reduce(sc[:, :, :], s16[:, :, :].rearrange("p t (h e) -> p t e h", h=HEADS), AX.X, ALU.add))
            v.do(nv.tensor_scalar(sc[:, :, :], sc[:, :, :], 1.0 / HEADS, None, ALU.mult))
            v.did(nv.tensor_tensor(earlier[:, :, :], mid(c.iota[:, 0:E], E), last(c.iota[:, 0:E], E), ALU.is_lt))
            a4 = s16[:, :, :].rearrange("p t (i j) -> p t i j", i=E)
            b4 = q16[:, :, :].rearrange("p t (i j) -> p t i j", i=E)
            sj = sc[:, :, :].unsqueeze(2).broadcast_to([P, T, E, E])
            si = sc[:, :, :].unsqueeze(3).broadcast_to([P, T, E, E])
            v.do(nv.tensor_tensor(a4, sj, si, ALU.is_gt))
            v.do(nv.tensor_tensor(b4, sj, si, ALU.is_equal))
            v.do(nv.tensor_tensor(q16[:, :, :], q16[:, :, :], mid(earlier[:, :, :].rearrange("p i j -> p (i j)"), T), ALU.mult))
            v.do(nv.tensor_tensor(s16[:, :, :], s16[:, :, :], q16[:, :, :], ALU.add))
            v.do(nv.tensor_reduce(gates[:, :, :], a4, AX.X, ALU.add))
            v.do(nv.tensor_scalar(gates[:, :, :], gates[:, :, :], 1.5, None, ALU.is_lt))
            v.do(nv.tensor_reduce(m1[:, 2, :], sc[:, :, :], AX.X, ALU.max))
            v.did(nv.tensor_tensor(sc[:, :, :], sc[:, :, :], last(m1[:, 2, :], E), ALU.subtract))
            c.best = v.at + v.n
            dve.wait_ge(c.act_step.sem, c.act_step.base + 2)
            v.do(nv.tensor_tensor(gates[:, :, :], gates[:, :, :], sc[:, :, :], ALU.mult))
            v.do(nv.tensor_reduce(m1[:, 3, :], gates[:, :, :], AX.X, ALU.add))
            v.do(nv.reciprocal(m1[:, 3, :], m1[:, 3, :]))
            v.did(nv.tensor_tensor(gates[:, :, :], gates[:, :, :], last(m1[:, 3, :], E), ALU.mult))
            v.end()

        @block.scalar
        def _(act):
            a = Steps(act, c.act_step)
            act.wait_ge(c.dve_step.sem, c.var)
            a.did(nc.scalar.activation(m1[:, 1, :], m1[:, 1, :], ACT.Sqrt, bias=c.eps[:, 0:1]))
            act.wait_ge(c.dve_step.sem, c.best)
            a.did(nc.scalar.activation(sc[:, :, :], sc[:, :, :], ACT.Exp))
            a.end()


def experts(nc, c, ins, gates, out):
    E, KH, HB = EXPERTS, 2, HIDDEN // P
    turns = T // 2
    with (
        nc.sbuf_tensor("w1", [P, KH, E, HIDDEN], F32) as w1, nc.sbuf_tensor("w2", [P, E, HB, D], F32) as w2,
        nc.sbuf_tensor("b1", [P, E, HB], F32) as b1, nc.sbuf_tensor("xa", [P, 2, D], F32) as a,
        nc.sbuf_tensor("xT", [P, KH, 2 * P], F32) as xt, nc.sbuf_tensor("hid", [P, 2, HB, 2 * P], F32) as hid,
        nc.sbuf_tensor("eo", [P, 2, D], F32) as o,
    ):
        load(nc, c, [(w1[:, :, :, :].rearrange("p k e f -> p (k e f)"), ins["w1"]),
                     (w2[:, :, :, :].rearrange("p k e f -> p (k e f)"), ins["w2"]), (b1[:, :, :].rearrange("p e f -> p (e f)"), ins["b1"])])
        rows_at, flip_at, flat_at, hid_at, gelu_at, prod_at, taken_at = (
            s.base for s in (c.rows_in, c.flipped, c.feature_major, c.ready, c.expo, c.product, c.taken))
        stored_at = c.stored.base
        with (
            nc.psum_tensor("eflip", [P, KH, 2 * P], F32) as flip, nc.psum_tensor("hidp", [P, 2, HB, 2 * P], F32) as hidp,
            nc.psum_tensor("eprod", [P, 2, 512], F32) as prod, nc.Block() as block,
        ):
            @block.vector
            def _(dve):
                v = Steps(dve, c.dve_step)
                nv = nc.vector
                with dve.Fori(0, turns) as i:
                    v.enter(i, 2 * E, turns)
                    for u in range(2):
                        dve.wait_ge(c.flipped.sem, flip_at + i)
                        normalized(nc, c, a[:, u, :], i * 2 + u).then_inc(c.rows_in.sem, 1)
                    for e in range(E):
                        for u in range(2):
                            n = e * 2 + u
                            dve.wait_ge(c.product.sem, prod_at + i * 2 * E + (n + 1))
                            dve.wait_ge(c.taken.sem, taken_at + i * 2 * E + n)
                            v.do(nv.tensor_tensor(o[:, u, :], prod[:, u, 0:D], row(c.rows, "eb2")[:, e * D:(e + 1) * D], ALU.add))
                            x = flat(c.x[:, bass.ds(i * 2 + u, 1), :])
                            nv.scalar_tensor_tensor(x, o[:, u, :], gates[:, bass.ds(i * 2 + u, 1), e], x, ALU.mult,
                                                    ALU.add).then_inc(c.taken.sem, 1)
                    v.leave()
                v.end()

            @block.scalar
            def _(act):
                with act.Fori(0, turns) as i:
                    act.wait_ge(c.flipped.sem, flip_at + i + 1)
                    act.wait_ge(c.ready.sem, hid_at + i * E)
                    nc.scalar.copy(xt[:, :, :], flip[:, :, :]).then_inc(c.feature_major.sem, 1)
                    for e in range(E):
                        act.wait_ge(c.ready.sem, hid_at + i * E + (e + 1))
                        act.wait_ge(c.product.sem, prod_at + i * 2 * E + (2 * e + 2 - 4))
                        for hb in range(HB):
                            ins_ = nc.scalar.activation(hid[:, e % 2, hb, :], hidp[:, e % 2, hb, :], ACT.Gelu, bias=b1[:, e, hb:hb + 1])
                        ins_.then_inc(c.expo.sem, 1)

            @block.tensor
            def _(pe):
                with pe.Fori(0, turns) as i:
                    pe.wait_ge(c.rows_in.sem, rows_at + i * 2 + 2)
                    pe.wait_ge(c.feature_major.sem, flat_at + i)
                    for u in range(2):
                        for k in range(KH):
                            ins_ = nc.tensor.transpose(flip[:, k, u * P:(u + 1) * P], a[:, u, k * P:(k + 1) * P], c.ident[:, :])
                    ins_.then_inc(c.flipped.sem, 1)
                    pe.wait_ge(c.feature_major.sem, flat_at + i + 1)

                    def up(e):
                        pe.wait_ge(c.expo.sem, gelu_at + i * E + (e - 1))
                        for hb in range(HB):
                            for k in range(KH):
                                ins_ = nc.tensor.matmul(hidp[:, e % 2, hb, :], w1[:, k, e, hb * P:(hb + 1) * P], xt[:, k, :],
                                                        start=(k == 0), stop=(k == KH - 1))
                        ins_.then_inc(c.ready.sem, 1)

                    def down(e):
                        pe.wait_ge(c.expo.sem, gelu_at + i * E + (e + 1))
                        for u in range(2):
                            pe.wait_ge(c.taken.sem, taken_at + i * 2 * E + (2 * e + u - 1))
                            for hb in range(HB):
                                ins_ = nc.tensor.matmul(prod[:, u, 0:D], hid[:, e % 2, hb, u * P:(u + 1) * P], w2[:, e, hb, :],
                                                        start=(hb == 0), stop=(hb == HB - 1))
                            ins_.then_inc(c.product.sem, 1)

                    up(0)
                    for e in range(1, E):
                        up(e)
                        down(e - 1)
                    down(E - 1)

            @block.sync
            def _(sp):
                with sp.Fori(0, turns) as i:
                    sp.wait_ge(c.taken.sem, taken_at + i * 2 * E + 2 * E)
                    sp.dma_start(out.rearrange("p (t f) -> p t f", t=T)[:, bass.ds(i * 2, 2), :],
                                 c.x[:, bass.ds(i * 2, 2), :]).then_inc(c.stored.sem, 16)
                sp.wait_ge(c.stored.sem, stored_at + 16 * turns)


class Slots:

    def __init__(self, nc, name, chunks):
        self.src = nc.alloc_sbuf_tensor(f"{name}_src", [P, chunks + RING], I32)
        self.place = nc.alloc_sbuf_tensor(f"{name}_place", [P, chunks], F32)
        self.tile = nc.alloc_sbuf_tensor(f"{name}_tile", [1, chunks], I32)


class Core:

    def __init__(self, nc):
        self.n = 0
        sb = nc.alloc_sbuf_tensor
        self.x = sb("x", [P, T, D], F32)
        self.rows = sb("rows", [P, ROWS_LEN], F32)
        self.iota, self.itmp = sb("iota", [P, 512], F32), sb("itmp", [P, 512], I32)
        self.part, self.ptmp = sb("part", [P, 1], F32), sb("ptmp", [P, 1], I32)
        self.ident, self.lower = sb("ident", [P, P], F32), sb("lower", [P, P], F32)
        self.ones, self.zero = sb("ones", [P, P], F32), sb("zero", [P, P], F32)
        self.pick = sb("pick", [HEADS, HEADS, P], F32)
        self.valid, self.eps = sb("valid", [P, T], F32), sb("eps", [P, 1], F32)
        self.stat = sb("stat", [P, T, 2], F32)
        self.ed, self.top = sb("ed", [P, T, HEADS], F32), sb("top", [P, T, HEADS], F32)
        self.edm = sb("edm", [P, T * 2 * HEADS], F32)
        self.counts = []

        def count(name):
            self.counts.append(Count(nc, name))
            return self.counts[-1]

        self.dve_step = count("dve_step")
        self.act_step = count("act_step")
        self.pool_step = count("pool_step")
        self.totals = count("totals")
        self.prefixes = count("prefixes")
        self.onehots = count("onehots")
        self.placed = count("placed")
        self.rows_in = count("rows_in")
        self.flipped = count("flipped")
        self.feature_major = count("feature_major")
        self.product = count("product")
        self.taken = count("taken")
        self.indexed = count("indexed")
        self.summed = count("summed")
        self.added = count("added")
        self.ready = count("ready")
        self.looked = count("looked")
        self.expo = count("expo")
        self.weighted = count("weighted")
        self.loaded, self.stored, self.max_gathered = Count(nc, "loaded"), Count(nc, "stored"), Count(nc, "max_gathered")
        for s in (self.loaded, self.stored, self.max_gathered):
            s.base = 0
        self.gathered = [nc.alloc_semaphore(f"gathered{u}") for u in range(RING)]
        self.gather_base = 0

    def fresh(self):
        self.n += 1
        return self.n


def graph_kernel(nc, ins, out):
    c = Core(nc)
    slots, rslots = Slots(nc, "graph", GRAPH_CHUNKS), Slots(nc, "router", ROUTER_CHUNKS)
    with nc.Block() as block:
        @block.gpsimd
        def _(pool):
            for s in c.counts:
                pool.sem_inc(s.sem, RING)
    constants(nc, c, ins)
    place_edges(nc, c, ins["dst"], ins["src"], GRAPH_EDGES, GRAPH_CHUNKS, slots)
    place_edges(nc, c, ins["rdst"], ins["rsrc"], ROUTER_EDGES, ROUTER_CHUNKS, rslots)
    c.table = nc.alloc_sbuf_tensor("table", [P, T, ROW], F32)
    c.acc = nc.alloc_sbuf_tensor("acc", [P, T, ROW], F32)
    c.dram = nc.dram_tensor("table_dram", (T * P, ROW), F32).ap()
    c.rdram = nc.dram_tensor("router_dram", (T * P, 20), F32).ap()
    layer_stats(nc, c)
    weighted_rows(nc, c)
    sage(nc, c, ins, 1, slots)
    sage(nc, c, ins, 2, slots)
    slice_layer(nc, c, ins)
    gat_layer(nc, c, ins, slots)
    expert_layer(nc, c, ins, rslots, out)


def layout(i):
    import numpy as np
    a = {k: np.asarray(v) for k, v in i.items()}
    x = np.zeros((T * P, D), np.float32)
    x[:NODES] = a["x"]
    kmaj = lambda w: np.ascontiguousarray(w.reshape(2, P, -1).transpose(1, 0, 2)).reshape(P, -1)
    rows = {"raw": "L0_gnn_raw_weights", "sb1": "L0_gnn_b1", "sb2": "L0_gnn_b2", "b_slice": "L0_ffn_b_slice",
            "temp": "L0_ffn_temperature", "b_out": "L0_ffn_b_out", "as0": "L1_gnn_a_src0", "ad0": "L1_gnn_a_dst0",
            "gb0": "L1_gnn_b0", "gamma0": "L1_gnn_gamma0", "beta0": "L1_gnn_beta0", "as1": "L1_gnn_a_src1",
            "ad1": "L1_gnn_a_dst1", "gb1": "L1_gnn_b1", "ras": "L1_ffn_att_src", "rad": "L1_ffn_att_dst",
            "rb": "L1_ffn_b_gat", "lng": "L1_ffn_ln_gamma", "lnb": "L1_ffn_ln_beta", "eb2": "L1_ffn_b2"}
    ei = a["L1_ffn_edge_index"]
    o = {
        "x": x.reshape(T, P, D).transpose(1, 0, 2).reshape(P, T * D),
        "rows": np.concatenate([a[rows[n]].reshape(-1) for n, _ in ROWS])[None],
        "dst": a["dst"].reshape(GRAPH_EDGES), "src": a["src"].reshape(GRAPH_EDGES),
        "rdst": ei[1].reshape(ROUTER_EDGES), "rsrc": ei[0].reshape(ROUTER_EDGES),
        "wxT": a["L0_ffn_W_x"].T.reshape(SLICE_HEADS, SLICE, D).transpose(1, 0, 2).reshape(SLICE, -1),
        "wslice": a["L0_ffn_W_slice"], "bx": a["L0_ffn_b_x"].reshape(SLICE_HEADS, SLICE).T,
        "wfx": kmaj(a["L0_ffn_W_fx"]), "bfx": a["L0_ffn_b_fx"].reshape(SLICE_HEADS, SLICE).T,
        "wqkv": np.concatenate([a["L0_ffn_W_q"], a["L0_ffn_W_k"], a["L0_ffn_W_v"]], 1),
        "wo": a["L0_ffn_W_out"].reshape(SLICE_HEADS, SLICE, D).transpose(1, 0, 2).reshape(SLICE, -1),
        "gw0": kmaj(a["L1_gnn_W0"]), "gw1": kmaj(a["L1_gnn_W1"]), "rw": kmaj(a["L1_ffn_W_gat"]),
        "w1": a["L1_ffn_W1"].reshape(EXPERTS, 2, P, HIDDEN).transpose(2, 1, 0, 3).reshape(P, -1),
        "w2": a["L1_ffn_W2"].reshape(EXPERTS, HIDDEN // P, P, D).transpose(2, 0, 1, 3).reshape(P, -1),
        "b1": a["L1_ffn_b1"].reshape(EXPERTS, HIDDEN // P, P).transpose(2, 0, 1).reshape(P, -1),
    }
    for k in (1, 2):
        o[f"sage{k}"] = np.concatenate([kmaj(a[f"L0_gnn_W_self{k}"].T), kmaj(a[f"L0_gnn_W_neigh{k}"].T)], 1)
    return {k: np.ascontiguousarray(v) for k, v in o.items()}


def kernel(**inputs):
    import numpy as np
    import concourse.bacc as bacc
    from concourse.bass_utils import run_bass_kernel_spmd

    arrays = layout(inputs)
    nc = bacc.Bacc("TRN2", target_bir_lowering=False, num_devices=1)
    ins = {k: nc.dram_tensor(f"in_{k}", a.shape, mybir.dt.from_np(a.dtype), kind="ExternalInput").ap() for k, a in arrays.items()}
    out = nc.dram_tensor("out_x", (P, T * D), F32, kind="ExternalOutput").ap()
    graph_kernel(nc, ins, out)
    r = run_bass_kernel_spmd(nc, [{f"in_{k}": a for k, a in arrays.items()}], core_ids=[0])
    got = np.asarray(r.results[0]["out_x"])
    return np.ascontiguousarray(got.reshape(P, T, D).transpose(1, 0, 2).reshape(T * P, D)[:NODES])
```

```python
import concourse.bass as bass
from concourse import mybir

F32 = mybir.dt.float32
F16 = mybir.dt.float16
I32 = mybir.dt.int32
ALU = mybir.AluOpType
ACT = mybir.ActivationFunctionType
AX = mybir.AxisListType

P = 128
NODES = 3125
D = 256
BUCKETS = -(-NODES // P)
T = BUCKETS + BUCKETS % 2
GRAPH_EDGES = (125, 400)
ROUTER_EDGES = (128, 256)
RING = 16
QUAD = 4
QUADS = RING // QUAD
ROW = 260
HEADS = 4
EXPERTS = 4
HIDDEN = 512
SLICE_HEADS = 8
SLICE = 64
EPS = 1e-5
FAR = 1e30
NEAR = 60.0


def chunks_of(edges):
    need = -(-edges[0] * edges[1] // P) + BUCKETS
    return -(-need // RING) * RING


GRAPH_CHUNKS = chunks_of(GRAPH_EDGES)
ROUTER_CHUNKS = chunks_of(ROUTER_EDGES)

ROWS = [("raw", D), ("sb1", D), ("sb2", D), ("b_slice", SLICE), ("temp", SLICE_HEADS), ("b_out", D),
        ("as0", D), ("ad0", D), ("gb0", D), ("gamma0", D), ("beta0", D), ("as1", D), ("ad1", D), ("gb1", D),
        ("ras", 16), ("rad", 16), ("rb", 16), ("lng", 16), ("lnb", 16), ("eb2", EXPERTS * D)]
ROW_AT = {}
for _name, _n in ROWS:
    ROW_AT[_name] = (sum(n for m, n in ROWS[:len(ROW_AT)]), _n)
ROWS_LEN = sum(n for _, n in ROWS)


class Count:

    def __init__(self, nc, name):
        self.sem, self.base = nc.alloc_semaphore(name), RING


class Steps:

    def __init__(self, eng, count):
        self.eng, self.count, self.at, self.n, self.per, self.parity = eng, count, count.base, 0, None, 0

    def did(self, ins):
        ins.then_inc(self.count.sem, 1)
        self.n += 1
        return self.n

    def wait(self, back=0):
        self.eng.wait_ge(self.count.sem, self.at + (self.n - back))

    def do(self, ins):
        self.did(ins)
        self.wait()

    def enter(self, turn, per, turns):
        self.at, self.after, self.per, self.n = self.at + self.n + turn * per, self.at + self.n + turns * per, per, 0

    def leave(self):
        assert self.n == self.per, (self.n, self.per)
        self.at, self.n = self.after, 0

    def end(self):
        self.count.base = self.at + self.n


def row(r, name):
    at, n = ROW_AT[name]
    return r[:, at:at + n]


def mid(ap, n):
    return ap.unsqueeze(1).broadcast_to([ap.shape[0], n, ap.shape[1]])


def last(ap, n):
    return ap.unsqueeze(2).broadcast_to([ap.shape[0], ap.shape[1], n])


def constants(nc, c, ins):
    with nc.Block() as block:
        @block.sync
        def _(sp):
            sp.dma_start(c.x[:, :, :].rearrange("p t f -> p (t f)"), ins["x"]).then_inc(c.loaded.sem, 16)
            sp.dma_start(c.rows[:, :], ins["rows"].broadcast_to([P, ROWS_LEN])).then_inc(c.loaded.sem, 16)
            sp.wait_ge(c.loaded.sem, 32)
            c.loaded.base = 32

        @block.gpsimd
        def _(pool):
            g = Steps(pool, c.pool_step)
            g.did(nc.gpsimd.iota(c.itmp[:, :], pattern=[[1, 512]], base=0, channel_multiplier=0))
            g.do(nc.gpsimd.iota(c.ptmp[:, :], pattern=[[1, 1]], base=0, channel_multiplier=1))
            g.did(nc.gpsimd.tensor_copy(c.iota[:, :], c.itmp[:, :]))
            g.did(nc.gpsimd.tensor_copy(c.iota16[:, :], c.itmp[:, :]))
            g.did(nc.gpsimd.tensor_copy(c.part[:, :], c.ptmp[:, :]))
            g.did(nc.gpsimd.memset(c.ones[:, :], 1.0))
            g.end()
            made = c.pool_step.base

        @block.vector
        def _(dve):
            v = Steps(dve, c.dve_step)
            dve.wait_ge(c.pool_step.sem, c.pool_step.base)
            v.did(nc.vector.tensor_scalar(c.ident[:, :], c.iota[:, 0:P], c.part[:, 0:1], None, ALU.is_equal))
            v.did(nc.vector.tensor_scalar(c.lower[:, :], c.iota[:, 0:P], c.part[:, 0:1], None, ALU.is_gt))
            v.did(nc.vector.tensor_scalar(c.pick[:, :, :], last(c.iota[0:HEADS, 0:HEADS], P), c.part[0:HEADS, 0:1],
                                          None, ALU.is_equal))
            v.did(nc.vector.memset(c.zero[:, :], 0.0))
            v.did(nc.vector.memset(c.zero16[:, :], 0.0))
            v.did(nc.vector.memset(c.valid[:, :], 1.0))
            v.wait()
            v.did(nc.vector.memset(c.valid[:, BUCKETS:T], 0.0))
            v.did(nc.vector.tensor_scalar(c.valid[:, BUCKETS - 1:BUCKETS], c.part[:, 0:1],
                                          float(NODES - (BUCKETS - 1) * P), None, ALU.is_lt))
            v.did(nc.vector.memset(c.eps[:, :], EPS))
            v.end()

        @block.scalar
        def _(act):
            a = Steps(act, c.act_step)
            act.wait_ge(c.pool_step.sem, c.pool_step.base)
            a.did(nc.scalar.activation(c.ptmp[:, :], c.part[:, :], ACT.Identity))
            a.end()


def place_edges(nc, c, dst, src, edges, chunks, out):
    E, J = edges
    with (
        nc.sbuf_tensor(f"dst_{chunks}", [E, J], I32) as di, nc.sbuf_tensor(f"src_{chunks}", [E, J], I32) as si,
        nc.sbuf_tensor(f"hi_{chunks}", [E, J], F32) as hi, nc.sbuf_tensor(f"field_{chunks}", [E, 2, J], F32) as field,
        nc.sbuf_tensor(f"slot_{chunks}", [E, J], F32) as slot, nc.sbuf_tensor(f"ti_{chunks}", [E, J], I32) as ti,
        nc.sbuf_tensor(f"tj_{chunks}", [E, J], I32) as tj,
        nc.sbuf_tensor(f"spot_{chunks}", [E, 2, J], F32) as spot,
        nc.sbuf_tensor(f"oh_{chunks}", [E, BUCKETS * J], F32) as oh, nc.sbuf_tensor(f"pre_{chunks}", [E, BUCKETS * J], F32) as pre,
        nc.sbuf_tensor(f"tot_{chunks}", [P, 8, 32], F32) as tot, nc.sbuf_tensor(f"toti_{chunks}", [P, 32], I32) as toti,
        nc.sbuf_tensor(f"begun_{chunks}", [BUCKETS, chunks], F32) as atk, nc.psum_tensor(f"ahead_{chunks}", [1, 512], F32) as ahead,
        nc.sbuf_tensor(f"at_{chunks}", [E, 4, P], F16) as at,
        nc.sbuf_tensor(f"a1_{chunks}", [E, 4, 2, P], F16) as a1, nc.sbuf_tensor(f"a2_{chunks}", [E, 4, chunks], F16) as a2,
        nc.sbuf_tensor(f"gi_{chunks}", [P, chunks], I32) as gi,
        nc.psum_tensor(f"base_{chunks}", [P, 64], F32) as basep, nc.psum_tensor(f"grid_{chunks}", [P, 2, 512], F32) as grid,
        nc.Block() as block,
    ):
        counts_at, ready_at, used_at, prefix_at = c.totals.base + 1, c.onehots.base, c.placed.base, c.prefixes.base + 1
        loaded_at, source_at, times_at = c.loaded.base + 32, c.ready.base, c.weighted.base

        @block.sync
        def _(sp):
            sp.dma_start(di[:, :], dst).then_inc(c.loaded.sem, 16)
            sp.dma_start(si[:, :], src).then_inc(c.loaded.sem, 16)
            sp.wait_ge(c.loaded.sem, loaded_at)

        @block.vector
        def _(dve):
            v = Steps(dve, c.dve_step)
            nv = nc.vector
            dve.wait_ge(c.loaded.sem, loaded_at)
            v.did(nv.tensor_scalar(ti[:, :], di[:, :], 7, None, ALU.arith_shift_right))
            v.do(nv.tensor_scalar(tj[:, :], di[:, :], P - 1, None, ALU.bitwise_and))
            v.did(nv.tensor_copy(hi[:, :], ti[:, :]))
            v.do(nv.tensor_scalar(field[:, 0, :], tj[:, :], 1.0, None, ALU.add))
            v.did(nv.tensor_scalar(tj[:, :], si[:, :], 7, None, ALU.bitwise_and))
            v.do(nv.tensor_scalar(ti[:, :], si[:, :], 3, None, ALU.arith_shift_right))
            v.did(nv.tensor_copy(field[:, 1, :], ti[:, :]))
            v.do(nv.scalar_tensor_tensor(field[:, 0, :], tj[:, :], 256.0, field[:, 0, :], ALU.mult, ALU.add))
            oh3, pre3 = (x[:, :].rearrange("p (b j) -> p b j", b=BUCKETS) for x in (oh, pre))
            v.do(nv.tensor_tensor(oh3, mid(hi[:, :], BUCKETS), last(c.iota[0:E, 0:BUCKETS], J), ALU.is_equal))
            v.do(nv.tensor_tensor_scan(pre[:, :], oh[:, :], c.zero[0:E, 0:1].broadcast_to([E, BUCKETS * J]), 0.0, ALU.add, ALU.add))
            v.did(nv.memset(tot[:, :, :], 0.0))
            v.wait()
            v.do(nv.tensor_copy(tot[0:E, 0, 1:BUCKETS + 1], pre3[:, :, J - 1]))
            nv.tensor_tensor(tot[0:E, 1, 0:BUCKETS], tot[0:E, 0, 1:BUCKETS + 1], tot[0:E, 0, 0:BUCKETS],
                             ALU.subtract).then_inc(c.totals.sem, 1)
            dve.wait_ge(c.prefixes.sem, prefix_at)
            v.do(nv.tensor_scalar(tot[:, 2, 0:BUCKETS], basep[:, 32:32 + BUCKETS], float(P - 1), None, ALU.add))
            v.do(nv.tensor_copy(toti[:, 0:BUCKETS], tot[:, 2, 0:BUCKETS]))
            v.do(nv.tensor_scalar(toti[:, 0:BUCKETS], toti[:, 0:BUCKETS], 7, None, ALU.arith_shift_right))
            v.do(nv.tensor_copy(tot[:, 3, 0:BUCKETS], toti[:, 0:BUCKETS]))
            v.do(nv.tensor_tensor_scan(tot[:, 4, 0:BUCKETS], tot[:, 3, 0:BUCKETS], tot[:, 7, 0:BUCKETS], 0.0, ALU.add, ALU.add))
            v.do(nv.tensor_tensor(tot[:, 5, 0:BUCKETS], tot[:, 4, 0:BUCKETS], tot[:, 3, 0:BUCKETS], ALU.subtract))
            v.do(nv.scalar_tensor_tensor(tot[:, 6, 0:BUCKETS], tot[:, 5, 0:BUCKETS], float(P), basep[:, 0:BUCKETS],
                                         ALU.mult, ALU.add))
            v.do(nv.tensor_tensor(tot[0:E, 6, 0:BUCKETS], tot[0:E, 6, 0:BUCKETS], tot[0:E, 0, 0:BUCKETS], ALU.subtract))
            v.do(nv.tensor_scalar(tot[0:E, 6, 0:BUCKETS], tot[0:E, 6, 0:BUCKETS], -1.0, None, ALU.add))
            v.do(nv.tensor_tensor(pre3, pre3, last(tot[0:E, 6, 0:BUCKETS], J), ALU.add))
            v.do(nv.tensor_tensor(oh3, pre3, oh3, ALU.mult))
            v.do(nv.tensor_reduce(slot[:, :], oh[:, :].rearrange("p (b j) -> p j b", b=BUCKETS), AX.X, ALU.add))
            v.do(nv.tensor_copy(ti[:, :], slot[:, :]))
            v.do(nv.tensor_scalar(tj[:, :], ti[:, :], P - 1, None, ALU.bitwise_and))
            v.did(nv.tensor_copy(spot[:, 0, :], tj[:, :]))
            v.do(nv.tensor_scalar(ti[:, :], ti[:, :], 7, None, ALU.arith_shift_right))
            v.do(nv.tensor_copy(spot[:, 1, :], ti[:, :]))
            v.do(nv.tensor_tensor(tot[0:BUCKETS, 0, 0:BUCKETS], tot[0:BUCKETS, 5, 0:BUCKETS], c.ident[0:BUCKETS, 0:BUCKETS], ALU.mult))
            v.do(nv.tensor_reduce(tot[0:BUCKETS, 1, 0:1], tot[0:BUCKETS, 0, 0:BUCKETS], AX.X, ALU.add))
            nv.tensor_scalar(atk[:, :], c.iota[0:BUCKETS, 0:chunks], tot[0:BUCKETS, 1, 0:1], None, ALU.is_ge).then_inc(c.totals.sem, 1)
            v.did(nv.memset(out.tile[:, 0:QUAD], 0))
            v.did(nv.memset(out.tile[:, QUAD + chunks:], 0))
            dve.wait_ge(c.prefixes.sem, prefix_at + 1)
            v.did(nv.tensor_scalar(out.tile[:, QUAD:QUAD + chunks], ahead[:, 0:chunks], -1.0, None, ALU.add))
            with dve.Fori(0, J // 4) as i:
                for u in range(4):
                    j = i * 4 + u
                    dve.wait_ge(c.placed.sem, used_at + i * 4 + (u - 2))
                    nv.tensor_scalar(at[:, u, :], c.iota16[0:E, 0:P], spot[:, 0, bass.ds(j, 1)], None,
                                     ALU.is_equal).then_inc(c.ready.sem, 1)
                    nv.tensor_scalar(a2[:, u, :], c.iota16[0:E, 0:chunks], spot[:, 1, bass.ds(j, 1)], None,
                                     ALU.is_equal).then_inc(c.onehots.sem, 1)
            dve.wait_ge(c.placed.sem, used_at + J + 2)
            v.do(nv.tensor_copy(gi[:, :], grid[:, 0, 0:chunks]))
            v.did(nv.memset(out.src[:, chunks:chunks + RING], 0))
            v.do(nv.tensor_scalar(out.src[:, 0:chunks], gi[:, :], 8, None, ALU.arith_shift_right))
            v.do(nv.scalar_tensor_tensor(out.src[:, 0:chunks], grid[:, 1, 0:chunks], 8.0, out.src[:, 0:chunks], ALU.mult, ALU.add))
            v.do(nv.tensor_scalar(gi[:, :], gi[:, :], 255, None, ALU.bitwise_and))
            v.did(nv.memset(out.place[:, chunks:chunks + RING], -1.0))
            v.do(nv.tensor_scalar(out.place[:, 0:chunks], gi[:, :], -1.0, None, ALU.add))
            v.end()

        @block.scalar
        def _(act):
            with act.Fori(0, J // 4) as i:
                for u in range(4):
                    act.wait_ge(c.ready.sem, source_at + i * 4 + (u + 1))
                    for half in range(2):
                        ins_ = nc.scalar.activation(a1[:, u, half, :], at[:, u, :], ACT.Identity,
                                                    scale=field[:, half, bass.ds(i * 4 + u, 1)])
                    ins_.then_inc(c.weighted.sem, 1)

        @block.tensor
        def _(pe):
            pe.wait_ge(c.totals.sem, counts_at)
            nc.tensor.matmul(basep[:, 0:BUCKETS], c.lower[0:E, :], tot[0:E, 1, 0:BUCKETS], start=True, stop=True)
            nc.tensor.matmul(basep[:, 32:32 + BUCKETS], c.ones[0:E, :], tot[0:E, 1, 0:BUCKETS], start=True,
                             stop=True).then_inc(c.prefixes.sem, 1)
            pe.wait_ge(c.totals.sem, counts_at + 1)
            nc.tensor.matmul(ahead[:, 0:chunks], c.ones[0:BUCKETS, 0:1], atk[:, :], start=True, stop=True).then_inc(c.prefixes.sem, 1)
            for half in range(2):
                ins_ = nc.tensor.matmul(grid[:, half, 0:chunks], c.zero16[0:E, :], c.zero16[0:E, 0:1].broadcast_to([E, chunks]),
                                        start=True, stop=False)
            ins_.then_inc(c.placed.sem, 1)
            with pe.Fori(0, J // 4) as i:
                for u in range(4):
                    pe.wait_ge(c.onehots.sem, ready_at + i * 4 + (u + 1))
                    pe.wait_ge(c.weighted.sem, times_at + i * 4 + (u + 1))
                    nc.tensor.matmul(grid[:, 0, 0:chunks], a1[:, u, 0, :], a2[:, u, :], start=False, stop=False)
                    nc.tensor.matmul(grid[:, 1, 0:chunks], a1[:, u, 1, :], a2[:, u, :], start=False,
                                     stop=False).then_inc(c.placed.sem, 1)
            for half in range(2):
                ins_ = nc.tensor.matmul(grid[:, half, 0:chunks], c.zero16[0:E, :], c.zero16[0:E, 0:1].broadcast_to([E, chunks]),
                                        start=False, stop=True)
            ins_.then_inc(c.placed.sem, 1)

        c.loaded.base, c.totals.base, c.prefixes.base = loaded_at, counts_at + 1, prefix_at + 1
        c.ready.base, c.weighted.base = source_at + J, times_at + J
        c.onehots.base, c.placed.base = ready_at + J, used_at + J + 2


def layer_stats(nc, c):
    with nc.sbuf_tensor(f"bn{c.fresh()}", [P, T, 6], F32) as bn, nc.Block() as block:
        mean, rstd = c.stat[:, :, 0], c.stat[:, :, 1]

        @block.vector
        def _(dve):
            v = Steps(dve, c.dve_step)
            nv = nc.vector
            with dve.Fori(0, T // 2) as i:
                v.enter(i, 2, T // 2)
                for u in range(2):
                    v.did(nv.bn_stats(flat(bn[:, bass.ds(i * 2 + u, 1), :]), flat(c.x[:, bass.ds(i * 2 + u, 1), :])))
                v.leave()
            v.wait()
            v.did(nv.tensor_tensor(mean, bn[:, :, 1], bn[:, :, 4], ALU.add))
            v.do(nv.tensor_tensor(rstd, bn[:, :, 1], bn[:, :, 4], ALU.subtract))
            v.do(nv.tensor_tensor(rstd, rstd, rstd, ALU.mult))
            v.did(nv.tensor_scalar(mean, mean, 0.5, None, ALU.mult))
            v.do(nv.tensor_scalar(rstd, rstd, 0.25, None, ALU.mult))
            v.do(nv.scalar_tensor_tensor(rstd, bn[:, :, 2], 1.0 / D, rstd, ALU.mult, ALU.add))
            v.did(nv.scalar_tensor_tensor(rstd, bn[:, :, 5], 1.0 / D, rstd, ALU.mult, ALU.add))
            dve.wait_ge(c.act_step.sem, c.act_step.base + 1)
            v.did(nv.reciprocal(rstd, rstd))
            v.end()

        @block.scalar
        def _(act):
            a = Steps(act, c.act_step)
            act.wait_ge(c.dve_step.sem, c.dve_step.base - 1)
            a.did(nc.scalar.activation(rstd, rstd, ACT.Sqrt, bias=c.eps[:, 0:1]))
            a.end()


def weighted_rows(nc, c):
    with nc.sbuf_tensor("w_soft", [P, D], F32) as w, nc.sbuf_tensor("w_m", [P, 4], F32) as m, nc.Block() as block:
        @block.vector
        def _(dve):
            v = Steps(dve, c.dve_step)
            nv = nc.vector
            v.do(nv.tensor_reduce(m[:, 0:1], row(c.rows, "raw"), AX.X, ALU.max))
            v.did(nv.tensor_scalar(m[:, 1:2], m[:, 0:1], -1.0, None, ALU.mult))
            negated = v.at + v.n
            v.did(nv.memset(c.table[:, :, :], 0.0))
            v.wait()
            v.did(nv.memset(c.table[:, :, D:D + 1], 1.0))
            dve.wait_ge(c.act_step.sem, c.act_step.base + 1)
            v.do(nv.reciprocal(m[:, 3:4], m[:, 2:3]))
            v.do(nv.tensor_scalar(w[:, :], w[:, :], m[:, 3:4], None, ALU.mult))
            with dve.Fori(0, T) as t:
                v.enter(t, 2, T)
                v.do(normalized(nc, c, c.table[:, bass.ds(t, 1), 0:D].rearrange("p t f -> p (t f)"), t))
                tab = c.table[:, bass.ds(t, 1), 0:D].rearrange("p t f -> p (t f)")
                v.did(nv.tensor_tensor(tab, tab, w[:, :], ALU.mult))
                v.leave()
            v.end()
            c.negated = negated

        @block.scalar
        def _(act):
            a = Steps(act, c.act_step)
            act.wait_ge(c.dve_step.sem, c.negated)
            a.did(nc.scalar.activation(w[:, :], row(c.rows, "raw"), ACT.Exp, bias=m[:, 1:2], accum_out=m[:, 2:3]))
            a.end()


def normalized(nc, c, out, t):
    return nc.vector.tensor_scalar(out, c.x[:, bass.ds(t, 1), :].rearrange("p t f -> p (t f)"),
                                   c.stat[:, bass.ds(t, 1), 0], c.stat[:, bass.ds(t, 1), 1], ALU.subtract, ALU.mult)


def store_table(nc, c, table, dram):
    with nc.Block() as block:
        @block.sync
        def _(sp):
            sp.dma_start(dram.rearrange("(t p) f -> p t f", p=P), table[:, :, :]).then_inc(c.stored.sem, 16)
            c.stored.base += 16
            sp.wait_ge(c.stored.sem, c.stored.base)


def dense(nc, c, halves, width, weights, prep, post, per_prep, per_post, extra=None):
    n = c.fresh()
    turns = T // 2
    rows_at, flip_at, flat_at, prod_at, taken_at = (s.base for s in (c.rows_in, c.flipped, c.feature_major, c.product, c.taken))
    with (
        nc.sbuf_tensor(f"rows{n}", [P, 2, halves * P], F32) as a, nc.sbuf_tensor(f"rowsT{n}", [P, 2, halves, P], F32) as at,
        nc.psum_tensor(f"flip{n}", [P, 2, 512], F32) as flip, nc.psum_tensor(f"prod{n}", [P, 2, 512], F32) as prod,
        nc.Block() as block,
    ):
        @block.vector
        def _(dve):
            v = Steps(dve, c.dve_step)

            def prepare(i):
                for u in range(2):
                    dve.wait_ge(c.flipped.sem, flip_at + i * 2 + (u - 1))
                    prep(v, i * 2 + u, a[:, u, :]).then_inc(c.rows_in.sem, 1)

            def finish(i):
                for u in range(2):
                    dve.wait_ge(c.product.sem, prod_at + i * 2 + u + 1)
                    post(v, i * 2 + u, prod[:, u, 0:width]).then_inc(c.taken.sem, 1)

            prepare(0)
            prepare(1)
            with dve.Fori(0, turns - 2) as i:
                v.enter(i, 2 * (per_prep + per_post), turns - 2)
                prepare(i + 2)
                finish(i)
                v.leave()
            finish(turns - 2)
            finish(turns - 1)
            v.end()

        @block.tensor
        def _(pe):
            def turn(i):
                for u in range(2):
                    pe.wait_ge(c.rows_in.sem, rows_at + i * 2 + u + 1)
                    pe.wait_ge(c.feature_major.sem, flat_at + i * 2 + (u - 1))
                    for h in range(halves):
                        ins = nc.tensor.transpose(flip[:, u, h * P:(h + 1) * P], a[:, u, h * P:(h + 1) * P], c.ident[:, :])
                    ins.then_inc(c.flipped.sem, 1)

            def multiply(i):
                for u in range(2):
                    pe.wait_ge(c.feature_major.sem, flat_at + i * 2 + u + 1)
                    pe.wait_ge(c.taken.sem, taken_at + i * 2 + (u - 1))
                    for h in range(halves):
                        ins = nc.tensor.matmul(prod[:, u, 0:width], at[:, u, h, :], weights(h), start=(h == 0), stop=(h == halves - 1))
                    ins.then_inc(c.product.sem, 1)

            turn(0)
            with pe.Fori(0, turns - 1) as i:
                turn(i + 1)
                multiply(i)
            multiply(turns - 1)

        @block.scalar
        def _(act):
            with act.Fori(0, turns) as i:
                for u in range(2):
                    act.wait_ge(c.flipped.sem, flip_at + i * 2 + u + 1)
                    act.wait_ge(c.product.sem, prod_at + i * 2 + (u - 1))
                    nc.scalar.copy(at[:, u, :, :].rearrange("p h n -> p (h n)"), flip[:, u, 0:halves * P]).then_inc(c.feature_major.sem, 1)

        for s in (c.rows_in, c.flipped, c.feature_major, c.product, c.taken):
            s.base += T


def tiles_of(nc, engine, slots, first, n):
    _, tiles = nc.values_load_multi_w_load_instructions(
        slots.tile[0:1, bass.ds(first + QUAD, n)], engines=(engine,), min_val=0, max_val=BUCKETS - 1,
        skip_runtime_bounds_check_because="the placing makes them so")
    return tiles


def gather_sum(nc, c, table, width, heads, slots, chunks, acc):
    n = c.fresh()
    W = width + HEADS
    C = width // heads if heads else 0
    turns, quads = chunks // RING, QUADS
    opening = QUAD if heads else 0
    index_at, gathered_at, onehot_at = c.indexed.base, c.gather_base, c.onehots.base
    summed_at, added_at, ready_at, weighted_at = c.summed.base + opening, c.added.base + opening, c.ready.base, c.weighted.base
    flip_at, flat_at, looked_at, expo_at = (s.base for s in (c.flipped, c.feature_major, c.looked, c.expo))
    with (
        nc.sbuf_tensor(f"g{n}", [P, RING, W], F32) as g, nc.sbuf_tensor(f"oh{n}", [P, RING, P], F32) as oh,
        nc.sbuf_tensor(f"idx{n}", [P, RING], I32) as idx, nc.sbuf_tensor(f"ohT{n}", [P, 2, QUAD, P], F32) as oht,
        nc.sbuf_tensor(f"e{n}", [P, QUADS, QUAD, HEADS], F32) as e, nc.sbuf_tensor(f"e2{n}", [P, QUADS, QUAD, HEADS], F32) as e2,
        nc.psum_tensor(f"sum{n}", [P, 4, 512], F32) as total, nc.psum_tensor(f"flip{n}", [P, 2, QUAD, P], F32) as flip,
        nc.psum_tensor(f"look{n}", [P, 2, 64, 2 * HEADS], F32) as look,
        nc.Block() as block,
    ):
        @block.gpsimd
        def _(pool):
            freed = pool.alloc_register(f"freed{n}")
            pool.reg_mov(freed, summed_at + 1 - RING)
            with pool.Fori(0, turns) as i:
                for u in range(RING):
                    pool.wait_ge(c.indexed.sem, index_at + i * RING + (u + 1))
                    pool.wait_ge(c.summed.sem, freed)
                    pool.reg_add(freed, freed, 1)
                    nc.gpsimd.indirect_dma_start(
                        out=g[:, u, :], out_offset=None, in_=table,
                        in_offset=bass.IndirectOffsetOnAxis(ap=idx[:, u:u + 1], axis=0)).then_inc(c.gathered[u], 16)

        @block.scalar
        def _(act):
            def turned(i, q):
                act.wait_ge(c.flipped.sem, flip_at + i * quads + (q + 1))
                act.wait_ge(c.looked.sem, looked_at + i * quads + (q - 1))
                nc.scalar.copy(oht[:, q % 2, :, :], flip[:, q % 2, :, :]).then_inc(c.feature_major.sem, 1)

            for u in range(RING):
                nc.scalar.copy(idx[:, u:u + 1], slots.src[:, u:u + 1]).then_inc(c.indexed.sem, 1)
            if heads:
                turned(0, 0)
                turned(0, 1)
            with act.Fori(0, turns) as i:
                for q in range(quads):
                    if heads:
                        act.wait_ge(c.ready.sem, ready_at + i * quads + (q + 1))
                        p = g[:, QUAD * q:QUAD * q + QUAD, width:width + heads] if heads > 1 else e[:, q, :, 0:1]
                        nc.scalar.activation(p, e[:, q, :, 0:heads], ACT.Exp).then_inc(c.expo.sem, 1)
                        turned(i, q + 2)
                    for u in range(QUAD * q, QUAD * q + QUAD):
                        act.wait_ge(c.gathered[u], gathered_at + i * 16 + 16)
                        nc.scalar.copy(idx[:, u:u + 1], slots.src[:, bass.ds(i * RING + (u + RING), 1)]).then_inc(c.indexed.sem, 1)

        @block.vector
        def _(dve):
            nv = nc.vector
            v = Steps(dve, c.dve_step)

            def onehot(k, u):
                nv.tensor_scalar(oh[:, u, :], c.iota[:, 0:P], slots.place[:, bass.ds(k, 1)], None,
                                 ALU.is_equal).then_inc(c.onehots.sem, 1)

            def add(k, u, tile):
                dve.wait_ge(c.summed.sem, summed_at + k + 1)
                dve.wait_ge(c.added.sem, added_at + k)
                at = flat(acc[:, bass.ds(tile, 1), :])
                nv.tensor_tensor(at, at, total[:, u, 0:W], ALU.add).then_inc(c.added.sem, 1)

            for u in range(RING - opening):
                onehot(u, u)
            with dve.Fori(0, turns) as i:
                v.enter(i, 2 * QUADS if heads else 0, turns)
                tiles = tiles_of(nc, mybir.EngineType.DVE, slots, i * RING - opening, RING)
                for q in range(quads):
                    us = range(QUAD * q, QUAD * q + QUAD)
                    if heads:
                        for u in us:
                            dve.wait_ge(c.gathered[u], gathered_at + i * 16 + 16)
                        dve.wait_ge(c.looked.sem, looked_at + i * quads + (q + 1))
                        es = g[:, QUAD * q:QUAD * q + QUAD, width:width + heads]
                        v.do(nv.tensor_tensor(e2[:, q, :, 0:heads], es, look[:, q % 2, 0:QUAD, 0:heads], ALU.add))
                        v.do(nv.scalar_tensor_tensor(e2[:, q, :, 0:heads], e2[:, q, :, 0:heads], 0.2, e2[:, q, :, 0:heads], ALU.mult, ALU.max))
                        nv.tensor_tensor(e[:, q, :, 0:heads], e2[:, q, :, 0:heads], look[:, q % 2, 0:QUAD, HEADS:HEADS + heads],
                                         ALU.subtract).then_inc(c.ready.sem, 1)
                    for u in range(QUAD):
                        k = i * RING + (QUAD * q + u - opening)
                        add(k, u, tiles[QUAD * q + u])
                        onehot(k + RING, (QUAD * q + u - opening) % RING)
                    if heads:
                        dve.wait_ge(c.expo.sem, expo_at + i * quads + (q + 1))
                        for u in us:
                            if heads > 1:
                                gv = g[:, u, 0:width].rearrange("p (h c) -> p h c", h=heads)
                                nv.tensor_tensor(gv, gv, last(g[:, u, width:width + heads], C), ALU.mult).then_inc(c.weighted.sem, 1)
                            else:
                                nv.tensor_scalar(oh[:, u, :], oh[:, u, :], e[:, q, u % QUAD, 0:1], None, ALU.mult).then_inc(c.weighted.sem, 1)
                v.leave()
            if heads:
                tiles = tiles_of(nc, mybir.EngineType.DVE, slots, chunks - QUAD, QUAD)
                for u in range(QUAD):
                    add(chunks - QUAD + u, u, tiles[u])
            v.end()

        @block.tensor
        def _(pe):
            def turn(i, q):
                for u in range(QUAD * q, QUAD * q + QUAD):
                    pe.wait_ge(c.onehots.sem, onehot_at + i * RING + (u + 1))
                pe.wait_ge(c.feature_major.sem, flat_at + i * quads + (q - 1))
                for u in range(QUAD):
                    ins = nc.tensor.transpose(flip[:, q % 2, u, :], oh[:, (QUAD * q + u) % RING, :], c.ident[:, :])
                ins.then_inc(c.flipped.sem, 1)

            def look_up(i, q, tiles):
                pe.wait_ge(c.feature_major.sem, flat_at + i * quads + (q + 1))
                pe.wait_ge(c.ready.sem, ready_at + i * quads + (q - 1))
                for u in range(QUAD):
                    ins = nc.tensor.matmul(look[:, q % 2, u, :], oht[:, q % 2, u, :],
                                           c.edm[:, bass.ds(tiles[u] * (2 * HEADS), 2 * HEADS)], start=True, stop=True)
                ins.then_inc(c.looked.sem, 1)

            if heads:
                turn(0, 0)
                turn(0, 1)
                look_up(0, 0, tiles_of(nc, mybir.EngineType.PE, slots, 0, QUAD))
                for u in range(QUAD):
                    nc.tensor.matmul(total[:, u, 0:W], c.zero[:, :], c.zero[:, 0:1].broadcast_to([P, W]),
                                     start=True, stop=True).then_inc(c.summed.sem, 1)
            with pe.Fori(0, turns) as i:
                if heads:
                    tiles = tiles_of(nc, mybir.EngineType.PE, slots, i * RING + QUAD, RING)
                for q in range(quads):
                    if heads:
                        look_up(i, q + 1, tiles[QUAD * q:])
                        turn(i, q + 2)
                    for u in range(QUAD * q, QUAD * q + QUAD):
                        if heads:
                            pe.wait_ge(c.weighted.sem, weighted_at + i * RING + (u + 1))
                        else:
                            pe.wait_ge(c.onehots.sem, onehot_at + i * RING + (u + 1))
                            pe.wait_ge(c.gathered[u], gathered_at + i * 16 + 16)
                        pe.wait_ge(c.added.sem, added_at + i * RING + (u + 1 - 4))
                        nc.tensor.matmul(total[:, u % 4, 0:W], oh[:, u, :], g[:, u, :], start=True, stop=True).then_inc(c.summed.sem, 1)

    c.gather_base += 16 * turns
    c.indexed.base += chunks + RING
    c.onehots.base += chunks + RING - opening
    c.summed.base += chunks + opening
    c.added.base += chunks + opening
    if heads:
        for s in (c.flipped, c.feature_major):
            s.base += quads * turns + 2
        c.looked.base += quads * turns + 1
        c.weighted.base += chunks
        c.ready.base += quads * turns
        c.expo.base += quads * turns


def spread_guard(nc, c, table, width, heads, flag):
    with (
        nc.sbuf_tensor(f"ends{c.fresh()}", [P, 2 * HEADS], F32) as ends, nc.sbuf_tensor(f"end{c.fresh()}", [2 * HEADS, 1], F32) as end,
        nc.sbuf_tensor(f"diag{c.fresh()}", [2 * HEADS, 2 * HEADS], F32) as diag, nc.sbuf_tensor(f"far{c.fresh()}", [P, 2 * HEADS + 1], F32) as far,
        nc.psum_tensor(f"endsT{c.fresh()}", [2 * HEADS, P], F32) as endst, nc.psum_tensor(f"endall{c.fresh()}", [P, 2 * HEADS], F32) as endall,
        nc.Block() as block,
    ):
        @block.vector
        def _(dve):
            v = Steps(dve, c.dve_step)
            nv = nc.vector
            es = table[:, :, width:width + heads].rearrange("p t h -> p h t")
            v.do(nv.memset(ends[:, :], 0.0))
            v.did(nv.tensor_reduce(ends[:, 0:heads], es, AX.X, ALU.max))
            v.do(nv.tensor_reduce(ends[:, HEADS:HEADS + heads], es, AX.X, ALU.min))
            v.did(nv.tensor_scalar(ends[:, HEADS:HEADS + heads], ends[:, HEADS:HEADS + heads], -1.0, None, ALU.mult))
            c.ends_in = v.at + v.n
            dve.wait_ge(c.product.sem, c.product.base + 1)
            v.do(nv.tensor_reduce(end[:, :], endst[:, :], AX.X, ALU.max))
            v.did(nv.tensor_scalar(diag[:, :], c.ident[0:2 * HEADS, 0:2 * HEADS], end[:, 0:1], None, ALU.mult))
            c.diagonal = v.at + v.n
            dve.wait_ge(c.product.sem, c.product.base + 2)
            v.do(nv.tensor_copy(far[:, 0:2 * HEADS], endall[:, :]))
            v.did(nv.tensor_copy(c.top[:, :, :], mid(far[:, 0:HEADS], T)))
            v.do(nv.tensor_tensor(far[:, HEADS:2 * HEADS], far[:, 0:HEADS], far[:, HEADS:2 * HEADS], ALU.add))
            v.do(nv.tensor_reduce(far[:, 2 * HEADS:], far[:, HEADS:2 * HEADS], AX.X, ALU.max))
            v.did(nv.tensor_scalar(flag[:, :], far[0:1, 2 * HEADS:], NEAR, None, ALU.is_gt))
            v.end()

        @block.tensor
        def _(pe):
            pe.wait_ge(c.dve_step.sem, c.ends_in)
            nc.tensor.transpose(endst[:, :], ends[:, :], c.ident[:, :]).then_inc(c.product.sem, 1)
            pe.wait_ge(c.dve_step.sem, c.diagonal)
            nc.tensor.matmul(endall[:, :], c.ones[0:2 * HEADS, :], diag[:, :], start=True, stop=True).then_inc(c.product.sem, 1)
            c.product.base += 2


def segment_max(nc, c, table, dram, width, heads, slots, chunks, flag):
    n = c.fresh()
    W = width + HEADS
    indexed, gathered, onehot, flipped, copied, spreads, topped, step = (
        nc.alloc_semaphore(f"max_{name}{n}") for name in ("indexed", "gathered", "onehot", "flipped", "copied", "spread", "topped", "step"))
    with (
        nc.sbuf_tensor(f"mg{n}", [P, W], F32) as g, nc.sbuf_tensor(f"moh{n}", [P, P], F32) as oh,
        nc.sbuf_tensor(f"midx{n}", [P, 1], I32) as idx, nc.sbuf_tensor(f"mesT{n}", [HEADS, P], F32) as est,
        nc.sbuf_tensor(f"mfar{n}", [P, P], F32) as far, nc.sbuf_tensor(f"mv{n}", [P, HEADS, P], F32) as val,
        nc.sbuf_tensor(f"mc{n}", [P, HEADS], F32) as cm,
        nc.psum_tensor(f"mflip{n}", [P, P], F32) as flip, nc.psum_tensor(f"mest{n}", [HEADS, P], F32) as estp,
        nc.psum_tensor(f"mspread{n}", [P, HEADS, P], F32) as spread, nc.Block() as block,
    ):
        @block.scalar
        def _(act):
            far_apart = act.value_load(flag[0:1, 0:1], min_val=0, max_val=1)
            with act.If(far_apart > 0):
                with act.Fori(0, chunks) as k:
                    act.wait_ge(topped, k + 1)
                    nc.scalar.copy(idx[:, :], slots.src[:, bass.ds(k, 1)]).then_inc(indexed, 1)
                    act.wait_ge(flipped, k + 1)
                    nc.scalar.copy(est[0:heads, :], estp[0:heads, :]).then_inc(copied, 1)

        @block.gpsimd
        def _(pool):
            far_apart = pool.value_load(flag[0:1, 0:1], min_val=0, max_val=1)
            with pool.If(far_apart > 0):
                asked = pool.alloc_register(f"asked{n}")
                pool.reg_mov(asked, 1)
                with pool.Fori(0, chunks) as k:
                    pool.wait_ge(indexed, asked)
                    pool.reg_add(asked, asked, 1)
                    nc.gpsimd.indirect_dma_start(out=g[:, :], out_offset=None, in_=dram,
                                                 in_offset=bass.IndirectOffsetOnAxis(ap=idx[:, 0:1], axis=0)).then_inc(gathered, 16)

        @block.tensor
        def _(pe):
            far_apart = pe.value_load(flag[0:1, 0:1], min_val=0, max_val=1)
            with pe.If(far_apart > 0):
                with pe.Fori(0, chunks) as k:
                    pe.wait_ge(onehot, k + 1)
                    nc.tensor.transpose(flip[:, :], oh[:, :], c.ident[:, :])
                    pe.wait_ge(gathered, k * 16 + 16)
                    nc.tensor.transpose(estp[0:heads, :], g[:, width:width + heads], c.ident[:, :]).then_inc(flipped, 1)
                    pe.wait_ge(copied, k + 1)
                    for h in range(heads):
                        ins = nc.tensor.matmul(spread[:, h, :], c.pick[0:heads, h, :], est[0:heads, :], start=True, stop=True)
                    ins.then_inc(spreads, 1)

        @block.vector
        def _(dve):
            nv = nc.vector
            far_apart = dve.value_load(flag[0:1, 0:1], min_val=0, max_val=1)
            with dve.If(far_apart > 0):
                nv.tensor_copy(c.top[:, :, 0:heads], table[:, :, width:width + heads]).then_inc(topped, 1)
                with dve.Fori(0, chunks) as k:
                    nv.tensor_scalar(oh[:, :], c.iota[:, 0:P], slots.place[:, bass.ds(k, 1)], None, ALU.is_equal).then_inc(onehot, 1)
                    t = dve.value_load(slots.tile[0:1, bass.ds(k + QUAD, 1)], min_val=0, max_val=BUCKETS - 1)
                    dve.wait_ge(flipped, k + 1)
                    nv.tensor_scalar(far[:, :], flip[:, :], -1.0, FAR, ALU.add, ALU.mult).then_inc(step, 1)
                    dve.wait_ge(step, k * 3 + 1)
                    dve.wait_ge(spreads, k + 1)
                    nv.tensor_tensor(val[:, 0:heads, :], spread[:, 0:heads, :], mid(far[:, :], heads), ALU.add).then_inc(step, 1)
                    dve.wait_ge(step, k * 3 + 2)
                    nv.tensor_reduce(cm[:, 0:heads], val[:, 0:heads, :], AX.X, ALU.max).then_inc(step, 1)
                    dve.wait_ge(step, k * 3 + 3)
                    dve.wait_ge(topped, k + 1)
                    at = c.top[:, bass.ds(t, 1), 0:heads].rearrange("p t h -> p (t h)")
                    nv.tensor_tensor(at, at, cm[:, 0:heads], ALU.max).then_inc(topped, 1)


def attend(nc, c, table, dram, width, heads, slots, chunks, acc):
    C = width // heads
    store_table(nc, c, table, dram)
    spread_guard(nc, c, table, width, heads, c.flag)
    segment_max(nc, c, table, dram, width, heads, slots, chunks, c.flag)
    edm = c.edm[:, :].rearrange("p (t k) -> p t k", t=T)
    with nc.sbuf_tensor(f"self{c.fresh()}", [P, T, 3 * HEADS], F32) as s, nc.Block() as block:
        @block.vector
        def _(dve):
            v = Steps(dve, c.dve_step)
            nv = nc.vector
            es, a, b = table[:, :, width:width + heads], s[:, :, 0:heads], s[:, :, HEADS:HEADS + heads]
            ed, m = edm[:, :, 0:heads], edm[:, :, HEADS:HEADS + heads]
            v.did(nv.memset(c.edm[:, :], 0.0))
            v.did(nv.memset(acc[:, :, width:width + HEADS], 0.0))
            v.wait()
            v.did(nv.tensor_copy(ed, c.ed[:, :, 0:heads]))
            v.do(nv.tensor_tensor(b, c.top[:, :, 0:heads], c.ed[:, :, 0:heads], ALU.add))
            v.do(nv.scalar_tensor_tensor(m, b, 0.2, b, ALU.mult, ALU.max))
            v.do(nv.tensor_tensor(a, es, ed, ALU.add))
            v.do(nv.scalar_tensor_tensor(a, a, 0.2, a, ALU.mult, ALU.max))
            ready = v.did(nv.tensor_tensor(a, a, m, ALU.subtract)) + v.at
            c.self_ready = ready
            dve.wait_ge(c.act_step.sem, c.act_step.base + 1)
            for h in range(heads):
                v.did(nv.tensor_tensor(acc[:, :, h * C:(h + 1) * C], table[:, :, h * C:(h + 1) * C],
                                       s[:, :, 2 * HEADS + h].unsqueeze(2).broadcast_to([P, T, C]), ALU.mult))
            z = width if heads > 1 else width + 1
            v.did(nv.tensor_copy(acc[:, :, z:z + heads], s[:, :, 2 * HEADS:2 * HEADS + heads]))
            v.end()

        @block.scalar
        def _(act):
            a = Steps(act, c.act_step)
            act.wait_ge(c.dve_step.sem, c.self_ready)
            a.did(nc.scalar.activation(s[:, :, 2 * HEADS:2 * HEADS + heads], s[:, :, 0:heads], ACT.Exp))
            a.end()
    gather_sum(nc, c, dram, width, heads, slots, chunks, acc)


def load(nc, c, pairs):
    with nc.Block() as block:
        @block.sync
        def _(sp):
            for dst, src in pairs:
                sp.dma_start(dst, src).then_inc(c.loaded.sem, 16)
                c.loaded.base += 16
            sp.wait_ge(c.loaded.sem, c.loaded.base)


def flat(ap):
    return ap.rearrange("p t f -> p (t f)")


def sage(nc, c, ins, k, slots):
    store_table(nc, c, c.table, c.dram)
    with nc.Block() as block:
        @block.vector
        def _(dve):
            v = Steps(dve, c.dve_step)
            v.did(nc.vector.memset(c.acc[:, :, :], 0.0))
            v.end()
    gather_sum(nc, c, c.dram, D, 0, slots, GRAPH_CHUNKS, c.acc)
    n = c.fresh()
    with nc.sbuf_tensor(f"sw{n}", [P, 4, D], F32) as w, nc.sbuf_tensor(f"rdeg{n}", [P, T], F32) as rdeg, \
            nc.sbuf_tensor(f"so{n}", [P, 2, D], F32) as o:
        load(nc, c, [(flat(w[:, :, :]), ins[f"sage{k}"])])
        with nc.Block() as block:
            @block.vector
            def _(dve):
                v = Steps(dve, c.dve_step)
                v.do(nc.vector.tensor_scalar(rdeg[:, :], c.acc[:, :, D], 1.0, None, ALU.max))
                v.do(nc.vector.reciprocal(rdeg[:, :], rdeg[:, :]))
                v.end()

        def prep(v, t, a):
            v.did(nc.vector.tensor_copy(a[:, 0:D], flat(c.table[:, bass.ds(t, 1), 0:D])))
            return nc.vector.tensor_scalar(a[:, D:2 * D], flat(c.acc[:, bass.ds(t, 1), 0:D]), rdeg[:, bass.ds(t, 1)], None, ALU.mult)

        def post(v, t, prod):
            u = v.parity
            v.parity ^= 1
            v.do(nc.vector.tensor_tensor(o[:, u, :], prod, row(c.rows, f"sb{k}"), ALU.add))
            tab = flat(c.table[:, bass.ds(t, 1), 0:D])
            if k == 1:
                return nc.vector.scalar_tensor_tensor(tab, o[:, u, :], 0.0, tab, ALU.max, ALU.add)
            v.do(nc.vector.scalar_tensor_tensor(o[:, u, :], o[:, u, :], 0.0, tab, ALU.max, ALU.add))
            x = flat(c.x[:, bass.ds(t, 1), :])
            return nc.vector.tensor_tensor(x, x, o[:, u, :], ALU.add)

        dense(nc, c, 4, D, lambda h: w[:, h, :], prep, post, 1, 1 if k == 1 else 2)


def ln_prep(nc, c):
    def prep(v, t, a):
        return normalized(nc, c, a, t)
    return prep


def gat_rows(nc, c, w, width, heads, table, from_acc=False):
    def prep(v, t, a):
        if from_acc:
            return nc.vector.tensor_copy(a, flat(c.acc[:, bass.ds(t, 1), 0:D]))
        return normalized(nc, c, a, t)

    def post(v, t, prod):
        v.did(nc.vector.tensor_copy(flat(table[:, bass.ds(t, 1), 0:width + heads]), prod[:, 0:width + heads]))
        return nc.vector.tensor_copy(flat(c.ed[:, bass.ds(t, 1), 0:heads]), prod[:, width + heads:width + 2 * heads])

    dense(nc, c, 2, width + 2 * heads, lambda h: w[:, h, :], prep, post, 0, 1)


def fold(nc, c, w, width, heads, src, dst):
    C = width // heads
    with nc.sbuf_tensor(f"fold{c.fresh()}", [P, 2, width], F32) as f, nc.Block() as block:
        @block.vector
        def _(dve):
            v = Steps(dve, c.dve_step)
            for n, name in enumerate((src, dst)):
                v.do(nc.vector.tensor_tensor(f[:, :, :], w[:, :, 0:width], mid(row(c.rows, name), 2), ALU.mult))
                for k in range(2):
                    v.do(nc.vector.tensor_reduce(w[:, k, width + n * heads:width + (n + 1) * heads],
                                                 f[:, k, :].rearrange("p (h c) -> p h c", h=heads), AX.X, ALU.add))
            v.end()


def gat_layer(nc, c, ins, slots):
    layer_stats(nc, c)
    with nc.sbuf_tensor("gw0", [P, 2, D + 2 * HEADS], F32) as w:
        load(nc, c, [(w[:, :, 0:D], ins["gw0"].rearrange("p (k f) -> p k f", k=2))])
        fold(nc, c, w, D, HEADS, "as0", "ad0")
        gat_rows(nc, c, w, D, HEADS, c.table)
    attend(nc, c, c.table, c.dram, D, HEADS, slots, GRAPH_CHUNKS, c.acc)
    with (
        nc.sbuf_tensor("bnrow", [P, 4, D], F32) as r, nc.psum_tensor("bnsum", [P, 2, 512], F32) as total, nc.Block() as block,
    ):
        full = c.acc[:, :, 0:D]
        tmp = c.table[:, :, 0:D]

        @block.vector
        def _(dve):
            v = Steps(dve, c.dve_step)
            nv = nc.vector
            v.do(nv.reciprocal(c.acc[:, :, D:D + HEADS], c.acc[:, :, D:D + HEADS]))
            for h in range(HEADS):
                part = c.acc[:, :, h * 64:(h + 1) * 64]
                v.did(nv.tensor_tensor(part, part, c.acc[:, :, D + h].unsqueeze(2).broadcast_to([P, T, 64]), ALU.mult))
            v.wait()
            v.do(nv.tensor_tensor(full, full, mid(row(c.rows, "gb0"), T), ALU.add))
            v.did(nv.tensor_tensor(full, full, last(c.valid[:, :], D), ALU.mult))
            c.bn1 = v.at + v.n
            dve.wait_ge(c.product.sem, c.product.base + 1)
            v.do(nv.tensor_scalar(r[:, 0, :], total[:, 0, 0:D], 1.0 / NODES, None, ALU.mult))
            v.do(nv.tensor_tensor(full, full, mid(r[:, 0, :], T), ALU.subtract))
            v.do(nv.tensor_tensor(full, full, last(c.valid[:, :], D), ALU.mult))
            v.did(nv.tensor_tensor(tmp, full, full, ALU.mult))
            c.bn2 = v.at + v.n
            dve.wait_ge(c.product.sem, c.product.base + 2)
            v.did(nv.tensor_scalar(r[:, 1, :], total[:, 1, 0:D], 1.0 / NODES, None, ALU.mult))
            c.bn3 = v.at + v.n
            dve.wait_ge(c.act_step.sem, c.act_step.base + 1)
            v.do(nv.reciprocal(r[:, 2, :], r[:, 2, :]))
            v.do(nv.tensor_tensor(r[:, 2, :], r[:, 2, :], row(c.rows, "gamma0"), ALU.mult))
            v.do(nv.tensor_tensor(full, full, mid(r[:, 2, :], T), ALU.mult))
            v.do(nv.tensor_tensor(full, full, mid(row(c.rows, "beta0"), T), ALU.add))
            v.did(nv.tensor_scalar(tmp, full, 0.0, None, ALU.min))
            c.bn4 = v.at + v.n
            dve.wait_ge(c.act_step.sem, c.act_step.base + 2)
            v.do(nv.scalar_tensor_tensor(full, full, 0.0, tmp, ALU.max, ALU.add))
            v.did(nv.tensor_scalar(full, full, -1.0, None, ALU.add))
            v.end()

        @block.scalar
        def _(act):
            a = Steps(act, c.act_step)
            act.wait_ge(c.dve_step.sem, c.bn3)
            a.did(nc.scalar.activation(r[:, 2, :], r[:, 1, :], ACT.Sqrt, bias=c.eps[:, 0:1]))
            act.wait_ge(c.dve_step.sem, c.bn4)
            a.did(nc.scalar.activation(tmp, tmp, ACT.Exp))
            a.end()

        @block.tensor
        def _(pe):
            for n, (at, what) in enumerate(((c.bn1, c.acc), (c.bn2, c.table))):
                pe.wait_ge(c.dve_step.sem, at)
                nc.tensor.matmul(total[:, n, 0:D], c.ones[:, :], what[:, 0, 0:D], start=True, stop=False)
                with pe.Fori(1, T - 1) as t:
                    nc.tensor.matmul(total[:, n, 0:D], c.ones[:, :], flat(what[:, bass.ds(t, 1), 0:D]), start=False, stop=False)
                nc.tensor.matmul(total[:, n, 0:D], c.ones[:, :], what[:, T - 1, 0:D], start=False, stop=True).then_inc(c.product.sem, 1)
            c.product.base += 2

    with nc.sbuf_tensor("gw1", [P, 2, D + 2], F32) as w:
        load(nc, c, [(w[:, :, 0:D], ins["gw1"].rearrange("p (k f) -> p k f", k=2))])
        fold(nc, c, w, D, 1, "as1", "ad1")
        with nc.Block() as block:
            @block.vector
            def _(dve):
                v = Steps(dve, c.dve_step)
                v.do(nc.vector.memset(c.table[:, :, D:ROW], 0.0))
                v.did(nc.vector.memset(c.table[:, :, D + 1:D + 2], 1.0))
                v.end()
        gat_rows(nc, c, w, D, 1, c.table, from_acc=True)
    attend(nc, c, c.table, c.dram, D, 1, slots, GRAPH_CHUNKS, c.acc)
    with nc.sbuf_tensor("nrm", [P, T, 2], F32) as nrm, nc.Block() as block:
        full, tmp = c.acc[:, :, 0:D], c.table[:, :, 0:D]

        @block.vector
        def _(dve):
            v = Steps(dve, c.dve_step)
            nv = nc.vector
            v.do(nv.reciprocal(nrm[:, :, 0], c.acc[:, :, D + 1]))
            v.do(nv.tensor_tensor(full, full, last(nrm[:, :, 0], D), ALU.mult))
            v.do(nv.tensor_tensor(full, full, mid(row(c.rows, "gb1"), T), ALU.add))
            v.do(nv.tensor_tensor(tmp, full, full, ALU.mult))
            v.did(nv.tensor_reduce(nrm[:, :, 1], tmp, AX.X, ALU.add))
            c.squares = v.at + v.n
            dve.wait_ge(c.act_step.sem, c.act_step.base + 1)
            v.do(nv.tensor_scalar(nrm[:, :, 1], nrm[:, :, 1], 1e-12, None, ALU.max))
            v.do(nv.reciprocal(nrm[:, :, 1], nrm[:, :, 1]))
            v.do(nv.tensor_tensor(full, full, last(nrm[:, :, 1], D), ALU.mult))
            v.did(nv.tensor_tensor(c.x[:, :, :], c.x[:, :, :], full, ALU.add))
            v.end()

        @block.scalar
        def _(act):
            a = Steps(act, c.act_step)
            act.wait_ge(c.dve_step.sem, c.squares)
            a.did(nc.scalar.activation(nrm[:, :, 1], nrm[:, :, 1], ACT.Sqrt))
            a.end()


def slice_layer(nc, c, ins):
    SH, G = SLICE_HEADS, SLICE
    HG = SH * G
    layer_stats(nc, c)
    with (
        nc.sbuf_tensor("sw", [P, T, HG], F32) as sw, nc.sbuf_tensor("pooled", [P, 3, HG], F32) as pooled,
        nc.sbuf_tensor("zout", [P, 4, D], F32) as zout,
    ):
        with (
            nc.sbuf_tensor("wxT", [G, SH, D], F32) as wxt, nc.sbuf_tensor("wsl", [G, G], F32) as wsl,
            nc.sbuf_tensor("bx", [G, SH], F32) as bx, nc.sbuf_tensor("wl", [P, 2, HG], F32) as wl,
            nc.sbuf_tensor("bl", [P, HG], F32) as bl, nc.sbuf_tensor("invt", [P, SH], F32) as invt,
            nc.sbuf_tensor("bxw", [G, SH, P], F32) as bxw,
        ):
            load(nc, c, [(wxt[:, :, :].rearrange("p h k -> p (h k)"), ins["wxT"]), (wsl[:, :], ins["wslice"]), (bx[:, :], ins["bx"])])
            with nc.psum_tensor("wlp", [P, 2, 512], F32) as wlp, nc.psum_tensor("blp", [P, 512], F32) as blp, nc.Block() as block:
                @block.vector
                def _(dve):
                    v = Steps(dve, c.dve_step)
                    nv = nc.vector
                    v.did(nv.tensor_copy(bxw[:, :, :], last(bx[:, :], P)))
                    c.wide = v.at + v.n
                    v.do(nv.tensor_scalar(invt[:, :], row(c.rows, "temp"), 0.1, 5.0, ALU.max, ALU.min))
                    v.did(nv.reciprocal(invt[:, :], invt[:, :]))
                    dve.wait_ge(c.product.sem, c.product.base + 1)
                    v.did(nv.tensor_copy(wl[:, :, :], wlp[:, :, :]))
                    v.did(nv.tensor_tensor(bl[:, :].rearrange("p (h g) -> p h g", h=SH), blp[:, :].rearrange("p (h g) -> p h g", h=SH),
                                           mid(row(c.rows, "b_slice"), SH), ALU.add))
                    v.end()

                @block.tensor
                def _(pe):
                    pe.wait_ge(c.dve_step.sem, c.wide)
                    for h in range(SH):
                        for k in range(2):
                            nc.tensor.matmul(wlp[:, k, h * G:(h + 1) * G], wxt[:, h, k * P:(k + 1) * P], wsl[:, :], start=True, stop=True)
                        ins_ = nc.tensor.matmul(blp[:, h * G:(h + 1) * G], bxw[:, h, :], wsl[:, :], start=True, stop=True)
                    ins_.then_inc(c.product.sem, 1)
                    c.product.base += 1
            slice_weights(nc, c, sw, wl, bl, invt, pooled)
        slice_attention(nc, c, ins, pooled, zout)
        with nc.sbuf_tensor("so", [P, 2, D], F32) as o:
            def prep(v, t, a):
                return nc.vector.tensor_copy(a, flat(sw[:, bass.ds(t, 1), :]))

            def post(v, t, prod):
                u = v.parity
                v.parity ^= 1
                v.do(nc.vector.tensor_tensor(o[:, u, :], prod, row(c.rows, "b_out"), ALU.add))
                x = flat(c.x[:, bass.ds(t, 1), :])
                return nc.vector.tensor_tensor(x, x, o[:, u, :], ALU.add)

            dense(nc, c, 4, D, lambda h: zout[:, h, :], prep, post, 0, 1)


def slice_weights(nc, c, sw, wl, bl, invt, pooled):
    SH, G = SLICE_HEADS, SLICE
    HG = SH * G
    turns = T // 2
    rows_at, flip_at, flat_at, prod_at, ready_at, expo_at, weighted_at, pooled_at = (
        s.base for s in (c.rows_in, c.flipped, c.feature_major, c.product, c.ready, c.expo, c.weighted, c.taken))
    with (
        nc.sbuf_tensor("srows", [P, 2, D], F32) as a, nc.sbuf_tensor("srowsT", [P, 2, 2, P], F32) as at,
        nc.sbuf_tensor("slog", [P, 2, HG], F32) as lg, nc.sbuf_tensor("smx", [P, 2, 2, SH], F32) as mx,
        nc.psum_tensor("sflip", [P, 2, 512], F32) as flip, nc.psum_tensor("sprod", [P, 2, 512], F32) as prod,
        nc.psum_tensor("spool", [P, 3, 512], F32) as pool_, nc.Block() as block,
    ):
        @block.vector
        def _(dve):
            v = Steps(dve, c.dve_step)
            nv = nc.vector
            with dve.Fori(0, turns) as i:
                v.enter(i, 12, turns)
                for u in range(2):
                    dve.wait_ge(c.taken.sem, pooled_at + i * 2 + (u - 1))
                    normalized(nc, c, a[:, u, :], i * 2 + u).then_inc(c.rows_in.sem, 1)
                for u in range(2):
                    lv = lg[:, u, :].rearrange("p (h g) -> p h g", h=SH)
                    dve.wait_ge(c.product.sem, prod_at + i * 2 + u + 1)
                    v.do(nv.tensor_tensor(lg[:, u, :], prod[:, u, :], bl[:, :], ALU.add))
                    v.do(nv.tensor_tensor(lv, lv, last(invt[:, :], G), ALU.mult))
                    v.do(nv.tensor_reduce(mx[:, u, 0, :], lv, AX.X, ALU.max))
                    nv.tensor_tensor(lv, lv, last(mx[:, u, 0, :], G), ALU.subtract).then_inc(c.ready.sem, 1)
                for u in range(2):
                    t = i * 2 + u
                    sv = flat(sw[:, bass.ds(t, 1), :]).rearrange("p (h g) -> p h g", h=SH)
                    dve.wait_ge(c.expo.sem, expo_at + i * 2 + u + 1)
                    v.do(nv.tensor_reduce(mx[:, u, 1, :], sv, AX.X, ALU.add))
                    v.do(nv.reciprocal(mx[:, u, 1, :], mx[:, u, 1, :]))
                    v.do(nv.tensor_scalar(mx[:, u, 1, :], mx[:, u, 1, :], c.valid[:, bass.ds(t, 1)], None, ALU.mult))
                    nv.tensor_tensor(sv, sv, last(mx[:, u, 1, :], G), ALU.mult).then_inc(c.weighted.sem, 1)
                v.leave()
            dve.wait_ge(c.taken.sem, pooled_at + T + 1)
            v.did(nv.tensor_copy(pooled[:, :, :], pool_[:, :, :]))
            v.end()

        @block.scalar
        def _(act):
            with act.Fori(0, turns) as i:
                for u in range(2):
                    act.wait_ge(c.flipped.sem, flip_at + i * 2 + u + 1)
                    act.wait_ge(c.product.sem, prod_at + i * 2 + (u - 1))
                    nc.scalar.copy(at[:, u, :, :].rearrange("p h n -> p (h n)"), flip[:, u, 0:D]).then_inc(c.feature_major.sem, 1)
                for u in range(2):
                    act.wait_ge(c.ready.sem, ready_at + i * 2 + u + 1)
                    nc.scalar.activation(flat(sw[:, bass.ds(i * 2 + u, 1), :]), lg[:, u, :], ACT.Exp).then_inc(c.expo.sem, 1)

        @block.tensor
        def _(pe):
            zero = c.zero[:, 0:1].broadcast_to([P, 512])
            for n in range(3):
                nc.tensor.matmul(pool_[:, n, :], c.zero[:, :], zero, start=True, stop=False)
            with pe.Fori(0, turns) as i:
                for u in range(2):
                    pe.wait_ge(c.rows_in.sem, rows_at + i * 2 + u + 1)
                    pe.wait_ge(c.feature_major.sem, flat_at + i * 2 + (u - 1))
                    for h in range(2):
                        ins = nc.tensor.transpose(flip[:, u, h * P:(h + 1) * P], a[:, u, h * P:(h + 1) * P], c.ident[:, :])
                    ins.then_inc(c.flipped.sem, 1)
                for u in range(2):
                    pe.wait_ge(c.feature_major.sem, flat_at + i * 2 + u + 1)
                    pe.wait_ge(c.ready.sem, ready_at + i * 2 + (u - 1))
                    for h in range(2):
                        ins = nc.tensor.matmul(prod[:, u, :], at[:, u, h, :], wl[:, h, :], start=(h == 0), stop=(h == 1))
                    ins.then_inc(c.product.sem, 1)
                for u in range(2):
                    pe.wait_ge(c.weighted.sem, weighted_at + i * 2 + u + 1)
                    s = flat(sw[:, bass.ds(i * 2 + u, 1), :])
                    for n, left in enumerate((a[:, u, 0:P], a[:, u, P:D], c.ones[:, :])):
                        ins = nc.tensor.matmul(pool_[:, n, :], left, s, start=False, stop=False)
                    ins.then_inc(c.taken.sem, 1)
            for n in range(3):
                ins = nc.tensor.matmul(pool_[:, n, :], c.zero[:, :], zero, start=False, stop=True)
            ins.then_inc(c.taken.sem, 1)

        for s in (c.rows_in, c.flipped, c.feature_major, c.product, c.ready, c.expo, c.weighted):
            s.base += T
        c.taken.base += T + 1


def slice_attention(nc, c, ins, pooled, zout):
    SH, G = SLICE_HEADS, SLICE
    HG = SH * G
    with (
        nc.sbuf_tensor("wfx", [P, 2, HG], F32) as wfx, nc.sbuf_tensor("bfx", [G, SH], F32) as bfx,
        nc.sbuf_tensor("wqkv", [G, 3, G], F32) as wqkv, nc.sbuf_tensor("wo", [G, SH, D], F32) as wo,
        nc.sbuf_tensor("tok", [G, 8, HG], F32) as tok, nc.sbuf_tensor("amx", [G, 2, SH], F32) as amx,
    ):
        load(nc, c, [(wfx[:, :, :].rearrange("p k f -> p (k f)"), ins["wfx"]), (bfx[:, :], ins["bfx"]),
                     (wqkv[:, :, :].rearrange("p k f -> p (k f)"), ins["wqkv"]), (wo[:, :, :].rearrange("p k f -> p (k f)"), ins["wo"])])
        with (
            nc.psum_tensor("tokp", [G, 512], F32) as tokp, nc.psum_tensor("qkvp", [G, 3, 512], F32) as qkvp,
            nc.psum_tensor("attp", [G, 512], F32) as attp, nc.psum_tensor("atT", [G, 512], F32) as atp,
            nc.psum_tensor("zp", [P, 4, D], F32) as zp, nc.Block() as block,
        ):
            st, den, q, k, val, att, attT, osT = (tok[:, n, :] for n in range(8))
            hs = lambda x, h: x[:, h * G:(h + 1) * G]
            by_head = lambda x: x.rearrange("p (h g) -> p h g", h=SH)
            done = c.product.base

            @block.vector
            def _(dve):
                v = Steps(dve, c.dve_step)
                nv = nc.vector
                c.marks = []

                def mark():
                    c.marks.append(v.at + v.n)
                norm = pooled[0:G, 2, :]
                v.did(nv.tensor_tensor(by_head(st), by_head(norm), last(bfx[:, :], G), ALU.mult))
                v.do(nv.tensor_scalar(den, norm, EPS, None, ALU.add))
                v.do(nv.reciprocal(den, den))
                dve.wait_ge(c.product.sem, done + 1)
                v.do(nv.tensor_tensor(st, st, tokp[:, :], ALU.add))
                v.did(nv.tensor_tensor(st, st, den, ALU.mult))
                mark()
                dve.wait_ge(c.product.sem, done + 2)
                for n, x in enumerate((q, k, val)):
                    v.did(nv.tensor_copy(x, qkvp[:, n, :]))
                mark()
                dve.wait_ge(c.product.sem, done + 3)
                v.do(nv.tensor_scalar(att, attp[:, :], G ** -0.5, None, ALU.mult))
                v.do(nv.tensor_reduce(amx[:, 0, :], by_head(att), AX.X, ALU.max))
                v.did(nv.tensor_tensor(by_head(att), by_head(att), last(amx[:, 0, :], G), ALU.subtract))
                mark()
                dve.wait_ge(c.act_step.sem, c.act_step.base + 1)
                v.do(nv.tensor_reduce(amx[:, 1, :], by_head(att), AX.X, ALU.add))
                v.do(nv.reciprocal(amx[:, 1, :], amx[:, 1, :]))
                v.did(nv.tensor_tensor(by_head(att), by_head(att), last(amx[:, 1, :], G), ALU.mult))
                mark()
                dve.wait_ge(c.product.sem, done + 4)
                v.did(nv.tensor_copy(attT, atp[:, :]))
                mark()
                dve.wait_ge(c.product.sem, done + 5)
                v.did(nv.tensor_copy(osT, attp[:, :]))
                mark()
                dve.wait_ge(c.product.sem, done + 6)
                v.did(nv.tensor_copy(zout[:, :, :], zp[:, :, :]))
                v.end()

            @block.scalar
            def _(act):
                a = Steps(act, c.act_step)
                act.wait_ge(c.dve_step.sem, c.marks[2])
                a.did(nc.scalar.activation(att, att, ACT.Exp))
                a.end()

            @block.tensor
            def _(pe):
                mm = lambda out, l, r, s=True, e=True: nc.tensor.matmul(out, l, r, start=s, stop=e)
                for h in range(SH):
                    for kk in range(2):
                        ins_ = mm(hs(tokp, h), wfx[:, kk, h * G:(h + 1) * G], pooled[:, kk, h * G:(h + 1) * G], kk == 0, kk == 1)
                ins_.then_inc(c.product.sem, 1)
                pe.wait_ge(c.dve_step.sem, c.marks[0])
                mm(qkvp[:, 0, :], wqkv[:, 0, :], st)
                mm(qkvp[:, 1, :], wqkv[:, 1, :], st)
                for h in range(SH):
                    ins_ = mm(qkvp[:, 2, h * G:(h + 1) * G], hs(st, h), wqkv[:, 2, :])
                ins_.then_inc(c.product.sem, 1)
                pe.wait_ge(c.dve_step.sem, c.marks[1])
                for h in range(SH):
                    ins_ = mm(hs(attp, h), hs(q, h), hs(k, h))
                ins_.then_inc(c.product.sem, 1)
                pe.wait_ge(c.dve_step.sem, c.marks[3])
                for h in range(SH):
                    ins_ = nc.tensor.transpose(hs(atp, h), hs(att, h), c.ident[0:G, 0:G])
                ins_.then_inc(c.product.sem, 1)
                pe.wait_ge(c.dve_step.sem, c.marks[4])
                for h in range(SH):
                    ins_ = mm(hs(attp, h), hs(val, h), hs(attT, h))
                ins_.then_inc(c.product.sem, 1)
                pe.wait_ge(c.dve_step.sem, c.marks[5])
                for h in range(SH):
                    ins_ = mm(zp[(h % 2) * G:(h % 2 + 1) * G, h // 2, :], hs(osT, h), wo[:, h, :])
                ins_.then_inc(c.product.sem, 1)
                c.product.base += 6


def expert_layer(nc, c, ins, slots, out):
    T20 = 20
    layer_stats(nc, c)
    with (
        nc.sbuf_tensor("rtab", [P, T, T20], F32) as rtab, nc.sbuf_tensor("racc", [P, T, T20], F32) as racc,
        nc.sbuf_tensor("gates", [P, T, EXPERTS], F32) as gates,
    ):
        with nc.sbuf_tensor("rw", [P, 2, 24], F32) as w:
            load(nc, c, [(w[:, :, 0:16], ins["rw"].rearrange("p (k f) -> p k f", k=2))])
            fold(nc, c, w, 16, HEADS, "ras", "rad")
            gat_rows(nc, c, w, 16, HEADS, rtab)
        attend(nc, c, rtab, c.rdram, 16, HEADS, slots, ROUTER_CHUNKS, racc)
        route(nc, c, racc, gates)
        experts(nc, c, ins, gates, out)


def route(nc, c, racc, gates):
    E = EXPERTS
    with (
        nc.sbuf_tensor("r16", [P, T, 16], F32) as s16, nc.sbuf_tensor("q16", [P, T, 16], F32) as q16,
        nc.sbuf_tensor("m1", [P, 4, T], F32) as m1, nc.sbuf_tensor("sc", [P, T, E], F32) as sc,
        nc.sbuf_tensor("earlier", [P, E, E], F32) as earlier, nc.Block() as block,
    ):
        @block.vector
        def _(dve):
            v = Steps(dve, c.dve_step)
            nv = nc.vector
            z = racc[:, :, 16:16 + HEADS]
            v.do(nv.tensor_scalar(z, z, 1e-16, None, ALU.add))
            v.do(nv.reciprocal(z, z))
            for h in range(HEADS):
                v.did(nv.tensor_tensor(s16[:, :, h * E:(h + 1) * E], racc[:, :, h * E:(h + 1) * E],
                                       racc[:, :, 16 + h].unsqueeze(2).broadcast_to([P, T, E]), ALU.mult))
            v.wait()
            v.do(nv.tensor_tensor(s16[:, :, :], s16[:, :, :], mid(row(c.rows, "rb"), T), ALU.add))
            v.do(nv.tensor_reduce(m1[:, 0, :], s16[:, :, :], AX.X, ALU.add))
            v.do(nv.tensor_scalar(m1[:, 0, :], m1[:, 0, :], 1.0 / 16, None, ALU.mult))
            v.do(nv.tensor_tensor(s16[:, :, :], s16[:, :, :], last(m1[:, 0, :], 16), ALU.subtract))
            v.do(nv.tensor_tensor(q16[:, :, :], s16[:, :, :], s16[:, :, :], ALU.mult))
            v.do(nv.tensor_reduce(m1[:, 1, :], q16[:, :, :], AX.X, ALU.add))
            v.did(nv.tensor_scalar(m1[:, 1, :], m1[:, 1, :], 1.0 / 16, None, ALU.mult))
            c.var = v.at + v.n
            dve.wait_ge(c.act_step.sem, c.act_step.base + 1)
            v.do(nv.reciprocal(m1[:, 1, :], m1[:, 1, :]))
            v.do(nv.tensor_tensor(s16[:, :, :], s16[:, :, :], last(m1[:, 1, :], 16), ALU.mult))
            v.do(nv.tensor_tensor(s16[:, :, :], s16[:, :, :], mid(row(c.rows, "lng"), T), ALU.mult))
            v.do(nv.tensor_tensor(s16[:, :, :], s16[:, :, :], mid(row(c.rows, "lnb"), T), ALU.add))
            v.do(nv.tensor_reduce(sc[:, :, :], s16[:, :, :].rearrange("p t (h e) -> p t e h", h=HEADS), AX.X, ALU.add))
            v.do(nv.tensor_scalar(sc[:, :, :], sc[:, :, :], 1.0 / HEADS, None, ALU.mult))
            v.did(nv.tensor_tensor(earlier[:, :, :], mid(c.iota[:, 0:E], E), last(c.iota[:, 0:E], E), ALU.is_lt))
            a4 = s16[:, :, :].rearrange("p t (i j) -> p t i j", i=E)
            b4 = q16[:, :, :].rearrange("p t (i j) -> p t i j", i=E)
            sj = sc[:, :, :].unsqueeze(2).broadcast_to([P, T, E, E])
            si = sc[:, :, :].unsqueeze(3).broadcast_to([P, T, E, E])
            v.do(nv.tensor_tensor(a4, sj, si, ALU.is_gt))
            v.do(nv.tensor_tensor(b4, sj, si, ALU.is_equal))
            v.do(nv.tensor_tensor(q16[:, :, :], q16[:, :, :], mid(earlier[:, :, :].rearrange("p i j -> p (i j)"), T), ALU.mult))
            v.do(nv.tensor_tensor(s16[:, :, :], s16[:, :, :], q16[:, :, :], ALU.add))
            v.do(nv.tensor_reduce(gates[:, :, :], a4, AX.X, ALU.add))
            v.do(nv.tensor_scalar(gates[:, :, :], gates[:, :, :], 1.5, None, ALU.is_lt))
            v.do(nv.tensor_reduce(m1[:, 2, :], sc[:, :, :], AX.X, ALU.max))
            v.did(nv.tensor_tensor(sc[:, :, :], sc[:, :, :], last(m1[:, 2, :], E), ALU.subtract))
            c.best = v.at + v.n
            dve.wait_ge(c.act_step.sem, c.act_step.base + 2)
            v.do(nv.tensor_tensor(gates[:, :, :], gates[:, :, :], sc[:, :, :], ALU.mult))
            v.do(nv.tensor_reduce(m1[:, 3, :], gates[:, :, :], AX.X, ALU.add))
            v.do(nv.reciprocal(m1[:, 3, :], m1[:, 3, :]))
            v.did(nv.tensor_tensor(gates[:, :, :], gates[:, :, :], last(m1[:, 3, :], E), ALU.mult))
            v.end()

        @block.scalar
        def _(act):
            a = Steps(act, c.act_step)
            act.wait_ge(c.dve_step.sem, c.var)
            a.did(nc.scalar.activation(m1[:, 1, :], m1[:, 1, :], ACT.Sqrt, bias=c.eps[:, 0:1]))
            act.wait_ge(c.dve_step.sem, c.best)
            a.did(nc.scalar.activation(sc[:, :, :], sc[:, :, :], ACT.Exp))
            a.end()


def experts(nc, c, ins, gates, out):
    E, KH, HB = EXPERTS, 2, HIDDEN // P
    turns = T // 2
    with (
        nc.sbuf_tensor("w1", [P, KH, E, HIDDEN], F32) as w1, nc.sbuf_tensor("w2", [P, E, HB, D], F32) as w2,
        nc.sbuf_tensor("b1", [P, E, HB], F32) as b1, nc.sbuf_tensor("xa", [P, 2, D], F32) as a,
        nc.sbuf_tensor("xT", [P, KH, 2 * P], F32) as xt, nc.sbuf_tensor("hid", [P, 2, HB, 2 * P], F32) as hid,
        nc.sbuf_tensor("eo", [P, 2, D], F32) as o,
    ):
        load(nc, c, [(w1[:, :, :, :].rearrange("p k e f -> p (k e f)"), ins["w1"]),
                     (w2[:, :, :, :].rearrange("p k e f -> p (k e f)"), ins["w2"]), (b1[:, :, :].rearrange("p e f -> p (e f)"), ins["b1"])])
        rows_at, flip_at, flat_at, hid_at, gelu_at, prod_at, taken_at = (
            s.base for s in (c.rows_in, c.flipped, c.feature_major, c.ready, c.expo, c.product, c.taken))
        stored_at = c.stored.base
        with (
            nc.psum_tensor("eflip", [P, KH, 2 * P], F32) as flip, nc.psum_tensor("hidp", [P, 2, HB, 2 * P], F32) as hidp,
            nc.psum_tensor("eprod", [P, 2, 512], F32) as prod, nc.Block() as block,
        ):
            @block.vector
            def _(dve):
                v = Steps(dve, c.dve_step)
                nv = nc.vector
                with dve.Fori(0, turns) as i:
                    v.enter(i, 2 * E, turns)
                    for u in range(2):
                        dve.wait_ge(c.flipped.sem, flip_at + i)
                        normalized(nc, c, a[:, u, :], i * 2 + u).then_inc(c.rows_in.sem, 1)
                    for e in range(E):
                        for u in range(2):
                            n = e * 2 + u
                            dve.wait_ge(c.product.sem, prod_at + i * 2 * E + (n + 1))
                            dve.wait_ge(c.taken.sem, taken_at + i * 2 * E + n)
                            v.do(nv.tensor_tensor(o[:, u, :], prod[:, u, 0:D], row(c.rows, "eb2")[:, e * D:(e + 1) * D], ALU.add))
                            x = flat(c.x[:, bass.ds(i * 2 + u, 1), :])
                            nv.scalar_tensor_tensor(x, o[:, u, :], gates[:, bass.ds(i * 2 + u, 1), e], x, ALU.mult,
                                                    ALU.add).then_inc(c.taken.sem, 1)
                    v.leave()
                v.end()

            @block.scalar
            def _(act):
                with act.Fori(0, turns) as i:
                    act.wait_ge(c.flipped.sem, flip_at + i + 1)
                    act.wait_ge(c.ready.sem, hid_at + i * E)
                    nc.scalar.copy(xt[:, :, :], flip[:, :, :]).then_inc(c.feature_major.sem, 1)
                    for e in range(E):
                        act.wait_ge(c.ready.sem, hid_at + i * E + (e + 1))
                        act.wait_ge(c.product.sem, prod_at + i * 2 * E + (2 * e + 2 - 4))
                        for hb in range(HB):
                            ins_ = nc.scalar.activation(hid[:, e % 2, hb, :], hidp[:, e % 2, hb, :], ACT.Gelu, bias=b1[:, e, hb:hb + 1])
                        ins_.then_inc(c.expo.sem, 1)

            @block.tensor
            def _(pe):
                with pe.Fori(0, turns) as i:
                    pe.wait_ge(c.rows_in.sem, rows_at + i * 2 + 2)
                    pe.wait_ge(c.feature_major.sem, flat_at + i)
                    for u in range(2):
                        for k in range(KH):
                            ins_ = nc.tensor.transpose(flip[:, k, u * P:(u + 1) * P], a[:, u, k * P:(k + 1) * P], c.ident[:, :])
                    ins_.then_inc(c.flipped.sem, 1)
                    pe.wait_ge(c.feature_major.sem, flat_at + i + 1)

                    def up(e):
                        pe.wait_ge(c.expo.sem, gelu_at + i * E + (e - 1))
                        for hb in range(HB):
                            for k in range(KH):
                                ins_ = nc.tensor.matmul(hidp[:, e % 2, hb, :], w1[:, k, e, hb * P:(hb + 1) * P], xt[:, k, :],
                                                        start=(k == 0), stop=(k == KH - 1))
                        ins_.then_inc(c.ready.sem, 1)

                    def down(e):
                        pe.wait_ge(c.expo.sem, gelu_at + i * E + (e + 1))
                        for u in range(2):
                            pe.wait_ge(c.taken.sem, taken_at + i * 2 * E + (2 * e + u - 1))
                            for hb in range(HB):
                                ins_ = nc.tensor.matmul(prod[:, u, 0:D], hid[:, e % 2, hb, u * P:(u + 1) * P], w2[:, e, hb, :],
                                                        start=(hb == 0), stop=(hb == HB - 1))
                            ins_.then_inc(c.product.sem, 1)

                    up(0)
                    for e in range(1, E):
                        up(e)
                        down(e - 1)
                    down(E - 1)

            @block.sync
            def _(sp):
                with sp.Fori(0, turns) as i:
                    sp.wait_ge(c.taken.sem, taken_at + i * 2 * E + 2 * E)
                    sp.dma_start(out.rearrange("p (t f) -> p t f", t=T)[:, bass.ds(i * 2, 2), :],
                                 c.x[:, bass.ds(i * 2, 2), :]).then_inc(c.stored.sem, 16)
                sp.wait_ge(c.stored.sem, stored_at + 16 * turns)


class Slots:

    def __init__(self, nc, name, chunks):
        self.src = nc.alloc_sbuf_tensor(f"{name}_src", [P, chunks + RING], I32)
        self.place = nc.alloc_sbuf_tensor(f"{name}_place", [P, chunks + RING], F32)
        self.tile = nc.alloc_sbuf_tensor(f"{name}_tile", [1, QUAD + chunks + RING], I32)


class Core:

    def __init__(self, nc):
        self.n = 0
        sb = nc.alloc_sbuf_tensor
        self.x = sb("x", [P, T, D], F32)
        self.rows = sb("rows", [P, ROWS_LEN], F32)
        self.iota, self.itmp = sb("iota", [P, 512], F32), sb("itmp", [P, 512], I32)
        self.iota16, self.zero16 = sb("iota16", [P, 512], F16), sb("zero16", [P, P], F16)
        self.part, self.ptmp = sb("part", [P, 1], F32), sb("ptmp", [P, 1], I32)
        self.ident, self.lower = sb("ident", [P, P], F32), sb("lower", [P, P], F32)
        self.ones, self.zero = sb("ones", [P, P], F32), sb("zero", [P, P], F32)
        self.pick = sb("pick", [HEADS, HEADS, P], F32)
        self.valid, self.eps = sb("valid", [P, T], F32), sb("eps", [P, 1], F32)
        self.stat = sb("stat", [P, T, 2], F32)
        self.ed, self.top = sb("ed", [P, T, HEADS], F32), sb("top", [P, T, HEADS], F32)
        self.flag = sb("flag", [1, 1], I32)
        self.edm = sb("edm", [P, T * 2 * HEADS], F32)
        self.counts = []

        def count(name):
            self.counts.append(Count(nc, name))
            return self.counts[-1]

        self.dve_step = count("dve_step")
        self.act_step = count("act_step")
        self.pool_step = count("pool_step")
        self.totals = count("totals")
        self.prefixes = count("prefixes")
        self.onehots = count("onehots")
        self.placed = count("placed")
        self.rows_in = count("rows_in")
        self.flipped = count("flipped")
        self.feature_major = count("feature_major")
        self.product = count("product")
        self.taken = count("taken")
        self.indexed = count("indexed")
        self.summed = count("summed")
        self.added = count("added")
        self.ready = count("ready")
        self.looked = count("looked")
        self.expo = count("expo")
        self.weighted = count("weighted")
        self.loaded, self.stored = Count(nc, "loaded"), Count(nc, "stored")
        for s in (self.loaded, self.stored):
            s.base = 0
        self.gathered = [nc.alloc_semaphore(f"gathered{u}") for u in range(RING)]
        self.gather_base = 0

    def fresh(self):
        self.n += 1
        return self.n


def graph_kernel(nc, ins, out):
    c = Core(nc)
    slots, rslots = Slots(nc, "graph", GRAPH_CHUNKS), Slots(nc, "router", ROUTER_CHUNKS)
    with nc.Block() as block:
        @block.gpsimd
        def _(pool):
            for s in c.counts:
                pool.sem_inc(s.sem, RING)
    constants(nc, c, ins)
    place_edges(nc, c, ins["dst"], ins["src"], GRAPH_EDGES, GRAPH_CHUNKS, slots)
    place_edges(nc, c, ins["rdst"], ins["rsrc"], ROUTER_EDGES, ROUTER_CHUNKS, rslots)
    c.table = nc.alloc_sbuf_tensor("table", [P, T, ROW], F32)
    c.acc = nc.alloc_sbuf_tensor("acc", [P, T, ROW], F32)
    c.dram = nc.dram_tensor("table_dram", (T * P, ROW), F32).ap()
    c.rdram = nc.dram_tensor("router_dram", (T * P, 20), F32).ap()
    layer_stats(nc, c)
    weighted_rows(nc, c)
    sage(nc, c, ins, 1, slots)
    sage(nc, c, ins, 2, slots)
    slice_layer(nc, c, ins)
    gat_layer(nc, c, ins, slots)
    expert_layer(nc, c, ins, rslots, out)


def layout(i):
    import numpy as np
    a = {k: np.asarray(v) for k, v in i.items()}
    x = np.zeros((T * P, D), np.float32)
    x[:NODES] = a["x"]
    kmaj = lambda w: np.ascontiguousarray(w.reshape(2, P, -1).transpose(1, 0, 2)).reshape(P, -1)
    rows = {"raw": "L0_gnn_raw_weights", "sb1": "L0_gnn_b1", "sb2": "L0_gnn_b2", "b_slice": "L0_ffn_b_slice",
            "temp": "L0_ffn_temperature", "b_out": "L0_ffn_b_out", "as0": "L1_gnn_a_src0", "ad0": "L1_gnn_a_dst0",
            "gb0": "L1_gnn_b0", "gamma0": "L1_gnn_gamma0", "beta0": "L1_gnn_beta0", "as1": "L1_gnn_a_src1",
            "ad1": "L1_gnn_a_dst1", "gb1": "L1_gnn_b1", "ras": "L1_ffn_att_src", "rad": "L1_ffn_att_dst",
            "rb": "L1_ffn_b_gat", "lng": "L1_ffn_ln_gamma", "lnb": "L1_ffn_ln_beta", "eb2": "L1_ffn_b2"}
    ei = a["L1_ffn_edge_index"]
    o = {
        "x": x.reshape(T, P, D).transpose(1, 0, 2).reshape(P, T * D),
        "rows": np.concatenate([a[rows[n]].reshape(-1) for n, _ in ROWS])[None],
        "dst": a["dst"].reshape(GRAPH_EDGES), "src": a["src"].reshape(GRAPH_EDGES),
        "rdst": ei[1].reshape(ROUTER_EDGES), "rsrc": ei[0].reshape(ROUTER_EDGES),
        "wxT": a["L0_ffn_W_x"].T.reshape(SLICE_HEADS, SLICE, D).transpose(1, 0, 2).reshape(SLICE, -1),
        "wslice": a["L0_ffn_W_slice"], "bx": a["L0_ffn_b_x"].reshape(SLICE_HEADS, SLICE).T,
        "wfx": kmaj(a["L0_ffn_W_fx"]), "bfx": a["L0_ffn_b_fx"].reshape(SLICE_HEADS, SLICE).T,
        "wqkv": np.concatenate([a["L0_ffn_W_q"], a["L0_ffn_W_k"], a["L0_ffn_W_v"]], 1),
        "wo": a["L0_ffn_W_out"].reshape(SLICE_HEADS, SLICE, D).transpose(1, 0, 2).reshape(SLICE, -1),
        "gw0": kmaj(a["L1_gnn_W0"]), "gw1": kmaj(a["L1_gnn_W1"]), "rw": kmaj(a["L1_ffn_W_gat"]),
        "w1": a["L1_ffn_W1"].reshape(EXPERTS, 2, P, HIDDEN).transpose(2, 1, 0, 3).reshape(P, -1),
        "w2": a["L1_ffn_W2"].reshape(EXPERTS, HIDDEN // P, P, D).transpose(2, 0, 1, 3).reshape(P, -1),
        "b1": a["L1_ffn_b1"].reshape(EXPERTS, HIDDEN // P, P).transpose(2, 0, 1).reshape(P, -1),
    }
    for k in (1, 2):
        o[f"sage{k}"] = np.concatenate([kmaj(a[f"L0_gnn_W_self{k}"].T), kmaj(a[f"L0_gnn_W_neigh{k}"].T)], 1)
    return {k: np.ascontiguousarray(v) for k, v in o.items()}


def kernel(**inputs):
    import numpy as np
    import concourse.bacc as bacc
    from concourse.bass_utils import run_bass_kernel_spmd

    arrays = layout(inputs)
    nc = bacc.Bacc("TRN2", target_bir_lowering=False, num_devices=1)
    ins = {k: nc.dram_tensor(f"in_{k}", a.shape, mybir.dt.from_np(a.dtype), kind="ExternalInput").ap() for k, a in arrays.items()}
    out = nc.dram_tensor("out_x", (P, T * D), F32, kind="ExternalOutput").ap()
    graph_kernel(nc, ins, out)
    r = run_bass_kernel_spmd(nc, [{f"in_{k}": a for k, a in arrays.items()}], core_ids=[0])
    got = np.asarray(r.results[0]["out_x"])
    return np.ascontiguousarray(got.reshape(P, T, D).transpose(1, 0, 2).reshape(T * P, D)[:NODES])
```

```python
from contextlib import contextmanager

import concourse.bass as bass
from concourse import mybir

F32 = mybir.dt.float32
F16 = mybir.dt.float16
I32 = mybir.dt.int32
ALU = mybir.AluOpType
ACT = mybir.ActivationFunctionType
AX = mybir.AxisListType

P = 128
NODES = 3125
D = 256
BUCKETS = -(-NODES // P)
assert BUCKETS % 5 == 0
T = BUCKETS + BUCKETS % 2
GRAPH_EDGES = (125, 400)
ROUTER_EDGES = (128, 256)
RING = 16
QUAD = 4
QUADS = RING // QUAD
ROW = 260
HEADS = 4
EXPERTS = 4
HIDDEN = 512
SLICE_HEADS = 8
SLICE = 64
EPS = 1e-5
FAR = 1e30
NEAR = 60.0


def chunks_of(edges):
    need = -(-edges[0] * edges[1] // P) + BUCKETS
    return -(-need // RING) * RING


GRAPH_CHUNKS = chunks_of(GRAPH_EDGES)
ROUTER_CHUNKS = chunks_of(ROUTER_EDGES)
SIDE_STEPS = 10
SIDE_LEAD = 3
assert SIDE_STEPS * (GRAPH_CHUNKS // RING) >= ROUTER_EDGES[1]

ROWS = [("raw", D), ("sb1", D), ("sb2", D), ("b_slice", SLICE), ("temp", SLICE_HEADS), ("b_out", D),
        ("as0", D), ("ad0", D), ("gb0", D), ("gamma0", D), ("beta0", D), ("as1", D), ("ad1", D), ("gb1", D),
        ("ras", 16), ("rad", 16), ("rb", 16), ("lng", 16), ("lnb", 16), ("eb2", EXPERTS * D)]
ROW_AT = {}
for _name, _n in ROWS:
    ROW_AT[_name] = (sum(n for m, n in ROWS[:len(ROW_AT)]), _n)
ROWS_LEN = sum(n for _, n in ROWS)


class Count:

    def __init__(self, nc, name):
        self.sem, self.base = nc.alloc_semaphore(name), RING


class Steps:

    def __init__(self, eng, count):
        self.eng, self.count, self.at, self.n, self.per, self.parity = eng, count, count.base, 0, None, 0

    def did(self, ins):
        ins.then_inc(self.count.sem, 1)
        self.n += 1
        return self.n

    def wait(self, back=0):
        self.eng.wait_ge(self.count.sem, self.at + (self.n - back))

    def do(self, ins):
        self.did(ins)
        self.wait()

    def enter(self, turn, per, turns):
        self.at, self.after, self.per, self.n = self.at + self.n + turn * per, self.at + self.n + turns * per, per, 0

    def leave(self):
        assert self.n == self.per, (self.n, self.per)
        self.at, self.n = self.after, 0

    def end(self):
        self.count.base = self.at + self.n


def row(r, name):
    at, n = ROW_AT[name]
    return r[:, at:at + n]


def mid(ap, n):
    return ap.unsqueeze(1).broadcast_to([ap.shape[0], n, ap.shape[1]])


def last(ap, n):
    return ap.unsqueeze(2).broadcast_to([ap.shape[0], ap.shape[1], n])


def constants(nc, c):
    with nc.Block() as block:
        @block.gpsimd
        def _(pool):
            g = Steps(pool, c.pool_step)
            g.did(nc.gpsimd.iota(c.itmp[:, :], pattern=[[1, 512]], base=0, channel_multiplier=0))
            g.do(nc.gpsimd.iota(c.ptmp[:, :], pattern=[[1, 1]], base=0, channel_multiplier=1))
            g.did(nc.gpsimd.tensor_copy(c.iota[:, :], c.itmp[:, :]))
            g.did(nc.gpsimd.tensor_copy(c.iota16[:, :], c.itmp[:, :]))
            g.did(nc.gpsimd.tensor_copy(c.part[:, :], c.ptmp[:, :]))
            g.did(nc.gpsimd.memset(c.ones[:, :], 1.0))
            g.end()
            made = c.pool_step.base

        @block.vector
        def _(dve):
            v = Steps(dve, c.dve_step)
            dve.wait_ge(c.pool_step.sem, c.pool_step.base)
            v.did(nc.vector.tensor_scalar(c.ident[:, :], c.iota[:, 0:P], c.part[:, 0:1], None, ALU.is_equal))
            v.did(nc.vector.tensor_scalar(c.lower[:, :], c.iota[:, 0:P], c.part[:, 0:1], None, ALU.is_gt))
            v.did(nc.vector.tensor_scalar(c.pick[:, :, :], last(c.iota[0:HEADS, 0:HEADS], P), c.part[0:HEADS, 0:1],
                                          None, ALU.is_equal))
            v.did(nc.vector.memset(c.zero[:, :], 0.0))
            v.did(nc.vector.memset(c.zero16[:, :], 0.0))
            v.did(nc.vector.memset(c.valid[:, :], 1.0))
            v.wait()
            v.did(nc.vector.memset(c.valid[:, BUCKETS:T], 0.0))
            v.did(nc.vector.tensor_scalar(c.valid[:, BUCKETS - 1:BUCKETS], c.part[:, 0:1],
                                          float(NODES - (BUCKETS - 1) * P), None, ALU.is_lt))
            v.did(nc.vector.memset(c.eps[:, :], EPS))
            v.end()

        @block.scalar
        def _(act):
            a = Steps(act, c.act_step)
            act.wait_ge(c.pool_step.sem, c.pool_step.base)
            a.did(nc.scalar.activation(c.ptmp[:, :], c.part[:, :], ACT.Identity))
            a.end()


class Placing:
    SLOTS, SHARE = 10, 9

    def __init__(self, nc, c, edges, chunks, steps, tensors, lead=0):
        self.lead = lead
        self.nc, self.c, self.chunks, self.E, self.J, self.steps = nc, c, chunks, edges[0], edges[1], steps
        self.field, self.spot, self.where, self.left, self.right = tensors

    def begin(self, grid):
        c = self.c
        self.grid = grid
        self.placed_at, self.where_at, self.left_at, self.right_at = (s.base for s in (c.placed, c.located, c.fielded, c.chunked))


    def shared(self, i, per, n):
        return i * (per // self.SLOTS * self.SHARE) + (n // self.SLOTS * self.SHARE + n % self.SLOTS)

    def vector_step(self, dve, i, per, n):
        nc, c, j, u = self.nc, self.c, i * per + n, n % self.SLOTS
        dve.wait_ge(c.placed.sem, self.placed_at + j + (2 - self.SLOTS))
        if u < self.SHARE:
            nc.vector.tensor_scalar(self.where[:, u, :], c.iota16[0:self.E, 0:P], self.spot[:, 0, bass.ds(j, 1)], None,
                                    ALU.is_equal).then_inc(c.located.sem, 1)
        else:
            for half in range(2):
                nc.vector.tensor_scalar(self.left[:, u, half, :], c.iota16[0:self.E, 0:P], self.spot[:, 0, bass.ds(j, 1)],
                                        self.field[:, half, bass.ds(j, 1)], ALU.is_equal, ALU.mult)
        nc.vector.tensor_scalar(self.right[:, u, :], c.iota16[0:self.E, 0:self.chunks], self.spot[:, 1, bass.ds(j, 1)], None,
                                ALU.is_equal).then_inc(c.chunked.sem, 1)

    def scalar_step(self, act, i, per, n):
        j, u = i * per + n, n % self.SLOTS
        if u >= self.SHARE:
            return
        act.wait_ge(self.c.located.sem, self.where_at + self.shared(i, per, n) + 1)
        for half in range(2):
            ins = self.nc.scalar.activation(self.left[:, u, half, :], self.where[:, u, :], ACT.Identity,
                                            scale=self.field[:, half, bass.ds(j, 1)])
        ins.then_inc(self.c.fielded.sem, 1)

    def edge(self, first):
        zero = self.c.zero16
        for half in range(2):
            ins = self.nc.tensor.matmul(self.grid[:, half, 0:self.chunks], zero[0:self.E, :],
                                        zero[0:self.E, 0:1].broadcast_to([self.E, self.chunks]), start=first, stop=not first)
        ins.then_inc(self.c.placed.sem, 1)

    def tensor_step(self, pe, i, per, n):
        j, u = i * per + n, n % self.SLOTS
        pe.wait_ge(self.c.chunked.sem, self.right_at + j + 1)
        if u < self.SHARE:
            pe.wait_ge(self.c.fielded.sem, self.left_at + self.shared(i, per, n) + 1)
        for half in range(2):
            ins = self.nc.tensor.matmul(self.grid[:, half, 0:self.chunks], self.left[:, u, half, :], self.right[:, u, :],
                                        start=False, stop=False)
        ins.then_inc(self.c.placed.sem, 1)

    def finish(self, dve, v, gi, out):
        nv, chunks, grid = self.nc.vector, self.chunks, self.grid
        dve.wait_ge(self.c.placed.sem, self.placed_at + self.steps + 2)
        v.do(nv.tensor_copy(gi[:, 0:chunks], grid[:, 0, 0:chunks]))
        v.did(nv.memset(out.src[:, chunks:chunks + RING], 0))
        v.do(nv.tensor_scalar(out.src[:, 0:chunks], gi[:, 0:chunks], 8, None, ALU.arith_shift_right))
        v.do(nv.scalar_tensor_tensor(out.src[:, 0:chunks], grid[:, 1, 0:chunks], 8.0, out.src[:, 0:chunks], ALU.mult, ALU.add))
        v.do(nv.tensor_scalar(gi[:, 0:chunks], gi[:, 0:chunks], 255, None, ALU.bitwise_and))
        v.did(nv.memset(out.place[:, chunks:chunks + RING], -1.0))
        v.do(nv.tensor_scalar(out.place[:, 0:chunks], gi[:, 0:chunks], -1.0, None, ALU.add))

    def end(self):
        c = self.c
        c.placed.base = self.placed_at + self.steps + 2
        c.located.base, c.fielded.base = (at + self.shared(0, 0, self.steps + self.lead) for at in (self.where_at, self.left_at))
        c.chunked.base = self.right_at + self.steps + self.lead


@contextmanager
def placing_tensors(nc, name, edges, chunks, steps):
    E, n = edges[0], Placing.SLOTS
    with (
        nc.sbuf_tensor(f"{name}_field", [E, 2, steps], F32) as field, nc.sbuf_tensor(f"{name}_spot", [E, 2, steps], F32) as spot,
        nc.sbuf_tensor(f"{name}_where", [E, n, P], F16) as where, nc.sbuf_tensor(f"{name}_left", [E, n, 2, P], F16) as left,
        nc.sbuf_tensor(f"{name}_right", [E, n, chunks], F16) as right,
    ):
        yield field, spot, where, left, right


def find_slots(nc, c, dst, src, placing, out, behind=()):
    E, J, chunks, field, spot = placing.E, placing.J, placing.chunks, placing.field, placing.spot
    with (
        nc.sbuf_tensor(f"dst_{chunks}", [E, J], I32) as di, nc.sbuf_tensor(f"src_{chunks}", [E, J], I32) as si,
        nc.sbuf_tensor(f"hi_{chunks}", [E, J], F32) as hi,
        nc.sbuf_tensor(f"slot_{chunks}", [E, J], F32) as slot, nc.sbuf_tensor(f"ti_{chunks}", [E, J], I32) as ti,
        nc.sbuf_tensor(f"tj_{chunks}", [E, J], I32) as tj,
        nc.sbuf_tensor(f"oh_{chunks}", [E, BUCKETS * J], F32) as oh, nc.sbuf_tensor(f"pre_{chunks}", [E, BUCKETS * J], F32) as pre,
        nc.sbuf_tensor(f"tot_{chunks}", [P, 8, 32], F32) as tot, nc.sbuf_tensor(f"toti_{chunks}", [P, 32], I32) as toti,
        nc.sbuf_tensor(f"begun_{chunks}", [BUCKETS, chunks], F32) as begun,
        nc.psum_tensor(f"ahead_{chunks}", [1, 512], F32) as ahead, nc.psum_tensor(f"base_{chunks}", [P, 64], F32) as basep,
        nc.Block() as block,
    ):
        counts_at, prefix_at, loaded_at = c.totals.base + 1, c.prefixes.base + 1, c.loaded.base + 32

        @block.sync
        def _(sp):
            sp.dma_start(di[:, :], dst).then_inc(c.loaded.sem, 16)
            sp.dma_start(si[:, :], src).then_inc(c.loaded.sem, 16)
            for to, what in behind:
                sp.dma_start(to, what).then_inc(c.opened, 16)
            sp.wait_ge(c.loaded.sem, loaded_at)

        @block.vector
        def _(dve):
            v = Steps(dve, c.dve_step)
            nv = nc.vector
            v.did(nv.memset(tot[:, :, :], 0.0))
            v.did(nv.memset(field[:, :, :], 0.0))
            v.did(nv.memset(spot[:, :, :], 0.0))
            v.wait()
            dve.wait_ge(c.loaded.sem, loaded_at)
            v.did(nv.tensor_scalar(ti[:, :], di[:, :], 7, None, ALU.arith_shift_right))
            v.do(nv.tensor_scalar(tj[:, :], di[:, :], P - 1, None, ALU.bitwise_and))
            v.did(nv.tensor_copy(hi[:, :], ti[:, :]))
            v.do(nv.tensor_scalar(field[:, 0, 0:J], tj[:, :], 1.0, None, ALU.add))
            v.did(nv.tensor_scalar(tj[:, :], si[:, :], 7, None, ALU.bitwise_and))
            v.do(nv.tensor_scalar(ti[:, :], si[:, :], 3, None, ALU.arith_shift_right))
            v.did(nv.tensor_copy(field[:, 1, 0:J], ti[:, :]))
            v.do(nv.scalar_tensor_tensor(field[:, 0, 0:J], tj[:, :], 256.0, field[:, 0, 0:J], ALU.mult, ALU.add))
            oh3, pre3 = (x[:, :].rearrange("p (b j) -> p b j", b=BUCKETS) for x in (oh, pre))
            v.do(nv.tensor_tensor(oh3, mid(hi[:, :], BUCKETS), last(c.iota[0:E, 0:BUCKETS], J), ALU.is_equal))
            v.do(nv.tensor_tensor_scan(pre[:, :], oh[:, :], c.zero[0:E, 0:1].broadcast_to([E, BUCKETS * J]), 0.0, ALU.add, ALU.add))
            v.do(nv.tensor_copy(tot[0:E, 0, 1:BUCKETS + 1], pre3[:, :, J - 1]))
            nv.tensor_tensor(tot[0:E, 1, 0:BUCKETS], tot[0:E, 0, 1:BUCKETS + 1], tot[0:E, 0, 0:BUCKETS],
                             ALU.subtract).then_inc(c.totals.sem, 1)
            dve.wait_ge(c.prefixes.sem, prefix_at)
            v.do(nv.tensor_scalar(tot[:, 2, 0:BUCKETS], basep[:, 32:32 + BUCKETS], float(P - 1), None, ALU.add))
            v.do(nv.tensor_copy(toti[:, 0:BUCKETS], tot[:, 2, 0:BUCKETS]))
            v.do(nv.tensor_scalar(toti[:, 0:BUCKETS], toti[:, 0:BUCKETS], 7, None, ALU.arith_shift_right))
            v.do(nv.tensor_copy(tot[:, 3, 0:BUCKETS], toti[:, 0:BUCKETS]))
            v.do(nv.tensor_tensor_scan(tot[:, 4, 0:BUCKETS], tot[:, 3, 0:BUCKETS], tot[:, 7, 0:BUCKETS], 0.0, ALU.add, ALU.add))
            v.do(nv.tensor_tensor(tot[:, 5, 0:BUCKETS], tot[:, 4, 0:BUCKETS], tot[:, 3, 0:BUCKETS], ALU.subtract))
            v.do(nv.scalar_tensor_tensor(tot[:, 6, 0:BUCKETS], tot[:, 5, 0:BUCKETS], float(P), basep[:, 0:BUCKETS],
                                         ALU.mult, ALU.add))
            v.do(nv.tensor_tensor(tot[0:E, 6, 0:BUCKETS], tot[0:E, 6, 0:BUCKETS], tot[0:E, 0, 0:BUCKETS], ALU.subtract))
            v.do(nv.tensor_scalar(tot[0:E, 6, 0:BUCKETS], tot[0:E, 6, 0:BUCKETS], -1.0, None, ALU.add))
            with dve.Fori(0, BUCKETS // 5) as i:
                v.enter(i, 5, BUCKETS // 5)
                for u in range(5):
                    b = bass.ds((i * 5 + u) * J, J)
                    v.did(nv.scalar_tensor_tensor(oh[:, b], pre[:, b], tot[0:E, 6, bass.ds(i * 5 + u, 1)], oh[:, b], ALU.add, ALU.mult))
                v.leave()
            v.wait()
            v.do(nv.tensor_reduce(slot[:, :], oh[:, :].rearrange("p (b j) -> p j b", b=BUCKETS), AX.X, ALU.add))
            v.do(nv.tensor_copy(ti[:, :], slot[:, :]))
            v.do(nv.tensor_scalar(tj[:, :], ti[:, :], P - 1, None, ALU.bitwise_and))
            v.did(nv.tensor_copy(spot[:, 0, 0:J], tj[:, :]))
            v.do(nv.tensor_scalar(ti[:, :], ti[:, :], 7, None, ALU.arith_shift_right))
            v.did(nv.tensor_copy(spot[:, 1, 0:J], ti[:, :]))
            v.do(nv.tensor_tensor(tot[0:BUCKETS, 0, 0:BUCKETS], tot[0:BUCKETS, 5, 0:BUCKETS], c.ident[0:BUCKETS, 0:BUCKETS], ALU.mult))
            v.do(nv.tensor_reduce(tot[0:BUCKETS, 1, 0:1], tot[0:BUCKETS, 0, 0:BUCKETS], AX.X, ALU.add))
            nv.tensor_scalar(begun[:, :], c.iota[0:BUCKETS, 0:chunks], tot[0:BUCKETS, 1, 0:1], None, ALU.is_ge).then_inc(c.totals.sem, 1)
            v.did(nv.memset(out.tile[:, 0:QUAD], 0))
            v.did(nv.memset(out.tile[:, QUAD + chunks:], 0))
            dve.wait_ge(c.prefixes.sem, prefix_at + 1)
            v.did(nv.tensor_scalar(out.tile[:, QUAD:QUAD + chunks], ahead[:, 0:chunks], -1.0, None, ALU.add))
            v.end()

        @block.tensor
        def _(pe):
            pe.wait_ge(c.totals.sem, counts_at)
            nc.tensor.matmul(basep[:, 0:BUCKETS], c.lower[0:E, :], tot[0:E, 1, 0:BUCKETS], start=True, stop=True)
            nc.tensor.matmul(basep[:, 32:32 + BUCKETS], c.ones[0:E, :], tot[0:E, 1, 0:BUCKETS], start=True,
                             stop=True).then_inc(c.prefixes.sem, 1)
            pe.wait_ge(c.totals.sem, counts_at + 1)
            nc.tensor.matmul(ahead[:, 0:chunks], c.ones[0:BUCKETS, 0:1], begun[:, :], start=True, stop=True).then_inc(c.prefixes.sem, 1)

        c.loaded.base, c.totals.base, c.prefixes.base = loaded_at, counts_at + 1, prefix_at + 1


def place_edges(nc, c, placing, out):
    with (
        nc.sbuf_tensor("gi", [P, placing.chunks], I32) as gi, nc.psum_tensor("grid", [P, 2, 512], F32) as grid, nc.Block() as block,
    ):
        placing.begin(grid)
        n = placing.SLOTS
        groups = placing.steps // n

        @block.vector
        def _(dve):
            v = Steps(dve, c.dve_step)
            dve.wait_ge(c.opened, 16 * 5)
            with dve.Fori(0, T) as i:
                v.enter(i, 1, T)
                for u in range(n):
                    placing.vector_step(dve, i, n, u)
                v.did(tile_stats(nc, c, i))
                v.leave()
            with dve.Fori(T, groups) as i:
                for u in range(n):
                    placing.vector_step(dve, i, n, u)
            placing.finish(dve, v, gi, out)
            v.end()

        @block.scalar
        def _(act):
            with act.Fori(0, groups) as i:
                for u in range(n):
                    placing.scalar_step(act, i, n, u)

        @block.tensor
        def _(pe):
            placing.edge(True)
            with pe.Fori(0, groups) as i:
                for u in range(n):
                    placing.tensor_step(pe, i, n, u)
            placing.edge(False)

        placing.end()


def tile_stats(nc, c, t):
    return nc.vector.bn_stats(flat(c.bn[:, bass.ds(t, 1), :]), flat(c.x[:, bass.ds(t, 1), :]))


def layer_stats(nc, c):
    bn = c.bn
    with nc.Block() as block:
        mean, rstd = c.stat[:, :, 0], c.stat[:, :, 1]

        @block.vector
        def _(dve):
            v = Steps(dve, c.dve_step)
            nv = nc.vector
            v.did(nv.tensor_tensor(mean, bn[:, :, 1], bn[:, :, 4], ALU.add))
            v.do(nv.tensor_tensor(rstd, bn[:, :, 1], bn[:, :, 4], ALU.subtract))
            v.do(nv.tensor_tensor(rstd, rstd, rstd, ALU.mult))
            v.did(nv.tensor_scalar(mean, mean, 0.5, None, ALU.mult))
            v.do(nv.tensor_scalar(rstd, rstd, 0.25, None, ALU.mult))
            v.do(nv.scalar_tensor_tensor(rstd, bn[:, :, 2], 1.0 / D, rstd, ALU.mult, ALU.add))
            v.did(nv.scalar_tensor_tensor(rstd, bn[:, :, 5], 1.0 / D, rstd, ALU.mult, ALU.add))
            dve.wait_ge(c.act_step.sem, c.act_step.base + 1)
            v.did(nv.reciprocal(rstd, rstd))
            v.end()

        @block.scalar
        def _(act):
            a = Steps(act, c.act_step)
            act.wait_ge(c.dve_step.sem, c.dve_step.base - 1)
            a.did(nc.scalar.activation(rstd, rstd, ACT.Sqrt, bias=c.eps[:, 0:1]))
            a.end()


def weighted_rows(nc, c):
    ready_at, scaled_at, stored_at = c.ready.base, c.scaled.base, c.stored.base
    with nc.sbuf_tensor("w_soft", [P, D], F32) as w, nc.sbuf_tensor("w_m", [P, 4], F32) as m, nc.Block() as block:
        @block.vector
        def _(dve):
            v = Steps(dve, c.dve_step)
            nv = nc.vector
            v.do(nv.tensor_reduce(m[:, 0:1], row(c.rows, "raw"), AX.X, ALU.max))
            v.did(nv.tensor_scalar(m[:, 1:2], m[:, 0:1], -1.0, None, ALU.mult))
            negated = v.at + v.n
            v.do(nv.memset(c.table[:, :, D:ROW], 0.0))
            v.did(nv.memset(c.table[:, :, D:D + 1], 1.0))
            dve.wait_ge(c.act_step.sem, c.act_step.base + 1)
            v.do(nv.reciprocal(m[:, 3:4], m[:, 2:3]))
            v.do(nv.tensor_scalar(w[:, :], w[:, :], m[:, 3:4], None, ALU.mult))
            with dve.Fori(0, T // 2) as i:
                for u in range(2):
                    t = bass.ds(i * 2 + u, 1)
                    nv.scalar_tensor_tensor(flat(c.table[:, t, 0:D]), flat(c.x[:, t, :]), c.stat[:, t, 0], w[:, :], ALU.subtract,
                                            ALU.mult).then_inc(c.ready.sem, 1)
            v.end()
            c.negated = negated

        @block.scalar
        def _(act):
            a = Steps(act, c.act_step)
            act.wait_ge(c.dve_step.sem, c.negated)
            a.did(nc.scalar.activation(w[:, :], row(c.rows, "raw"), ACT.Exp, bias=m[:, 1:2], accum_out=m[:, 2:3]))
            a.end()
            with act.Fori(0, T // 2) as i:
                for u in range(2):
                    act.wait_ge(c.ready.sem, ready_at + i * 2 + u + 1)
                    rows = flat(c.table[:, bass.ds(i * 2 + u, 1), 0:D])
                    nc.scalar.activation(rows, rows, ACT.Identity, scale=c.stat[:, bass.ds(i * 2 + u, 1), 1]).then_inc(c.scaled.sem, 1)

        @block.sync
        def _(sp):
            with sp.Fori(0, T // 2) as i:
                sp.wait_ge(c.scaled.sem, scaled_at + i * 2 + 2)
                sp.dma_start(c.dram.rearrange("(t p) f -> p t f", p=P)[:, bass.ds(i * 2, 2), :],
                             c.table[:, bass.ds(i * 2, 2), :]).then_inc(c.stored.sem, 16)
            sp.wait_ge(c.stored.sem, stored_at + 16 * (T // 2))

        c.ready.base, c.scaled.base, c.stored.base = ready_at + T, scaled_at + T, stored_at + 16 * (T // 2)


def normalized(nc, c, out, t):
    return nc.vector.tensor_scalar(out, c.x[:, bass.ds(t, 1), :].rearrange("p t f -> p (t f)"),
                                   c.stat[:, bass.ds(t, 1), 0], c.stat[:, bass.ds(t, 1), 1], ALU.subtract, ALU.mult)


def dense(nc, c, halves, width, weights, prep, post, per_prep, per_post, store=None):
    n = c.fresh()
    turns = T // 2
    rows_at, flip_at, flat_at, prod_at, taken_at = (s.base for s in (c.rows_in, c.flipped, c.feature_major, c.product, c.taken))
    with (
        nc.sbuf_tensor(f"rows{n}", [P, 2, halves * P], F32) as a, nc.sbuf_tensor(f"rowsT{n}", [P, 2, halves, P], F32) as at,
        nc.psum_tensor(f"flip{n}", [P, 2, 512], F32) as flip, nc.psum_tensor(f"prod{n}", [P, 2, 512], F32) as prod,
        nc.Block() as block,
    ):
        @block.vector
        def _(dve):
            v = Steps(dve, c.dve_step)

            def prepare(i):
                for u in range(2):
                    dve.wait_ge(c.flipped.sem, flip_at + i * 2 + (u - 1))
                    prep(v, i * 2 + u, a[:, u, :]).then_inc(c.rows_in.sem, 1)

            def finish(i):
                for u in range(2):
                    dve.wait_ge(c.product.sem, prod_at + i * 2 + u + 1)
                    post(v, i * 2 + u, prod[:, u, 0:width]).then_inc(c.taken.sem, 1)

            prepare(0)
            prepare(1)
            with dve.Fori(0, turns - 2) as i:
                v.enter(i, 2 * (per_prep + per_post), turns - 2)
                prepare(i + 2)
                finish(i)
                v.leave()
            finish(turns - 2)
            finish(turns - 1)
            v.end()

        @block.tensor
        def _(pe):
            def turn(i):
                for u in range(2):
                    pe.wait_ge(c.rows_in.sem, rows_at + i * 2 + u + 1)
                    pe.wait_ge(c.feature_major.sem, flat_at + i * 2 + (u - 1))
                    for h in range(halves):
                        ins = nc.tensor.transpose(flip[:, u, h * P:(h + 1) * P], a[:, u, h * P:(h + 1) * P], c.ident[:, :])
                    ins.then_inc(c.flipped.sem, 1)

            def multiply(i):
                for u in range(2):
                    pe.wait_ge(c.feature_major.sem, flat_at + i * 2 + u + 1)
                    pe.wait_ge(c.taken.sem, taken_at + i * 2 + (u - 1))
                    for h in range(halves):
                        ins = nc.tensor.matmul(prod[:, u, 0:width], at[:, u, h, :], weights(h), start=(h == 0), stop=(h == halves - 1))
                    ins.then_inc(c.product.sem, 1)

            turn(0)
            with pe.Fori(0, turns - 1) as i:
                turn(i + 1)
                multiply(i)
            multiply(turns - 1)

        @block.scalar
        def _(act):
            with act.Fori(0, turns) as i:
                for u in range(2):
                    act.wait_ge(c.flipped.sem, flip_at + i * 2 + u + 1)
                    act.wait_ge(c.product.sem, prod_at + i * 2 + (u - 1))
                    nc.scalar.copy(at[:, u, :, :].rearrange("p h n -> p (h n)"), flip[:, u, 0:halves * P]).then_inc(c.feature_major.sem, 1)

        if store:
            table, dram = store
            stored_at = c.stored.base

            @block.sync
            def _(sp):
                with sp.Fori(0, turns) as i:
                    sp.wait_ge(c.taken.sem, taken_at + i * 2 + 2)
                    sp.dma_start(dram.rearrange("(t p) f -> p t f", p=P)[:, bass.ds(i * 2, 2), :],
                                 table[:, bass.ds(i * 2, 2), :]).then_inc(c.stored.sem, 16)
                sp.wait_ge(c.stored.sem, stored_at + 16 * turns)
            c.stored.base += 16 * turns

        for s in (c.rows_in, c.flipped, c.feature_major, c.product, c.taken):
            s.base += T


def tiles_of(nc, engine, slots, first, n):
    _, tiles = nc.values_load_multi_w_load_instructions(
        slots.tile[0:1, bass.ds(first + QUAD, n)], engines=(engine,), min_val=0, max_val=BUCKETS - 1,
        skip_runtime_bounds_check_because="the placing makes them so")
    return tiles


def gather_sum(nc, c, table, width, heads, slots, chunks, acc, begin=None, side=None, side_out=None, own=None):
    n = c.fresh()
    W = width + HEADS
    C = width // heads if heads else 0
    turns, quads = chunks // RING, QUADS
    spread_out = heads > 1 and width == D
    scaled_at = c.scaled.base
    opening = QUAD if heads else 0
    index_at, gathered_at, onehot_at = c.indexed.base, c.gather_base, c.onehots.base
    summed_at, added_at, ready_at, weighted_at = c.summed.base + opening, c.added.base + opening, c.ready.base, c.weighted.base
    flip_at, flat_at, looked_at, expo_at = (s.base for s in (c.flipped, c.feature_major, c.looked, c.expo))
    with (
        nc.sbuf_tensor(f"g{n}", [P, RING, W], F32) as g, nc.sbuf_tensor(f"oh{n}", [P, RING, P], F32) as oh,
        nc.sbuf_tensor(f"idx{n}", [P, RING], I32) as idx, nc.sbuf_tensor(f"ohT{n}", [P, 2, QUAD, P], F32) as oht,
        nc.sbuf_tensor(f"e{n}", [P, QUADS, QUAD, HEADS], F32) as e, nc.sbuf_tensor(f"e2{n}", [P, QUADS, QUAD, HEADS], F32) as e2,
        nc.psum_tensor(f"sum{n}", [P, 4, 512], F32) as total,
        nc.psum_tensor(f"flip{n}", [P, 2, QUAD, P], F32) as flip,
        nc.psum_tensor(f"look{n}", [P, 2, 64, 2 * HEADS], F32) as look, nc.sbuf_tensor(f"gi{n}", [P, ROUTER_CHUNKS], I32) as gi,
        nc.Block() as block,
    ):
        if side:
            side.begin(flip[:, :, :, :].rearrange("p b q n -> p b (q n)"))

        if own:
            own.begin(look[:, :, :, :].rearrange("p b q n -> p b (q n)"))
        own_step = own.step if own else lambda part, eng, i, u: None

        def side_step(step, eng, i, u, lead=SIDE_LEAD):
            for m in range(SIDE_STEPS if side else 0):
                if m * RING // SIDE_STEPS == u:
                    step(eng, i, SIDE_STEPS, m + lead)

        @block.gpsimd
        def _(pool):
            freed = pool.alloc_register(f"freed{n}")
            pool.reg_mov(freed, summed_at + 1 - RING)
            with pool.Fori(0, turns) as i:
                for u in range(RING):
                    pool.wait_ge(c.indexed.sem, index_at + i * RING + (u + 1))
                    pool.wait_ge(c.summed.sem, freed)
                    pool.reg_add(freed, freed, 1)
                    nc.gpsimd.indirect_dma_start(
                        out=g[:, u, :], out_offset=None, in_=table,
                        in_offset=bass.IndirectOffsetOnAxis(ap=idx[:, u:u + 1], axis=0)).then_inc(c.gathered[u], 16)

        @block.vector
        def _(dve):
            nv = nc.vector
            v = Steps(dve, c.dve_step)

            def onehot(k, u):
                nv.tensor_scalar(oh[:, u, :], c.iota[:, 0:P], slots.place[:, bass.ds(k, 1)], None,
                                 ALU.is_equal).then_inc(c.onehots.sem, 1)

            def add(k, u, tile):
                dve.wait_ge(c.summed.sem, summed_at + k + 1)
                dve.wait_ge(c.added.sem, added_at + k)
                at = flat(acc[:, bass.ds(tile, 1), :])
                nv.tensor_tensor(at, at, total[:, u, 0:W], ALU.add).then_inc(c.added.sem, 1)

            for j in range(SIDE_LEAD if side else 0):
                side.vector_step(dve, 0, 0, j)
            for u in range(RING - opening):
                onehot(u, u)
            if heads:
                begin[0](dve, v)
            else:
                v.did(nv.memset(acc[:, :, :], 0.0))
            v.wait()
            with dve.Fori(0, turns) as i:
                v.enter(i, 2 * QUADS if heads else 0, turns)
                tiles = tiles_of(nc, mybir.EngineType.DVE, slots, i * RING - opening, RING)
                for q in range(quads):
                    us = range(QUAD * q, QUAD * q + QUAD)
                    k0 = i * RING + (QUAD * q - opening)

                    def add_up(u):
                        add(k0 + u, u, tiles[QUAD * q + u])

                    def renew(u):
                        onehot(k0 + (u + RING), (QUAD * q + u - opening) % RING)

                    if heads:
                        for u in us:
                            dve.wait_ge(c.gathered[u], gathered_at + i * 16 + 16)
                        dve.wait_ge(c.looked.sem, looked_at + i * quads + (q + 1))
                        es = g[:, QUAD * q:QUAD * q + QUAD, width:width + heads]
                        v.did(nv.tensor_tensor(e2[:, q, :, 0:heads], es, look[:, q % 2, 0:QUAD, 0:heads], ALU.add))
                        add_up(0)
                        v.wait()
                        v.did(nv.scalar_tensor_tensor(e2[:, q, :, 0:heads], e2[:, q, :, 0:heads], 0.2, e2[:, q, :, 0:heads], ALU.mult, ALU.max))
                        renew(0)
                        v.wait()
                        nv.tensor_tensor(e[:, q, :, 0:heads], e2[:, q, :, 0:heads], look[:, q % 2, 0:QUAD, HEADS:HEADS + heads],
                                         ALU.subtract).then_inc(c.ready.sem, 1)
                        for u in range(1, QUAD):
                            add_up(u)
                            renew(u)
                    else:
                        for u in range(QUAD):
                            add_up(u)
                            renew(u)
                            side_step(side and side.vector_step, dve, i, QUAD * q + u)
                            own_step("vector", dve, i, QUAD * q + u)
                    if heads:
                        dve.wait_ge(c.expo.sem, expo_at + i * quads + (q + 1))
                        for u in us[0:QUAD - 1] if spread_out else us:
                            if heads > 1:
                                gv = g[:, u, 0:width].rearrange("p (h c) -> p h c", h=heads)
                                nv.tensor_tensor(gv, gv, last(g[:, u, width:width + heads], C), ALU.mult).then_inc(c.weighted.sem, 1)
                            else:
                                nv.tensor_scalar(oh[:, u, :], oh[:, u, :], e[:, q, u % QUAD, 0:1], None, ALU.mult).then_inc(c.weighted.sem, 1)
                v.leave()
            if heads:
                tiles = tiles_of(nc, mybir.EngineType.DVE, slots, chunks - QUAD, QUAD)
                for u in range(QUAD):
                    add(chunks - QUAD + u, u, tiles[u])
            if side:
                side.finish(dve, v, gi, side_out)
            v.end()

        @block.scalar
        def _(act):
            def turned(i, q):
                act.wait_ge(c.flipped.sem, flip_at + i * quads + (q + 1))
                act.wait_ge(c.looked.sem, looked_at + i * quads + (q - 1))
                nc.scalar.copy(oht[:, q % 2, :, :], flip[:, q % 2, :, :]).then_inc(c.feature_major.sem, 1)

            for j in range(SIDE_LEAD if side else 0):
                side.scalar_step(act, 0, 0, j)
            for u in range(RING):
                nc.scalar.copy(idx[:, u:u + 1], slots.src[:, u:u + 1]).then_inc(c.indexed.sem, 1)
            if heads:
                begin[1](act)
                turned(0, 0)
                turned(0, 1)
            with act.Fori(0, turns) as i:
                for q in range(quads):
                    if heads:
                        act.wait_ge(c.ready.sem, ready_at + i * quads + (q + 1))
                        p = g[:, QUAD * q:QUAD * q + QUAD, width:width + heads] if heads > 1 else e[:, q, :, 0:1]
                        nc.scalar.activation(p, e[:, q, :, 0:heads], ACT.Exp).then_inc(c.expo.sem, 1)
                        if spread_out:
                            act.wait_ge(c.expo.sem, expo_at + i * quads + (q + 1))
                            u = QUAD * q + QUAD - 1
                            for h in range(heads):
                                ins = nc.scalar.activation(g[:, u, h * C:(h + 1) * C], g[:, u, h * C:(h + 1) * C], ACT.Identity,
                                                           scale=g[:, u, width + h:width + h + 1])
                            ins.then_inc(c.scaled.sem, 1)
                        turned(i, q + 2)
                    for u in range(QUAD * q, QUAD * q + QUAD):
                        act.wait_ge(c.gathered[u], gathered_at + i * 16 + 16)
                        nc.scalar.copy(idx[:, u:u + 1], slots.src[:, bass.ds(i * RING + (u + RING), 1)]).then_inc(c.indexed.sem, 1)
                        side_step(side and side.scalar_step, act, i, u)
                        own_step("scalar", act, i, u)

        @block.tensor
        def _(pe):
            def turn(i, q):
                for u in range(QUAD * q, QUAD * q + QUAD):
                    pe.wait_ge(c.onehots.sem, onehot_at + i * RING + (u + 1))
                pe.wait_ge(c.feature_major.sem, flat_at + i * quads + (q - 1))
                for u in range(QUAD):
                    ins = nc.tensor.transpose(flip[:, q % 2, u, :], oh[:, (QUAD * q + u) % RING, :], c.ident[:, :])
                ins.then_inc(c.flipped.sem, 1)

            def look_up(i, q, tiles):
                pe.wait_ge(c.feature_major.sem, flat_at + i * quads + (q + 1))
                pe.wait_ge(c.ready.sem, ready_at + i * quads + (q - 1))
                for u in range(QUAD):
                    ins = nc.tensor.matmul(look[:, q % 2, u, :], oht[:, q % 2, u, :],
                                           c.edm[:, bass.ds(tiles[u] * (2 * HEADS), 2 * HEADS)], start=True, stop=True)
                ins.then_inc(c.looked.sem, 1)

            if heads:
                turn(0, 0)
                turn(0, 1)
                pe.wait_ge(c.dve_step.sem, c.edm_ready)
                look_up(0, 0, tiles_of(nc, mybir.EngineType.PE, slots, 0, QUAD))
                for u in range(QUAD):
                    nc.tensor.matmul(total[:, u, 0:W], c.zero[:, :], c.zero[:, 0:1].broadcast_to([P, W]),
                                     start=True, stop=True).then_inc(c.summed.sem, 1)
            if side:
                side.edge(True)
            with pe.Fori(0, turns) as i:
                if heads:
                    tiles = tiles_of(nc, mybir.EngineType.PE, slots, i * RING + QUAD, RING)
                for q in range(quads):
                    if heads:
                        look_up(i, q + 1, tiles[QUAD * q:])
                        turn(i, q + 2)
                    for u in range(QUAD * q, QUAD * q + QUAD):
                        if spread_out and u % QUAD == QUAD - 1:
                            pe.wait_ge(c.scaled.sem, scaled_at + i * quads + (q + 1))
                        elif spread_out:
                            pe.wait_ge(c.weighted.sem, weighted_at + (i * quads + q) * (QUAD - 1) + (u % QUAD + 1))
                        elif heads:
                            pe.wait_ge(c.weighted.sem, weighted_at + i * RING + (u + 1))
                        else:
                            pe.wait_ge(c.onehots.sem, onehot_at + i * RING + (u + 1))
                            pe.wait_ge(c.gathered[u], gathered_at + i * 16 + 16)
                        pe.wait_ge(c.added.sem, added_at + i * RING + (u + 1 - 4))
                        nc.tensor.matmul(total[:, u % 4, 0:W], oh[:, u, :], g[:, u, :], start=True, stop=True).then_inc(c.summed.sem, 1)
                        side_step(side and side.tensor_step, pe, i, u, lead=0)
                        own_step("tensor", pe, i, u)
            if side:
                side.edge(False)
                side.end()

    if own:
        own.end()
    c.gather_base += 16 * turns
    c.indexed.base += chunks + RING
    c.onehots.base += chunks + RING - opening
    c.summed.base += chunks + opening
    c.added.base += chunks + opening
    if heads:
        for s in (c.flipped, c.feature_major):
            s.base += quads * turns + 2
        c.looked.base += quads * turns + 1
        if spread_out:
            c.scaled.base += quads * turns
        c.weighted.base += quads * turns * (QUAD - 1) if spread_out else chunks
        c.ready.base += quads * turns
        c.expo.base += quads * turns


def spread_guard(nc, c, table, width, heads, flag):
    with (
        nc.sbuf_tensor(f"ends{c.fresh()}", [P, 2 * HEADS], F32) as ends, nc.sbuf_tensor(f"end{c.fresh()}", [2 * HEADS, 1], F32) as end,
        nc.sbuf_tensor(f"diag{c.fresh()}", [2 * HEADS, 2 * HEADS], F32) as diag, nc.sbuf_tensor(f"far{c.fresh()}", [P, 2 * HEADS + 1], F32) as far,
        nc.psum_tensor(f"endsT{c.fresh()}", [2 * HEADS, P], F32) as endst, nc.psum_tensor(f"endall{c.fresh()}", [P, 2 * HEADS], F32) as endall,
        nc.Block() as block,
    ):
        @block.vector
        def _(dve):
            v = Steps(dve, c.dve_step)
            nv = nc.vector
            es = table[:, :, width:width + heads].rearrange("p t h -> p h t")
            v.do(nv.memset(ends[:, :], 0.0))
            v.did(nv.tensor_reduce(ends[:, 0:heads], es, AX.X, ALU.max))
            v.do(nv.tensor_reduce(ends[:, HEADS:HEADS + heads], es, AX.X, ALU.min))
            v.did(nv.tensor_scalar(ends[:, HEADS:HEADS + heads], ends[:, HEADS:HEADS + heads], -1.0, None, ALU.mult))
            c.ends_in = v.at + v.n
            dve.wait_ge(c.product.sem, c.product.base + 1)
            v.do(nv.tensor_reduce(end[:, :], endst[:, :], AX.X, ALU.max))
            v.did(nv.tensor_scalar(diag[:, :], c.ident[0:2 * HEADS, 0:2 * HEADS], end[:, 0:1], None, ALU.mult))
            c.diagonal = v.at + v.n
            dve.wait_ge(c.product.sem, c.product.base + 2)
            v.do(nv.tensor_copy(far[:, 0:2 * HEADS], endall[:, :]))
            v.did(nv.tensor_copy(c.top[:, :, :], mid(far[:, 0:HEADS], T)))
            v.do(nv.tensor_tensor(far[:, HEADS:2 * HEADS], far[:, 0:HEADS], far[:, HEADS:2 * HEADS], ALU.add))
            v.do(nv.tensor_reduce(far[:, 2 * HEADS:], far[:, HEADS:2 * HEADS], AX.X, ALU.max))
            v.did(nv.tensor_scalar(flag[:, :], far[0:1, 2 * HEADS:], NEAR, None, ALU.is_gt))
            v.end()

        @block.tensor
        def _(pe):
            pe.wait_ge(c.dve_step.sem, c.ends_in)
            nc.tensor.transpose(endst[:, :], ends[:, :], c.ident[:, :]).then_inc(c.product.sem, 1)
            pe.wait_ge(c.dve_step.sem, c.diagonal)
            nc.tensor.matmul(endall[:, :], c.ones[0:2 * HEADS, :], diag[:, :], start=True, stop=True).then_inc(c.product.sem, 1)
            c.product.base += 2


def segment_max(nc, c, table, dram, width, heads, slots, chunks, flag):
    n = c.fresh()
    W = width + HEADS
    indexed, gathered, onehot, flipped, copied, spreads, topped, step = (
        nc.alloc_semaphore(f"max_{name}{n}") for name in ("indexed", "gathered", "onehot", "flipped", "copied", "spread", "topped", "step"))
    with (
        nc.sbuf_tensor(f"mg{n}", [P, W], F32) as g, nc.sbuf_tensor(f"moh{n}", [P, P], F32) as oh,
        nc.sbuf_tensor(f"midx{n}", [P, 1], I32) as idx, nc.sbuf_tensor(f"mesT{n}", [HEADS, P], F32) as est,
        nc.sbuf_tensor(f"mfar{n}", [P, P], F32) as far, nc.sbuf_tensor(f"mv{n}", [P, HEADS, P], F32) as val,
        nc.sbuf_tensor(f"mc{n}", [P, HEADS], F32) as cm,
        nc.psum_tensor(f"mflip{n}", [P, P], F32) as flip, nc.psum_tensor(f"mest{n}", [HEADS, P], F32) as estp,
        nc.psum_tensor(f"mspread{n}", [P, HEADS, P], F32) as spread, nc.Block() as block,
    ):
        @block.scalar
        def _(act):
            far_apart = act.value_load(flag[0:1, 0:1], min_val=0, max_val=1)
            with act.If(far_apart > 0):
                with act.Fori(0, chunks) as k:
                    act.wait_ge(topped, k + 1)
                    nc.scalar.copy(idx[:, :], slots.src[:, bass.ds(k, 1)]).then_inc(indexed, 1)
                    act.wait_ge(flipped, k + 1)
                    nc.scalar.copy(est[0:heads, :], estp[0:heads, :]).then_inc(copied, 1)

        @block.gpsimd
        def _(pool):
            far_apart = pool.value_load(flag[0:1, 0:1], min_val=0, max_val=1)
            with pool.If(far_apart > 0):
                asked = pool.alloc_register(f"asked{n}")
                pool.reg_mov(asked, 1)
                with pool.Fori(0, chunks) as k:
                    pool.wait_ge(indexed, asked)
                    pool.reg_add(asked, asked, 1)
                    nc.gpsimd.indirect_dma_start(out=g[:, :], out_offset=None, in_=dram,
                                                 in_offset=bass.IndirectOffsetOnAxis(ap=idx[:, 0:1], axis=0)).then_inc(gathered, 16)

        @block.tensor
        def _(pe):
            far_apart = pe.value_load(flag[0:1, 0:1], min_val=0, max_val=1)
            with pe.If(far_apart > 0):
                with pe.Fori(0, chunks) as k:
                    pe.wait_ge(onehot, k + 1)
                    nc.tensor.transpose(flip[:, :], oh[:, :], c.ident[:, :])
                    pe.wait_ge(gathered, k * 16 + 16)
                    nc.tensor.transpose(estp[0:heads, :], g[:, width:width + heads], c.ident[:, :]).then_inc(flipped, 1)
                    pe.wait_ge(copied, k + 1)
                    for h in range(heads):
                        ins = nc.tensor.matmul(spread[:, h, :], c.pick[0:heads, h, :], est[0:heads, :], start=True, stop=True)
                    ins.then_inc(spreads, 1)

        @block.vector
        def _(dve):
            nv = nc.vector
            far_apart = dve.value_load(flag[0:1, 0:1], min_val=0, max_val=1)
            with dve.If(far_apart > 0):
                nv.tensor_copy(c.top[:, :, 0:heads], table[:, :, width:width + heads]).then_inc(topped, 1)
                with dve.Fori(0, chunks) as k:
                    nv.tensor_scalar(oh[:, :], c.iota[:, 0:P], slots.place[:, bass.ds(k, 1)], None, ALU.is_equal).then_inc(onehot, 1)
                    t = dve.value_load(slots.tile[0:1, bass.ds(k + QUAD, 1)], min_val=0, max_val=BUCKETS - 1)
                    dve.wait_ge(flipped, k + 1)
                    nv.tensor_scalar(far[:, :], flip[:, :], -1.0, FAR, ALU.add, ALU.mult).then_inc(step, 1)
                    dve.wait_ge(step, k * 3 + 1)
                    dve.wait_ge(spreads, k + 1)
                    nv.tensor_tensor(val[:, 0:heads, :], spread[:, 0:heads, :], mid(far[:, :], heads), ALU.add).then_inc(step, 1)
                    dve.wait_ge(step, k * 3 + 2)
                    nv.tensor_reduce(cm[:, 0:heads], val[:, 0:heads, :], AX.X, ALU.max).then_inc(step, 1)
                    dve.wait_ge(step, k * 3 + 3)
                    dve.wait_ge(topped, k + 1)
                    at = c.top[:, bass.ds(t, 1), 0:heads].rearrange("p t h -> p (t h)")
                    nv.tensor_tensor(at, at, cm[:, 0:heads], ALU.max).then_inc(topped, 1)


def attend(nc, c, table, dram, width, heads, slots, chunks, acc):
    C = width // heads
    spread_guard(nc, c, table, width, heads, c.flag)
    segment_max(nc, c, table, dram, width, heads, slots, chunks, c.flag)
    edm = c.edm[:, :].rearrange("p (t k) -> p t k", t=T)
    with nc.sbuf_tensor(f"self{c.fresh()}", [P, T, 3 * HEADS], F32) as s:
        def begin(dve, v):
            nv = nc.vector
            es, a, b = table[:, :, width:width + heads], s[:, :, 0:heads], s[:, :, HEADS:HEADS + heads]
            ed, m = edm[:, :, 0:heads], edm[:, :, HEADS:HEADS + heads]
            v.did(nv.memset(c.edm[:, :], 0.0))
            v.did(nv.memset(acc[:, :, width:width + HEADS], 0.0))
            v.wait()
            v.did(nv.tensor_copy(ed, c.ed[:, :, 0:heads]))
            v.do(nv.tensor_tensor(b, c.top[:, :, 0:heads], c.ed[:, :, 0:heads], ALU.add))
            v.do(nv.scalar_tensor_tensor(m, b, 0.2, b, ALU.mult, ALU.max))
            c.edm_ready = v.at + v.n
            v.do(nv.tensor_tensor(a, es, ed, ALU.add))
            v.do(nv.scalar_tensor_tensor(a, a, 0.2, a, ALU.mult, ALU.max))
            v.did(nv.tensor_tensor(a, a, m, ALU.subtract))
            c.self_ready = v.at + v.n
            dve.wait_ge(c.act_step.sem, c.act_step.base + 1)
            for h in range(heads):
                v.did(nv.tensor_tensor(acc[:, :, h * C:(h + 1) * C], table[:, :, h * C:(h + 1) * C],
                                       s[:, :, 2 * HEADS + h].unsqueeze(2).broadcast_to([P, T, C]), ALU.mult))
            z = width if heads > 1 else width + 1
            v.did(nv.tensor_copy(acc[:, :, z:z + heads], s[:, :, 2 * HEADS:2 * HEADS + heads]))

        def exponentials(act):
            a = Steps(act, c.act_step)
            act.wait_ge(c.dve_step.sem, c.self_ready)
            a.did(nc.scalar.activation(s[:, :, 2 * HEADS:2 * HEADS + heads], s[:, :, 0:heads], ACT.Exp))
            a.end()

        gather_sum(nc, c, dram, width, heads, slots, chunks, acc, (begin, exponentials))


def load(nc, c, pairs, behind=(), fetched=None):
    with nc.Block() as block:
        @block.sync
        def _(sp):
            for dst, src in pairs:
                sp.dma_start(dst, src).then_inc(c.loaded.sem, 16)
                c.loaded.base += 16
            for dst, src in behind:
                sp.dma_start(dst, src).then_inc(fetched, 16)
            if pairs:
                sp.wait_ge(c.loaded.sem, c.loaded.base)


def flat(ap):
    return ap.rearrange("p t f -> p (t f)")


class OwnProducts:

    def __init__(self, nc, c, a, at, w, bias, out, residual):
        self.residual = residual
        self.nc, self.c, self.a, self.at, self.w, self.bias, self.out = nc, c, a, at, w, bias, out

    def begin(self, banks):
        c = self.c
        self.flip, self.prod = banks[:, 0, 0:D], banks[:, 1, 0:D]
        self.rows_at, self.flip_at, self.flat_at, self.prod_at, self.taken_at = (
            s.base for s in (c.rows_in, c.flipped, c.feature_major, c.product, c.taken))

    def step(self, part, eng, i, u):
        nc, c = self.nc, self.c
        if part == "scalar" and u == 1:
            eng.wait_ge(c.flipped.sem, self.flip_at + i)
            nc.scalar.copy(self.a[:, :], flat(c.table[:, bass.ds(i, 1), 0:D])).then_inc(c.rows_in.sem, 1)
        if part == "tensor" and u == 4:
            eng.wait_ge(c.rows_in.sem, self.rows_at + i + 1)
            eng.wait_ge(c.feature_major.sem, self.flat_at + i)
            for h in range(2):
                ins = nc.tensor.transpose(self.flip[:, h * P:(h + 1) * P], self.a[:, h * P:(h + 1) * P], c.ident[:, :])
            ins.then_inc(c.flipped.sem, 1)
        if part == "scalar" and u == 7:
            eng.wait_ge(c.flipped.sem, self.flip_at + i + 1)
            eng.wait_ge(c.product.sem, self.prod_at + i)
            nc.scalar.copy(self.at[:, :], self.flip).then_inc(c.feature_major.sem, 1)
        if part == "tensor" and u == 10:
            eng.wait_ge(c.feature_major.sem, self.flat_at + i + 1)
            eng.wait_ge(c.taken.sem, self.taken_at + i)
            for h in range(2):
                ins = nc.tensor.matmul(self.prod, self.at[:, h * P:(h + 1) * P], self.w[:, h, :], start=(h == 0), stop=(h == 1))
            ins.then_inc(c.product.sem, 1)
        if part == "vector" and u == 5 and self.residual:
            x = flat(c.x[:, bass.ds(i, 1), :])
            nc.vector.tensor_tensor(x, x, flat(c.table[:, bass.ds(i, 1), 0:D]), ALU.add)
        if part == "vector" and u == 13:
            eng.wait_ge(c.product.sem, self.prod_at + i + 1)
            nc.vector.tensor_tensor(flat(self.out[:, bass.ds(i, 1), :]), self.prod, self.bias, ALU.add).then_inc(c.taken.sem, 1)

    def end(self):
        c = self.c
        for s in (c.rows_in, c.flipped, c.feature_major, c.product, c.taken):
            s.base += T


def sage(nc, c, ins, k, slots, side=None, side_out=None):
    n = c.fresh()
    assert GRAPH_CHUNKS // RING == T
    with (
        nc.sbuf_tensor(f"sw{n}", [P, 4, D], F32) as w, nc.sbuf_tensor(f"rdeg{n}", [P, T], F32) as rdeg,
        nc.sbuf_tensor(f"so{n}", [P, 2, D], F32) as o, nc.sbuf_tensor(f"own{n}", [P, T, D], F32) as own,
        nc.sbuf_tensor(f"ownrows{n}", [P, D], F32) as a, nc.sbuf_tensor(f"ownrowsT{n}", [P, D], F32) as at,
    ):
        load(nc, c, [(flat(w[:, :, :]), ins[f"sage{k}"])])
        gather_sum(nc, c, c.dram, D, 0, slots, GRAPH_CHUNKS, c.acc, None, side, side_out,
                   OwnProducts(nc, c, a, at, w, row(c.rows, f"sb{k}"), own, k == 2))
        with nc.Block() as block:
            @block.vector
            def _(dve):
                v = Steps(dve, c.dve_step)
                v.do(nc.vector.tensor_scalar(rdeg[:, :], c.acc[:, :, D], 1.0, None, ALU.max))
                v.do(nc.vector.reciprocal(rdeg[:, :], rdeg[:, :]))
                v.end()

        def prep(v, t, a):
            return nc.vector.tensor_scalar(a, flat(c.acc[:, bass.ds(t, 1), 0:D]), rdeg[:, bass.ds(t, 1)], None, ALU.mult)

        def post(v, t, prod):
            u = v.parity
            v.parity ^= 1
            v.do(nc.vector.tensor_tensor(o[:, u, :], prod, flat(own[:, bass.ds(t, 1), :]), ALU.add))
            to = flat(c.table[:, bass.ds(t, 1), 0:D] if k == 1 else c.x[:, bass.ds(t, 1), :])
            ins = nc.vector.scalar_tensor_tensor(to, o[:, u, :], 0.0, to, ALU.max, ALU.add)
            if k == 1:
                return ins
            v.do(ins)
            return tile_stats(nc, c, t)

        if k == 2:
            views = slice_inputs(c)
            load(nc, c, [], [(views[name], ins[name]) for name, _, _ in SLICE_ROOM], c.slice_in)
        dense(nc, c, 2, D, lambda h: w[:, 2 + h, :], prep, post, 0, 1 if k == 1 else 2, (c.table, c.dram) if k == 1 else None)


def gat_rows(nc, c, w, width, heads, table, dram, from_elu=False):
    def prep(v, t, a):
        if from_elu:
            return nc.vector.scalar_tensor_tensor(a, flat(table[:, bass.ds(t, 1), 0:D]), -1.0, flat(c.acc[:, bass.ds(t, 1), 0:D]),
                                                  ALU.add, ALU.max)
        return normalized(nc, c, a, t)

    def post(v, t, prod):
        v.did(nc.vector.tensor_copy(flat(table[:, bass.ds(t, 1), 0:width + heads]), prod[:, 0:width + heads]))
        return nc.vector.tensor_copy(flat(c.ed[:, bass.ds(t, 1), 0:heads]), prod[:, width + heads:width + 2 * heads])

    dense(nc, c, 2, width + 2 * heads, lambda h: w[:, h, :], prep, post, 0, 1, (table, dram))


def fold(nc, c, w, width, heads, src, dst):
    C = width // heads
    with nc.sbuf_tensor(f"fold{c.fresh()}", [P, 2, width], F32) as f, nc.Block() as block:
        @block.vector
        def _(dve):
            v = Steps(dve, c.dve_step)
            for n, name in enumerate((src, dst)):
                v.do(nc.vector.tensor_tensor(f[:, :, :], w[:, :, 0:width], mid(row(c.rows, name), 2), ALU.mult))
                for k in range(2):
                    v.do(nc.vector.tensor_reduce(w[:, k, width + n * heads:width + (n + 1) * heads],
                                                 f[:, k, :].rearrange("p (h c) -> p h c", h=heads), AX.X, ALU.add))
            v.end()


def gat_layer(nc, c, ins, slots):
    layer_stats(nc, c)
    fold(nc, c, c.gw0, D, HEADS, "as0", "ad0")
    gat_rows(nc, c, c.gw0, D, HEADS, c.table, c.dram)
    attend(nc, c, c.table, c.dram, D, HEADS, slots, GRAPH_CHUNKS, c.acc)
    with (
        nc.sbuf_tensor("bnrow", [P, 4, D], F32) as r, nc.sbuf_tensor("held", [P, P], F32) as held,
        nc.psum_tensor("bnsum", [P, 2, 512], F32) as total, nc.Block() as block,
    ):
        groups = [(g * 5, T if g == 4 else g * 5 + 5) for g in range(5)]
        part = lambda x, g: x[:, groups[g][0]:groups[g][1], 0:D]
        wide = lambda ap, g: mid(ap, groups[g][1] - groups[g][0])
        biased, centred, squared, low = [], [], [], []

        @block.vector
        def _(dve):
            v = Steps(dve, c.dve_step)
            nv = nc.vector
            v.did(nv.tensor_copy(held[:, :], c.valid[:, BUCKETS - 1:BUCKETS].broadcast_to([P, P])))
            v.do(nv.reciprocal(c.acc[:, :, D:D + HEADS], c.acc[:, :, D:D + HEADS]))
            for h in range(HEADS):
                cols = c.acc[:, :, h * 64:(h + 1) * 64]
                v.did(nv.tensor_tensor(cols, cols, c.acc[:, :, D + h].unsqueeze(2).broadcast_to([P, T, 64]), ALU.mult))
            v.wait()
            for g in range(len(groups)):
                v.did(nv.tensor_tensor(part(c.acc, g), part(c.acc, g), wide(row(c.rows, "gb0"), g), ALU.add))
                biased.append(v.at + v.n)
            dve.wait_ge(c.product.sem, c.product.base + 1)
            v.do(nv.tensor_scalar(r[:, 0, :], total[:, 0, 0:D], 1.0 / NODES, None, ALU.mult))
            for g in range(len(groups)):
                v.did(nv.tensor_tensor(part(c.acc, g), part(c.acc, g), wide(r[:, 0, :], g), ALU.subtract))
                centred.append(v.at + v.n)
            dve.wait_ge(c.product.sem, c.product.base + 2)
            v.did(nv.tensor_scalar(r[:, 1, :], total[:, 1, 0:D], 1.0 / NODES, None, ALU.mult))
            c.variance = v.at + v.n
            dve.wait_ge(c.act_step.sem, c.act_step.base + len(groups) + 1)
            v.do(nv.reciprocal(r[:, 2, :], r[:, 2, :]))
            v.do(nv.tensor_tensor(r[:, 2, :], r[:, 2, :], row(c.rows, "gamma0"), ALU.mult))
            for g in range(len(groups)):
                v.do(nv.tensor_tensor(part(c.acc, g), part(c.acc, g), wide(r[:, 2, :], g), ALU.mult))
                v.do(nv.tensor_tensor(part(c.acc, g), part(c.acc, g), wide(row(c.rows, "beta0"), g), ALU.add))
                v.did(nv.tensor_scalar(part(c.table, g), part(c.acc, g), 0.0, None, ALU.min))
                low.append(v.at + v.n)
            v.end()

        @block.scalar
        def _(act):
            a = Steps(act, c.act_step)
            for g in range(len(groups)):
                act.wait_ge(c.dve_step.sem, centred[g])
                a.did(nc.scalar.activation(part(c.table, g), part(c.acc, g), ACT.Square))
                squared.append(a.at + a.n)
            act.wait_ge(c.dve_step.sem, c.variance)
            a.did(nc.scalar.activation(r[:, 2, :], r[:, 1, :], ACT.Sqrt, bias=c.eps[:, 0:1]))
            for g in range(len(groups)):
                act.wait_ge(c.dve_step.sem, low[g])
                a.did(nc.scalar.activation(part(c.table, g), part(c.table, g), ACT.Exp))
            a.end()

        @block.tensor
        def _(pe):
            for n, (sem, ready, what) in enumerate(((c.dve_step.sem, biased, c.acc), (c.act_step.sem, squared, c.table))):
                for g, (first, end) in enumerate(groups):
                    pe.wait_ge(sem, ready[g])
                    for t in range(first, min(end, BUCKETS)):
                        ins = nc.tensor.matmul(total[:, n, 0:D], held[:, :] if t == BUCKETS - 1 else c.ones[:, :], what[:, t, 0:D],
                                               start=(t == 0), stop=(t == BUCKETS - 1))
                ins.then_inc(c.product.sem, 1)
            c.product.base += 2

    fold(nc, c, c.gw1, D, 1, "as1", "ad1")
    with nc.Block() as block:
        @block.vector
        def _(dve):
            v = Steps(dve, c.dve_step)
            v.do(nc.vector.memset(c.table[:, :, D:ROW], 0.0))
            v.did(nc.vector.memset(c.table[:, :, D + 1:D + 2], 1.0))
            v.end()
    gat_rows(nc, c, c.gw1, D, 1, c.table, c.dram, from_elu=True)
    attend(nc, c, c.table, c.dram, D, 1, slots, GRAPH_CHUNKS, c.acc)
    with nc.sbuf_tensor("nrm", [P, T, 2], F32) as nrm, nc.Block() as block:
        h_at = c.ready.base

        @block.vector
        def _(dve):
            v = Steps(dve, c.dve_step)
            nv = nc.vector
            v.do(nv.reciprocal(nrm[:, :, 0], c.acc[:, :, D + 1]))
            with dve.Fori(0, T // 2) as i:
                for u in range(2):
                    h = flat(c.acc[:, bass.ds(i * 2 + u, 1), 0:D])
                    nv.scalar_tensor_tensor(h, h, nrm[:, bass.ds(i * 2 + u, 1), 0], row(c.rows, "gb1"), ALU.mult, ALU.add).then_inc(c.ready.sem, 1)
            dve.wait_ge(c.act_step.sem, c.act_step.base + T + 1)
            v.do(nv.tensor_scalar(nrm[:, :, 1], nrm[:, :, 1], 1e-12, None, ALU.max))
            v.do(nv.reciprocal(nrm[:, :, 1], nrm[:, :, 1]))
            with dve.Fori(0, T // 2) as i:
                v.enter(i, 4, T // 2)
                for u in range(2):
                    x = flat(c.x[:, bass.ds(i * 2 + u, 1), :])
                    v.did(nv.scalar_tensor_tensor(x, flat(c.acc[:, bass.ds(i * 2 + u, 1), 0:D]), nrm[:, bass.ds(i * 2 + u, 1), 1], x,
                                                  ALU.mult, ALU.add))
                for u in range(2):
                    v.wait(back=1 - u)
                    v.did(tile_stats(nc, c, i * 2 + u))
                v.leave()
            v.end()

        @block.scalar
        def _(act):
            a = Steps(act, c.act_step)
            with act.Fori(0, T // 2) as i:
                a.enter(i, 2, T // 2)
                for u in range(2):
                    act.wait_ge(c.ready.sem, h_at + i * 2 + u + 1)
                    a.did(nc.scalar.activation(flat(c.table[:, bass.ds(i * 2 + u, 1), 0:D]), flat(c.acc[:, bass.ds(i * 2 + u, 1), 0:D]),
                                               ACT.Square, accum_out=nrm[:, bass.ds(i * 2 + u, 1), 1]))
                a.leave()
            a.wait()
            a.did(nc.scalar.activation(nrm[:, :, 1], nrm[:, :, 1], ACT.Sqrt))
            a.end()

        c.ready.base += T


SLICE_ROOM = [("wxT", SLICE, SLICE_HEADS * D), ("wslice", SLICE, SLICE), ("bx", SLICE, SLICE_HEADS), ("wfx", P, 2 * SLICE_HEADS * SLICE),
              ("bfx", SLICE, SLICE_HEADS), ("wqkv", SLICE, 3 * SLICE), ("wo", SLICE, SLICE_HEADS * D)]
assert sum(n for _, _, n in SLICE_ROOM) <= T * ROW


def slice_inputs(c):
    room, at, views = c.table[:, :, :].rearrange("p t f -> p (t f)"), 0, {}
    for name, parts, n in SLICE_ROOM:
        views[name] = room[0:parts, at:at + n]
        at += n
    return views


def slice_layer(nc, c, ins):
    SH, G = SLICE_HEADS, SLICE
    HG = SH * G
    layer_stats(nc, c)
    with (
        nc.sbuf_tensor("sw", [P, T, HG], F32) as sw, nc.sbuf_tensor("pooled", [P, 3, HG], F32) as pooled,
        nc.sbuf_tensor("zout", [P, 4, D], F32) as zout,
    ):
        with (
            nc.sbuf_tensor("wl", [P, 2, HG], F32) as wl,
            nc.sbuf_tensor("bl", [P, HG], F32) as bl, nc.sbuf_tensor("invt", [P, SH], F32) as invt,
            nc.sbuf_tensor("bxw", [G, SH, P], F32) as bxw,
        ):
            views = slice_inputs(c)
            wxt, wsl, bx = views["wxT"].rearrange("p (h k) -> p h k", h=SH), views["wslice"], views["bx"]
            with nc.psum_tensor("wlp", [P, 2, 512], F32) as wlp, nc.psum_tensor("blp", [P, 512], F32) as blp, nc.Block() as block:
                @block.vector
                def _(dve):
                    v = Steps(dve, c.dve_step)
                    nv = nc.vector
                    dve.wait_ge(c.slice_in, 16 * len(SLICE_ROOM))
                    v.did(nv.tensor_copy(bxw[:, :, :], last(bx, P)))
                    c.wide = v.at + v.n
                    v.do(nv.tensor_scalar(invt[:, :], row(c.rows, "temp"), 0.1, 5.0, ALU.max, ALU.min))
                    v.do(nv.reciprocal(invt[:, :], invt[:, :]))
                    dve.wait_ge(c.product.sem, c.product.base + 1)
                    for k in range(2):
                        v.did(nv.tensor_tensor(wl[:, k, :].rearrange("p (h g) -> p h g", h=SH), wlp[:, k, :].rearrange("p (h g) -> p h g", h=SH),
                                               last(invt[:, :], G), ALU.mult))
                    v.do(nv.tensor_tensor(bl[:, :].rearrange("p (h g) -> p h g", h=SH), blp[:, :].rearrange("p (h g) -> p h g", h=SH),
                                           mid(row(c.rows, "b_slice"), SH), ALU.add))
                    v.did(nv.tensor_tensor(bl[:, :].rearrange("p (h g) -> p h g", h=SH), bl[:, :].rearrange("p (h g) -> p h g", h=SH),
                                           last(invt[:, :], G), ALU.mult))
                    v.end()

                @block.tensor
                def _(pe):
                    pe.wait_ge(c.slice_in, 16 * len(SLICE_ROOM))
                    pe.wait_ge(c.dve_step.sem, c.wide)
                    for h in range(SH):
                        for k in range(2):
                            nc.tensor.matmul(wlp[:, k, h * G:(h + 1) * G], wxt[:, h, k * P:(k + 1) * P], wsl, start=True, stop=True)
                        ins_ = nc.tensor.matmul(blp[:, h * G:(h + 1) * G], bxw[:, h, :], wsl, start=True, stop=True)
                    ins_.then_inc(c.product.sem, 1)
                    c.product.base += 1
            slice_weights(nc, c, sw, wl, bl, pooled)
        slice_attention(nc, c, ins, pooled, zout)
        with nc.sbuf_tensor("so", [P, 2, D], F32) as o:
            def prep(v, t, a):
                return nc.vector.tensor_copy(a, flat(sw[:, bass.ds(t, 1), :]))

            def post(v, t, prod):
                u = v.parity
                v.parity ^= 1
                v.do(nc.vector.tensor_tensor(o[:, u, :], prod, row(c.rows, "b_out"), ALU.add))
                x = flat(c.x[:, bass.ds(t, 1), :])
                v.do(nc.vector.tensor_tensor(x, x, o[:, u, :], ALU.add))
                return tile_stats(nc, c, t)

            dense(nc, c, 4, D, lambda h: zout[:, h, :], prep, post, 0, 2)


def slice_weights(nc, c, sw, wl, bl, pooled):
    SH, G = SLICE_HEADS, SLICE
    HG = SH * G
    turns = T // 2
    rows_at, flip_at, flat_at, prod_at, ready_at, expo_at, weighted_at, pooled_at = (
        s.base for s in (c.rows_in, c.flipped, c.feature_major, c.product, c.ready, c.expo, c.weighted, c.taken))
    with (
        nc.sbuf_tensor("srows", [P, 2, D], F32) as a, nc.sbuf_tensor("pooling", [P, 2, D], F32) as b, nc.sbuf_tensor("srowsT", [P, 2, 2, P], F32) as at,
        nc.sbuf_tensor("slog", [P, 2, HG], F32) as lg, nc.sbuf_tensor("smx", [P, 2, 2, SH], F32) as mx,
        nc.psum_tensor("sflip", [P, 2, 512], F32) as flip, nc.psum_tensor("sprod", [P, 2, 512], F32) as prod,
        nc.psum_tensor("spool", [P, 3, 512], F32) as pool_, nc.Block() as block,
    ):
        @block.vector
        def _(dve):
            v = Steps(dve, c.dve_step)
            nv = nc.vector

            def rows(i):
                for u in range(2):
                    dve.wait_ge(c.flipped.sem, flip_at + i * 2 + (u - 1))
                    normalized(nc, c, a[:, u, :], i * 2 + u).then_inc(c.rows_in.sem, 1)

            def logits(i):
                for u in range(2):
                    lv = lg[:, u, :].rearrange("p (h g) -> p h g", h=SH)
                    dve.wait_ge(c.product.sem, prod_at + i * 2 + u + 1)
                    v.do(nv.tensor_tensor(lg[:, u, :], prod[:, u, :], bl[:, :], ALU.add))
                    v.do(nv.tensor_reduce(mx[:, u, 0, :], lv, AX.X, ALU.max))
                    nv.tensor_tensor(lv, lv, last(mx[:, u, 0, :], G), ALU.subtract).then_inc(c.ready.sem, 1)

            def weights(i):
                for u in range(2):
                    t = i * 2 + u
                    sv = flat(sw[:, bass.ds(t, 1), :]).rearrange("p (h g) -> p h g", h=SH)
                    dve.wait_ge(c.expo.sem, expo_at + i * 2 + u + 1)
                    v.do(nv.tensor_reduce(mx[:, u, 1, :], sv, AX.X, ALU.add))
                    v.do(nv.reciprocal(mx[:, u, 1, :], mx[:, u, 1, :]))
                    v.did(nv.tensor_scalar(mx[:, u, 1, :], mx[:, u, 1, :], c.valid[:, bass.ds(t, 1)], None, ALU.mult))
                    dve.wait_ge(c.taken.sem, pooled_at + i * 2 + (u - 1))
                    v.do(normalized(nc, c, b[:, u, :], t))
                    nv.tensor_tensor(sv, sv, last(mx[:, u, 1, :], G), ALU.mult).then_inc(c.weighted.sem, 1)

            for i in range(3):
                rows(i)
            logits(0)
            with dve.Fori(0, turns - 3) as i:
                v.enter(i, 12, turns - 3)
                rows(i + 3)
                weights(i)
                logits(i + 1)
                v.leave()
            for i in range(turns - 3, turns):
                weights(i)
                if i + 1 < turns:
                    logits(i + 1)
            dve.wait_ge(c.taken.sem, pooled_at + T + 1)
            v.did(nv.tensor_copy(pooled[:, :, :], pool_[:, :, :]))
            v.end()

        @block.scalar
        def _(act):
            def copies(i):
                for u in range(2):
                    act.wait_ge(c.flipped.sem, flip_at + i * 2 + u + 1)
                    act.wait_ge(c.product.sem, prod_at + i * 2 + (u - 1))
                    nc.scalar.copy(at[:, u, :, :].rearrange("p h n -> p (h n)"), flip[:, u, 0:D]).then_inc(c.feature_major.sem, 1)

            def exponentials(i):
                for u in range(2):
                    act.wait_ge(c.ready.sem, ready_at + i * 2 + u + 1)
                    nc.scalar.activation(flat(sw[:, bass.ds(i * 2 + u, 1), :]), lg[:, u, :], ACT.Exp).then_inc(c.expo.sem, 1)

            copies(0)
            copies(1)
            exponentials(0)
            with act.Fori(0, turns - 2) as i:
                copies(i + 2)
                exponentials(i + 1)
            exponentials(turns - 1)

        @block.tensor
        def _(pe):
            zero = c.zero[:, 0:1].broadcast_to([P, 512])

            def turn(i):
                for u in range(2):
                    pe.wait_ge(c.rows_in.sem, rows_at + i * 2 + u + 1)
                    pe.wait_ge(c.feature_major.sem, flat_at + i * 2 + (u - 1))
                    for h in range(2):
                        ins = nc.tensor.transpose(flip[:, u, h * P:(h + 1) * P], a[:, u, h * P:(h + 1) * P], c.ident[:, :])
                    ins.then_inc(c.flipped.sem, 1)

            def multiply(i):
                for u in range(2):
                    pe.wait_ge(c.feature_major.sem, flat_at + i * 2 + u + 1)
                    pe.wait_ge(c.ready.sem, ready_at + i * 2 + (u - 1))
                    for h in range(2):
                        ins = nc.tensor.matmul(prod[:, u, :], at[:, u, h, :], wl[:, h, :], start=(h == 0), stop=(h == 1))
                    ins.then_inc(c.product.sem, 1)

            def pool(i):
                for u in range(2):
                    pe.wait_ge(c.weighted.sem, weighted_at + i * 2 + u + 1)
                    weight = flat(sw[:, bass.ds(i * 2 + u, 1), :])
                    for n, left in enumerate((b[:, u, 0:P], b[:, u, P:D], c.ones[:, :])):
                        ins = nc.tensor.matmul(pool_[:, n, :], left, weight, start=False, stop=False)
                    ins.then_inc(c.taken.sem, 1)

            for n in range(3):
                nc.tensor.matmul(pool_[:, n, :], c.zero[:, :], zero, start=True, stop=False)
            turn(0)
            turn(1)
            multiply(0)
            with pe.Fori(0, turns - 2) as i:
                turn(i + 2)
                multiply(i + 1)
                pool(i)
            multiply(turns - 1)
            pool(turns - 2)
            pool(turns - 1)
            for n in range(3):
                ins = nc.tensor.matmul(pool_[:, n, :], c.zero[:, :], zero, start=False, stop=True)
            ins.then_inc(c.taken.sem, 1)

        for s in (c.rows_in, c.flipped, c.feature_major, c.product, c.ready, c.expo, c.weighted):
            s.base += T
        c.taken.base += T + 1


def slice_attention(nc, c, ins, pooled, zout):
    SH, G = SLICE_HEADS, SLICE
    HG = SH * G
    with (
        nc.sbuf_tensor("tok", [G, 8, HG], F32) as tok, nc.sbuf_tensor("amx", [G, 2, SH], F32) as amx,
    ):
        views = slice_inputs(c)
        wfx, bfx = views["wfx"].rearrange("p (k f) -> p k f", k=2), views["bfx"]
        wqkv, wo = views["wqkv"].rearrange("p (k f) -> p k f", k=3), views["wo"].rearrange("p (h f) -> p h f", h=SH)
        with (
            nc.psum_tensor("tokp", [G, 512], F32) as tokp, nc.psum_tensor("qkvp", [G, 3, 512], F32) as qkvp,
            nc.psum_tensor("attp", [G, 512], F32) as attp, nc.psum_tensor("atT", [G, 512], F32) as atp,
            nc.psum_tensor("zp", [P, 4, D], F32) as zp, nc.Block() as block,
        ):
            st, den, q, k, val, att, attT, osT = (tok[:, n, :] for n in range(8))
            hs = lambda x, h: x[:, h * G:(h + 1) * G]
            by_head = lambda x: x.rearrange("p (h g) -> p h g", h=SH)
            done = c.product.base

            @block.vector
            def _(dve):
                v = Steps(dve, c.dve_step)
                nv = nc.vector
                c.marks = []

                def mark():
                    c.marks.append(v.at + v.n)
                norm = pooled[0:G, 2, :]
                v.did(nv.tensor_tensor(by_head(st), by_head(norm), last(bfx, G), ALU.mult))
                v.do(nv.tensor_scalar(den, norm, EPS, None, ALU.add))
                v.do(nv.reciprocal(den, den))
                dve.wait_ge(c.product.sem, done + 1)
                v.do(nv.tensor_tensor(st, st, tokp[:, :], ALU.add))
                v.did(nv.tensor_tensor(st, st, den, ALU.mult))
                mark()
                dve.wait_ge(c.product.sem, done + 2)
                for n, x in enumerate((q, k, val)):
                    v.did(nv.tensor_copy(x, qkvp[:, n, :]))
                mark()
                dve.wait_ge(c.product.sem, done + 3)
                v.do(nv.tensor_scalar(att, attp[:, :], G ** -0.5, None, ALU.mult))
                v.do(nv.tensor_reduce(amx[:, 0, :], by_head(att), AX.X, ALU.max))
                v.did(nv.tensor_tensor(by_head(att), by_head(att), last(amx[:, 0, :], G), ALU.subtract))
                mark()
                dve.wait_ge(c.act_step.sem, c.act_step.base + 1)
                v.do(nv.tensor_reduce(amx[:, 1, :], by_head(att), AX.X, ALU.add))
                v.do(nv.reciprocal(amx[:, 1, :], amx[:, 1, :]))
                v.did(nv.tensor_tensor(by_head(att), by_head(att), last(amx[:, 1, :], G), ALU.mult))
                mark()
                dve.wait_ge(c.product.sem, done + 4)
                v.did(nv.tensor_copy(attT, atp[:, :]))
                mark()
                dve.wait_ge(c.product.sem, done + 5)
                v.did(nv.tensor_copy(osT, attp[:, :]))
                mark()
                dve.wait_ge(c.product.sem, done + 6)
                v.did(nv.tensor_copy(zout[:, :, :], zp[:, :, :]))
                v.end()

            @block.scalar
            def _(act):
                a = Steps(act, c.act_step)
                act.wait_ge(c.dve_step.sem, c.marks[2])
                a.did(nc.scalar.activation(att, att, ACT.Exp))
                a.end()

            @block.tensor
            def _(pe):
                mm = lambda out, l, r, s=True, e=True: nc.tensor.matmul(out, l, r, start=s, stop=e)
                for h in range(SH):
                    for kk in range(2):
                        ins_ = mm(hs(tokp, h), wfx[:, kk, h * G:(h + 1) * G], pooled[:, kk, h * G:(h + 1) * G], kk == 0, kk == 1)
                ins_.then_inc(c.product.sem, 1)
                pe.wait_ge(c.dve_step.sem, c.marks[0])
                mm(qkvp[:, 0, :], wqkv[:, 0, :], st)
                mm(qkvp[:, 1, :], wqkv[:, 1, :], st)
                for h in range(SH):
                    ins_ = mm(qkvp[:, 2, h * G:(h + 1) * G], hs(st, h), wqkv[:, 2, :])
                ins_.then_inc(c.product.sem, 1)
                pe.wait_ge(c.dve_step.sem, c.marks[1])
                for h in range(SH):
                    ins_ = mm(hs(attp, h), hs(q, h), hs(k, h))
                ins_.then_inc(c.product.sem, 1)
                pe.wait_ge(c.dve_step.sem, c.marks[3])
                for h in range(SH):
                    ins_ = nc.tensor.transpose(hs(atp, h), hs(att, h), c.ident[0:G, 0:G])
                ins_.then_inc(c.product.sem, 1)
                pe.wait_ge(c.dve_step.sem, c.marks[4])
                for h in range(SH):
                    ins_ = mm(hs(attp, h), hs(val, h), hs(attT, h))
                ins_.then_inc(c.product.sem, 1)
                pe.wait_ge(c.dve_step.sem, c.marks[5])
                for h in range(SH):
                    ins_ = mm(zp[(h % 2) * G:(h % 2 + 1) * G, h // 2, :], hs(osT, h), wo[:, h, :])
                ins_.then_inc(c.product.sem, 1)
                c.product.base += 6


def expert_layer(nc, c, ins, slots, out):
    T20 = 20
    layer_stats(nc, c)
    with (
        nc.sbuf_tensor("rtab", [P, T, T20], F32) as rtab, nc.sbuf_tensor("racc", [P, T, T20], F32) as racc,
        nc.sbuf_tensor("gates", [P, T, EXPERTS], F32) as gates,
        nc.sbuf_tensor("w1", [P, 2, EXPERTS, HIDDEN], F32) as w1, nc.sbuf_tensor("w2", [P, EXPERTS, HIDDEN // P, D], F32) as w2,
        nc.sbuf_tensor("b1", [P, EXPERTS, HIDDEN // P], F32) as b1,
    ):
        load(nc, c, [],
             [(w1[:, :, :, :].rearrange("p k e f -> p (k e f)"), ins["w1"]),
              (w2[:, :, :, :].rearrange("p k e f -> p (k e f)"), ins["w2"]), (b1[:, :, :].rearrange("p e f -> p (e f)"), ins["b1"])], c.fetched)
        fold(nc, c, c.rw, 16, HEADS, "ras", "rad")
        gat_rows(nc, c, c.rw, 16, HEADS, rtab, c.rdram)
        attend(nc, c, rtab, c.rdram, 16, HEADS, slots, ROUTER_CHUNKS, racc)
        route(nc, c, racc, gates)
        experts(nc, c, w1, w2, b1, gates, out)


def route(nc, c, racc, gates):
    E = EXPERTS
    with (
        nc.sbuf_tensor("r16", [P, T, 16], F32) as s16, nc.sbuf_tensor("q16", [P, T, 16], F32) as q16,
        nc.sbuf_tensor("m1", [P, 4, T], F32) as m1, nc.sbuf_tensor("sc", [P, T, E], F32) as sc,
        nc.sbuf_tensor("earlier", [P, E, E], F32) as earlier, nc.Block() as block,
    ):
        @block.vector
        def _(dve):
            v = Steps(dve, c.dve_step)
            nv = nc.vector
            z = racc[:, :, 16:16 + HEADS]
            v.do(nv.tensor_scalar(z, z, 1e-16, None, ALU.add))
            v.do(nv.reciprocal(z, z))
            for h in range(HEADS):
                v.did(nv.tensor_tensor(s16[:, :, h * E:(h + 1) * E], racc[:, :, h * E:(h + 1) * E],
                                       racc[:, :, 16 + h].unsqueeze(2).broadcast_to([P, T, E]), ALU.mult))
            v.wait()
            v.do(nv.tensor_tensor(s16[:, :, :], s16[:, :, :], mid(row(c.rows, "rb"), T), ALU.add))
            v.do(nv.tensor_reduce(m1[:, 0, :], s16[:, :, :], AX.X, ALU.add))
            v.do(nv.tensor_scalar(m1[:, 0, :], m1[:, 0, :], 1.0 / 16, None, ALU.mult))
            v.do(nv.tensor_tensor(s16[:, :, :], s16[:, :, :], last(m1[:, 0, :], 16), ALU.subtract))
            v.do(nv.tensor_tensor(q16[:, :, :], s16[:, :, :], s16[:, :, :], ALU.mult))
            v.do(nv.tensor_reduce(m1[:, 1, :], q16[:, :, :], AX.X, ALU.add))
            v.did(nv.tensor_scalar(m1[:, 1, :], m1[:, 1, :], 1.0 / 16, None, ALU.mult))
            c.var = v.at + v.n
            dve.wait_ge(c.act_step.sem, c.act_step.base + 1)
            v.do(nv.reciprocal(m1[:, 1, :], m1[:, 1, :]))
            v.do(nv.tensor_tensor(s16[:, :, :], s16[:, :, :], last(m1[:, 1, :], 16), ALU.mult))
            v.do(nv.tensor_tensor(s16[:, :, :], s16[:, :, :], mid(row(c.rows, "lng"), T), ALU.mult))
            v.do(nv.tensor_tensor(s16[:, :, :], s16[:, :, :], mid(row(c.rows, "lnb"), T), ALU.add))
            v.do(nv.tensor_reduce(sc[:, :, :], s16[:, :, :].rearrange("p t (h e) -> p t e h", h=HEADS), AX.X, ALU.add))
            v.do(nv.tensor_scalar(sc[:, :, :], sc[:, :, :], 1.0 / HEADS, None, ALU.mult))
            v.did(nv.tensor_tensor(earlier[:, :, :], mid(c.iota[:, 0:E], E), last(c.iota[:, 0:E], E), ALU.is_lt))
            a4 = s16[:, :, :].rearrange("p t (i j) -> p t i j", i=E)
            b4 = q16[:, :, :].rearrange("p t (i j) -> p t i j", i=E)
            sj = sc[:, :, :].unsqueeze(2).broadcast_to([P, T, E, E])
            si = sc[:, :, :].unsqueeze(3).broadcast_to([P, T, E, E])
            v.do(nv.tensor_tensor(a4, sj, si, ALU.is_gt))
            v.do(nv.tensor_tensor(b4, sj, si, ALU.is_equal))
            v.do(nv.tensor_tensor(q16[:, :, :], q16[:, :, :], mid(earlier[:, :, :].rearrange("p i j -> p (i j)"), T), ALU.mult))
            v.do(nv.tensor_tensor(s16[:, :, :], s16[:, :, :], q16[:, :, :], ALU.add))
            v.do(nv.tensor_reduce(gates[:, :, :], a4, AX.X, ALU.add))
            v.do(nv.tensor_scalar(gates[:, :, :], gates[:, :, :], 1.5, None, ALU.is_lt))
            v.do(nv.tensor_reduce(m1[:, 2, :], sc[:, :, :], AX.X, ALU.max))
            v.did(nv.tensor_tensor(sc[:, :, :], sc[:, :, :], last(m1[:, 2, :], E), ALU.subtract))
            c.best = v.at + v.n
            dve.wait_ge(c.act_step.sem, c.act_step.base + 2)
            v.do(nv.tensor_tensor(gates[:, :, :], gates[:, :, :], sc[:, :, :], ALU.mult))
            v.do(nv.tensor_reduce(m1[:, 3, :], gates[:, :, :], AX.X, ALU.add))
            v.do(nv.reciprocal(m1[:, 3, :], m1[:, 3, :]))
            v.did(nv.tensor_tensor(gates[:, :, :], gates[:, :, :], last(m1[:, 3, :], E), ALU.mult))
            v.end()

        @block.scalar
        def _(act):
            a = Steps(act, c.act_step)
            act.wait_ge(c.dve_step.sem, c.var)
            a.did(nc.scalar.activation(m1[:, 1, :], m1[:, 1, :], ACT.Sqrt, bias=c.eps[:, 0:1]))
            act.wait_ge(c.dve_step.sem, c.best)
            a.did(nc.scalar.activation(sc[:, :, :], sc[:, :, :], ACT.Exp))
            a.end()


def experts(nc, c, w1, w2, b1, gates, out):
    assert BUCKETS == T - 1
    E, KH, HB = EXPERTS, 2, HIDDEN // P
    turns = T // 2
    with (
        nc.sbuf_tensor("xa", [P, 2, D], F32) as a,
        nc.sbuf_tensor("xT", [P, KH, 2 * P], F32) as xt, nc.sbuf_tensor("hid", [P, 2, HB, 2 * P], F32) as hid,
        nc.sbuf_tensor("eo", [P, 2, D], F32) as o,
    ):
        rows_at, flip_at, flat_at, hid_at, gelu_at, prod_at, taken_at = (
            s.base for s in (c.rows_in, c.flipped, c.feature_major, c.ready, c.expo, c.product, c.taken))
        stored_at = c.stored.base
        with (
            nc.psum_tensor("eflip", [P, KH, 2 * P], F32) as flip, nc.psum_tensor("hidp", [P, 2, HB, 2 * P], F32) as hidp,
            nc.psum_tensor("eprod", [P, 2, 512], F32) as prod, nc.Block() as block,
        ):
            @block.vector
            def _(dve):
                v = Steps(dve, c.dve_step)
                nv = nc.vector

                def prepare(i):
                    for u in range(2):
                        dve.wait_ge(c.flipped.sem, flip_at + i)
                        normalized(nc, c, a[:, u, :], i * 2 + u).then_inc(c.rows_in.sem, 1)

                def turned(i):
                    dve.wait_ge(c.flipped.sem, flip_at + i + 1)
                    dve.wait_ge(c.ready.sem, hid_at + i * E)
                    nv.tensor_copy(xt[:, :, :], flip[:, :, :]).then_inc(c.feature_major.sem, 1)

                def gate(i, tiles=2):
                    for e in range(E):
                        if e == E - 2 and tiles == 2:
                            turned(i + 1)
                        for u in range(tiles):
                            n = e * tiles + u
                            dve.wait_ge(c.product.sem, prod_at + i * 2 * E + (n + 1))
                            dve.wait_ge(c.taken.sem, taken_at + i * 2 * E + n)
                            v.do(nv.tensor_tensor(o[:, u, :], prod[:, u, 0:D], row(c.rows, "eb2")[:, e * D:(e + 1) * D], ALU.add))
                            x = flat(c.x[:, bass.ds(i * 2 + u, 1), :])
                            nv.scalar_tensor_tensor(x, o[:, u, :], gates[:, bass.ds(i * 2 + u, 1), e], x, ALU.mult,
                                                    ALU.add).then_inc(c.taken.sem, 1)

                prepare(0)
                turned(0)
                prepare(1)
                with dve.Fori(0, turns - 2) as i:
                    v.enter(i, 2 * E, turns - 2)
                    prepare(i + 2)
                    gate(i)
                    v.leave()
                gate(turns - 2)
                gate(turns - 1, tiles=1)
                v.end()

            @block.scalar
            def _(act):
                def hidden(i, tiles=2):
                    for e in range(E):
                        act.wait_ge(c.ready.sem, hid_at + i * E + (e + 1))
                        act.wait_ge(c.product.sem, prod_at + i * 2 * E + (e - 1) * (tiles if e > 1 else 2))
                        for hb in range(HB):
                            ins_ = nc.scalar.activation(hid[:, e % 2, hb, 0:tiles * P], hidp[:, e % 2, hb, 0:tiles * P], ACT.Gelu,
                                                        bias=b1[:, e, hb:hb + 1])
                        ins_.then_inc(c.expo.sem, 1)

                act.wait_ge(c.fetched, 48)
                with act.Fori(0, turns - 1) as i:
                    hidden(i)
                hidden(turns - 1, tiles=1)

            @block.tensor
            def _(pe):
                def turn(i):
                    pe.wait_ge(c.rows_in.sem, rows_at + i * 2 + 2)
                    pe.wait_ge(c.feature_major.sem, flat_at + i)
                    for u in range(2):
                        for k in range(KH):
                            ins_ = nc.tensor.transpose(flip[:, k, u * P:(u + 1) * P], a[:, u, k * P:(k + 1) * P], c.ident[:, :])
                    ins_.then_inc(c.flipped.sem, 1)

                def up(i, e, tiles=2):
                    if e == 0:
                        pe.wait_ge(c.feature_major.sem, flat_at + i + 1)
                    pe.wait_ge(c.expo.sem, gelu_at + i * E + (e - 1))
                    for hb in range(HB):
                        for k in range(KH):
                            ins_ = nc.tensor.matmul(hidp[:, e % 2, hb, 0:tiles * P], w1[:, k, e, hb * P:(hb + 1) * P],
                                                    xt[:, k, 0:tiles * P], start=(k == 0), stop=(k == KH - 1))
                    ins_.then_inc(c.ready.sem, 1)

                def down(i, e, tiles=2):
                    pe.wait_ge(c.expo.sem, gelu_at + i * E + (e + 1))
                    for u in range(tiles):
                        pe.wait_ge(c.taken.sem, taken_at + i * 2 * E + (2 * e + u - 1 if tiles == 2 else e))
                        for hb in range(HB):
                            ins_ = nc.tensor.matmul(prod[:, u, 0:D], hid[:, e % 2, hb, u * P:(u + 1) * P], w2[:, e, hb, :],
                                                    start=(hb == 0), stop=(hb == HB - 1))
                        ins_.then_inc(c.product.sem, 1)

                pe.wait_ge(c.fetched, 48)
                turn(0)
                up(0, 0)
                with pe.Fori(0, turns - 1) as i:
                    turn(i + 1)
                    for e in range(1, E):
                        up(i, e)
                        down(i, e - 1)
                    up(i + 1, 0)
                    down(i, E - 1)
                for e in range(1, E):
                    up(turns - 1, e, tiles=1)
                    down(turns - 1, e - 1, tiles=1)
                down(turns - 1, E - 1, tiles=1)

            @block.sync
            def _(sp):
                def store(i, tiles=2):
                    sp.wait_ge(c.taken.sem, taken_at + i * 2 * E + tiles * E)
                    sp.dma_start(out.rearrange("p (t f) -> p t f", t=T)[:, bass.ds(i * 2, 2), :],
                                 c.x[:, bass.ds(i * 2, 2), :]).then_inc(c.stored.sem, 16)

                with sp.Fori(0, turns - 1) as i:
                    store(i)
                store(turns - 1, tiles=1)
                sp.wait_ge(c.stored.sem, stored_at + 16 * turns)


class Slots:

    def __init__(self, nc, name, chunks):
        self.src = nc.alloc_sbuf_tensor(f"{name}_src", [P, chunks + RING], I32)
        self.place = nc.alloc_sbuf_tensor(f"{name}_place", [P, chunks + RING], F32)
        self.tile = nc.alloc_sbuf_tensor(f"{name}_tile", [1, QUAD + chunks + RING], I32)


class Core:

    def __init__(self, nc):
        self.n = 0
        sb = nc.alloc_sbuf_tensor
        self.x = sb("x", [P, T, D], F32)
        self.rows = sb("rows", [P, ROWS_LEN], F32)
        self.iota, self.itmp = sb("iota", [P, 512], F32), sb("itmp", [P, 512], I32)
        self.iota16, self.zero16 = sb("iota16", [P, 512], F16), sb("zero16", [P, P], F16)
        self.part, self.ptmp = sb("part", [P, 1], F32), sb("ptmp", [P, 1], I32)
        self.ident, self.lower = sb("ident", [P, P], F32), sb("lower", [P, P], F32)
        self.ones, self.zero = sb("ones", [P, P], F32), sb("zero", [P, P], F32)
        self.pick = sb("pick", [HEADS, HEADS, P], F32)
        self.valid, self.eps = sb("valid", [P, T], F32), sb("eps", [P, 1], F32)
        self.stat, self.bn = sb("stat", [P, T, 2], F32), sb("bn", [P, T, 6], F32)
        self.ed, self.top = sb("ed", [P, T, HEADS], F32), sb("top", [P, T, HEADS], F32)
        self.flag = sb("flag", [1, 1], I32)
        self.edm = sb("edm", [P, T * 2 * HEADS], F32)
        self.gw0, self.gw1 = sb("gw0", [P, 2, D + 2 * HEADS], F32), sb("gw1", [P, 2, D + 2], F32)
        self.rw = sb("rw", [P, 2, 16 + 2 * HEADS], F32)
        self.counts = []

        def count(name):
            self.counts.append(Count(nc, name))
            return self.counts[-1]

        self.dve_step = count("dve_step")
        self.act_step = count("act_step")
        self.pool_step = count("pool_step")
        self.totals = count("totals")
        self.prefixes = count("prefixes")
        self.onehots = count("onehots")
        self.placed = count("placed")
        self.located = count("located")
        self.fielded = count("fielded")
        self.chunked = count("chunked")
        self.rows_in = count("rows_in")
        self.flipped = count("flipped")
        self.feature_major = count("feature_major")
        self.product = count("product")
        self.taken = count("taken")
        self.indexed = count("indexed")
        self.summed = count("summed")
        self.added = count("added")
        self.ready = count("ready")
        self.looked = count("looked")
        self.expo = count("expo")
        self.weighted = count("weighted")
        self.scaled = count("scaled")
        self.loaded, self.stored = Count(nc, "loaded"), Count(nc, "stored")
        self.opened, self.fetched = nc.alloc_semaphore("opened"), nc.alloc_semaphore("fetched")
        self.slice_in = nc.alloc_semaphore("slice_in")
        for s in (self.loaded, self.stored):
            s.base = 0
        self.gathered = [nc.alloc_semaphore(f"gathered{u}") for u in range(RING)]
        self.gather_base = 0

    def fresh(self):
        self.n += 1
        return self.n


def sort_and_sage(nc, c, ins, slots, rslots):
    steps = SIDE_STEPS * (GRAPH_CHUNKS // RING)
    with placing_tensors(nc, "graph", GRAPH_EDGES, GRAPH_CHUNKS, GRAPH_EDGES[1]) as tensors:
        graph = Placing(nc, c, GRAPH_EDGES, GRAPH_CHUNKS, GRAPH_EDGES[1], tensors)
        find_slots(nc, c, ins["dst"], ins["src"], graph, slots,
                   [(c.x[:, :, :].rearrange("p t f -> p (t f)"), ins["x"]), (c.rows[:, :], ins["rows"].broadcast_to([P, ROWS_LEN])),
                    (c.gw0[:, :, 0:D], ins["gw0"].rearrange("p (k f) -> p k f", k=2)),
                    (c.gw1[:, :, 0:D], ins["gw1"].rearrange("p (k f) -> p k f", k=2)),
                    (c.rw[:, :, 0:16], ins["rw"].rearrange("p (k f) -> p k f", k=2))])
        place_edges(nc, c, graph, slots)
    c.table = nc.alloc_sbuf_tensor("table", [P, T, ROW], F32)
    c.acc = nc.alloc_sbuf_tensor("acc", [P, T, ROW], F32)
    with placing_tensors(nc, "router", ROUTER_EDGES, ROUTER_CHUNKS, steps + SIDE_LEAD) as tensors:
        router = Placing(nc, c, ROUTER_EDGES, ROUTER_CHUNKS, steps, tensors, SIDE_LEAD)
        find_slots(nc, c, ins["rdst"], ins["rsrc"], router, rslots)
        layer_stats(nc, c)
        weighted_rows(nc, c)
        sage(nc, c, ins, 1, slots, router, rslots)
    sage(nc, c, ins, 2, slots)


def graph_kernel(nc, ins, out):
    c = Core(nc)
    slots, rslots = Slots(nc, "graph", GRAPH_CHUNKS), Slots(nc, "router", ROUTER_CHUNKS)
    with nc.Block() as block:
        @block.gpsimd
        def _(pool):
            for s in c.counts:
                pool.sem_inc(s.sem, RING)
    constants(nc, c)
    c.dram = nc.dram_tensor("table_dram", (T * P, ROW), F32).ap()
    c.rdram = nc.dram_tensor("router_dram", (T * P, 20), F32).ap()
    sort_and_sage(nc, c, ins, slots, rslots)
    slice_layer(nc, c, ins)
    gat_layer(nc, c, ins, slots)
    expert_layer(nc, c, ins, rslots, out)


def layout(i):
    import numpy as np
    a = {k: np.asarray(v) for k, v in i.items()}
    x = np.zeros((T * P, D), np.float32)
    x[:NODES] = a["x"]
    kmaj = lambda w: np.ascontiguousarray(w.reshape(2, P, -1).transpose(1, 0, 2)).reshape(P, -1)
    rows = {"raw": "L0_gnn_raw_weights", "sb1": "L0_gnn_b1", "sb2": "L0_gnn_b2", "b_slice": "L0_ffn_b_slice",
            "temp": "L0_ffn_temperature", "b_out": "L0_ffn_b_out", "as0": "L1_gnn_a_src0", "ad0": "L1_gnn_a_dst0",
            "gb0": "L1_gnn_b0", "gamma0": "L1_gnn_gamma0", "beta0": "L1_gnn_beta0", "as1": "L1_gnn_a_src1",
            "ad1": "L1_gnn_a_dst1", "gb1": "L1_gnn_b1", "ras": "L1_ffn_att_src", "rad": "L1_ffn_att_dst",
            "rb": "L1_ffn_b_gat", "lng": "L1_ffn_ln_gamma", "lnb": "L1_ffn_ln_beta", "eb2": "L1_ffn_b2"}
    ei = a["L1_ffn_edge_index"]
    o = {
        "x": x.reshape(T, P, D).transpose(1, 0, 2).reshape(P, T * D),
        "rows": np.concatenate([a[rows[n]].reshape(-1) for n, _ in ROWS])[None],
        "dst": a["dst"].reshape(GRAPH_EDGES), "src": a["src"].reshape(GRAPH_EDGES),
        "rdst": ei[1].reshape(ROUTER_EDGES), "rsrc": ei[0].reshape(ROUTER_EDGES),
        "wxT": a["L0_ffn_W_x"].T.reshape(SLICE_HEADS, SLICE, D).transpose(1, 0, 2).reshape(SLICE, -1),
        "wslice": a["L0_ffn_W_slice"], "bx": a["L0_ffn_b_x"].reshape(SLICE_HEADS, SLICE).T,
        "wfx": kmaj(a["L0_ffn_W_fx"]), "bfx": a["L0_ffn_b_fx"].reshape(SLICE_HEADS, SLICE).T,
        "wqkv": np.concatenate([a["L0_ffn_W_q"], a["L0_ffn_W_k"], a["L0_ffn_W_v"]], 1),
        "wo": a["L0_ffn_W_out"].reshape(SLICE_HEADS, SLICE, D).transpose(1, 0, 2).reshape(SLICE, -1),
        "gw0": kmaj(a["L1_gnn_W0"]), "gw1": kmaj(a["L1_gnn_W1"]), "rw": kmaj(a["L1_ffn_W_gat"]),
        "w1": a["L1_ffn_W1"].reshape(EXPERTS, 2, P, HIDDEN).transpose(2, 1, 0, 3).reshape(P, -1),
        "w2": a["L1_ffn_W2"].reshape(EXPERTS, HIDDEN // P, P, D).transpose(2, 0, 1, 3).reshape(P, -1),
        "b1": a["L1_ffn_b1"].reshape(EXPERTS, HIDDEN // P, P).transpose(2, 0, 1).reshape(P, -1),
    }
    for k in (1, 2):
        o[f"sage{k}"] = np.concatenate([kmaj(a[f"L0_gnn_W_self{k}"].T), kmaj(a[f"L0_gnn_W_neigh{k}"].T)], 1)
    return {k: np.ascontiguousarray(v) for k, v in o.items()}


def kernel(**inputs):
    import numpy as np
    import concourse.bacc as bacc
    from concourse.bass_utils import run_bass_kernel_spmd

    arrays = layout(inputs)
    nc = bacc.Bacc("TRN2", target_bir_lowering=False, num_devices=1)
    ins = {k: nc.dram_tensor(f"in_{k}", a.shape, mybir.dt.from_np(a.dtype), kind="ExternalInput").ap() for k, a in arrays.items()}
    out = nc.dram_tensor("out_x", (P, T * D), F32, kind="ExternalOutput").ap()
    graph_kernel(nc, ins, out)
    r = run_bass_kernel_spmd(nc, [{f"in_{k}": a for k, a in arrays.items()}], core_ids=[0])
    got = np.asarray(r.results[0]["out_x"])
    return np.ascontiguousarray(got.reshape(P, T, D).transpose(1, 0, 2).reshape(T * P, D)[:NODES])
```
